# Optimizing a Trainium2 kernel written in Bass

```python
import numpy as np
import jax
import jax.numpy as jnp

def _softmax(x, axis=-1):
    return jax.nn.softmax(x, axis=axis)

def _gelu(x):
    return jax.nn.gelu(x, approximate=True)

def _silu(x):
    return jax.nn.silu(x)

def _sigmoid(x):
    return jax.nn.sigmoid(x)

def _layernorm(x, axis=-1, eps=1e-05):
    m = jnp.mean(x, axis=axis, keepdims=True)
    v = jnp.var(x, axis=axis, keepdims=True)
    return (x - m) / jnp.sqrt(v + eps)

def _scatter_add(tgt, idx, src, axis=0):
    return tgt.at[idx].add(src)

def _segment_sum(src, seg, n):
    return jax.ops.segment_sum(src, seg, n)
kernel_name = 'mk_vit_tower_d1_tok_img768_r4_52b52c'

def setup_inputs(seed: int=0):
    np.random.seed(seed)
    _w = jnp.asarray

    def _rec_inputs():
        import jax
        import jax.numpy as jnp
        _rk = jax.random.key(seed)
        x = -0.00016672 + 0.999947 * jax.random.normal(jax.random.fold_in(_rk, 1), (16, 96, 96, 3), jnp.float32)
        return x
    x = _rec_inputs()

    def _L0_tok_setup():
        import jax, jax.numpy as jnp
        import numpy as np
        PATCH = 16

        def _patchify(images, p):
            B, H, W, C = images.shape
            gh, gw = (H // p, W // p)
            x = images.reshape(B, gh, p, gw, p, C)
            x = x.transpose(0, 1, 3, 2, 4, 5)
            return x.reshape(B, gh * gw, p * p * C)
        key = jax.random.key(seed)
        k1, k2, k3 = jax.random.split(key, 3)
        B, H, C, p, D = (64, 96, 3, PATCH, 192)
        N = (H // p) ** 2
        images = jax.random.normal(k1, (B, H, H, C), dtype=jnp.float32)
        W_proj = jax.random.normal(k2, (p * p * C, D), dtype=jnp.float32) * (1.0 / np.sqrt(p * p * C))
        b_proj = jnp.zeros((D,), dtype=jnp.float32)
        pos_table = jax.random.normal(k3, (N, D), dtype=jnp.float32) * 0.02
        return {'images': images, 'W_proj': W_proj, 'b_proj': b_proj, 'pos_table': pos_table}
    _L0_tok_all = _L0_tok_setup()
    _L0_tok_in = {k: v for k, v in _L0_tok_all.items() if k in ('W_proj', 'b_proj', 'pos_table')}
    del _L0_tok_all

    def _L0_attn_setup():
        import jax, jax.numpy as jnp
        import numpy as np
        H = 12

        def _attn(q, k, v):
            D = q.shape[-1]
            scores = jnp.einsum('bhnd,bhmd->bhnm', q, k) / jnp.sqrt(jnp.asarray(D, q.dtype))
            p = jax.nn.softmax(scores, axis=-1)
            return jnp.einsum('bhnm,bhmd->bhnd', p, v)
        key = jax.random.key(seed)
        ks = jax.random.split(key, 5)
        B, N, C = (2, 512, 192)
        s = 0.02
        return {'x': jax.random.normal(ks[0], (B, N, C), jnp.float32), 'Wq': jax.random.normal(ks[1], (C, 2 * C), jnp.float32) * s, 'Wk': jax.random.normal(ks[2], (C, 2 * C), jnp.float32) * s, 'Wv': jax.random.normal(ks[3], (C, C), jnp.float32) * s, 'lambda_p': jnp.zeros((H, 1, 1), jnp.float32), 'Wo': jax.random.normal(ks[4], (C, C), jnp.float32) * s, 'bo': jnp.zeros((C,), jnp.float32)}
    _L0_attn_all = _L0_attn_setup()
    _L0_attn_in = {k: v for k, v in _L0_attn_all.items() if k in ('Wq', 'Wk', 'Wv', 'lambda_p', 'Wo', 'bo')}
    del _L0_attn_all

    def _L0_ffn_setup():
        import jax, jax.numpy as jnp
        import numpy as np
        B, T, C, H, E, TOPK, DR = (2, 512, 192, 768, 8, 2, 24)

        def _normalize(v, axis=-1, eps=1e-12):
            return v / jnp.maximum(jnp.linalg.norm(v, axis=axis, keepdims=True), eps)
        key = jax.random.key(seed)
        ks = jax.random.split(key, 16)
        std = 0.02
        n = lambda k, shape, s=std: (s * jax.random.normal(k, shape)).astype(jnp.float32)
        emb = jax.random.normal(ks[3], (E, DR), dtype=jnp.float32)
        emb = emb / (jnp.linalg.norm(emb, axis=-1, keepdims=True) + 1e-08)
        return {'x': jax.random.normal(ks[0], (B, T, C), dtype=jnp.float32), 'router_w': n(ks[1], (E, C)), 'probe_w': n(ks[2], (DR, C)), 'router_emb': emb, 'fatigue': jnp.zeros((E,), jnp.float32), 'energy': jnp.ones((E,), jnp.float32), 'w_fast1': n(ks[4], (E, C, H)), 'w_slow1': n(ks[5], (E, C, H)), 'h_fast1': n(ks[6], (E, C, H), 0.005), 'm_gate1': jax.random.uniform(ks[7], (E,), dtype=jnp.float32), 'b1': jnp.zeros((E, H), jnp.float32), 'w_fast2': n(ks[8], (E, H, C)), 'w_slow2': n(ks[9], (E, H, C)), 'h_fast2': n(ks[10], (E, H, C), 0.005), 'm_gate2': jax.random.uniform(ks[11], (E,), dtype=jnp.float32), 'b2': jnp.zeros((E, C), jnp.float32)}
    _L0_ffn_all = _L0_ffn_setup()
    _L0_ffn_in = {k: v for k, v in _L0_ffn_all.items() if k in ('router_w', 'probe_w', 'router_emb', 'fatigue', 'energy', 'w_fast1', 'w_slow1', 'h_fast1', 'm_gate1', 'b1', 'w_fast2', 'w_slow2', 'h_fast2', 'm_gate2', 'b2')}
    del _L0_ffn_all
    return {'x': x, 'L0_tok_W_proj': _L0_tok_in['W_proj'], 'L0_tok_b_proj': _L0_tok_in['b_proj'], 'L0_tok_pos_table': _L0_tok_in['pos_table'], 'L0_attn_Wq': _L0_attn_in['Wq'], 'L0_attn_Wk': _L0_attn_in['Wk'], 'L0_attn_Wv': _L0_attn_in['Wv'], 'L0_attn_lambda_p': _L0_attn_in['lambda_p'], 'L0_attn_Wo': _L0_attn_in['Wo'], 'L0_attn_bo': _L0_attn_in['bo'], 'L0_ffn_router_w': _L0_ffn_in['router_w'], 'L0_ffn_probe_w': _L0_ffn_in['probe_w'], 'L0_ffn_router_emb': _L0_ffn_in['router_emb'], 'L0_ffn_fatigue': _L0_ffn_in['fatigue'], 'L0_ffn_energy': _L0_ffn_in['energy'], 'L0_ffn_w_fast1': _L0_ffn_in['w_fast1'], 'L0_ffn_w_slow1': _L0_ffn_in['w_slow1'], 'L0_ffn_h_fast1': _L0_ffn_in['h_fast1'], 'L0_ffn_m_gate1': _L0_ffn_in['m_gate1'], 'L0_ffn_b1': _L0_ffn_in['b1'], 'L0_ffn_w_fast2': _L0_ffn_in['w_fast2'], 'L0_ffn_w_slow2': _L0_ffn_in['w_slow2'], 'L0_ffn_h_fast2': _L0_ffn_in['h_fast2'], 'L0_ffn_m_gate2': _L0_ffn_in['m_gate2'], 'L0_ffn_b2': _L0_ffn_in['b2']}

def reference(x, L0_tok_W_proj, L0_tok_b_proj, L0_tok_pos_table, L0_attn_Wq, L0_attn_Wk, L0_attn_Wv, L0_attn_lambda_p, L0_attn_Wo, L0_attn_bo, L0_ffn_router_w, L0_ffn_probe_w, L0_ffn_router_emb, L0_ffn_fatigue, L0_ffn_energy, L0_ffn_w_fast1, L0_ffn_w_slow1, L0_ffn_h_fast1, L0_ffn_m_gate1, L0_ffn_b1, L0_ffn_w_fast2, L0_ffn_w_slow2, L0_ffn_h_fast2, L0_ffn_m_gate2, L0_ffn_b2):
    import jax
    import jax.numpy as jnp

    def _L0_tok_ref(images, W_proj, b_proj, pos_table):
        import jax, jax.numpy as jnp
        import numpy as np
        PATCH = 16

        def _patchify(images, p):
            B, H, W, C = images.shape
            gh, gw = (H // p, W // p)
            x = images.reshape(B, gh, p, gw, p, C)
            x = x.transpose(0, 1, 3, 2, 4, 5)
            return x.reshape(B, gh * gw, p * p * C)
        patches = _patchify(images, PATCH)
        emb = jnp.einsum('bnk,kd->bnd', patches, W_proj) + b_proj
        return emb + pos_table[None, :, :]

    def _L0_attn_ref(x, Wq, Wk, Wv, lambda_p, Wo, bo):
        import jax, jax.numpy as jnp
        import numpy as np
        H = 12

        def _attn(q, k, v):
            D = q.shape[-1]
            scores = jnp.einsum('bhnd,bhmd->bhnm', q, k) / jnp.sqrt(jnp.asarray(D, q.dtype))
            p = jax.nn.softmax(scores, axis=-1)
            return jnp.einsum('bhnm,bhmd->bhnd', p, v)
        B, N, C = x.shape
        D = C // H
        q = (x @ Wq).reshape(B, N, 2, H, D).transpose(2, 0, 3, 1, 4)
        k = (x @ Wk).reshape(B, N, 2, H, D).transpose(2, 0, 3, 1, 4)
        v = (x @ Wv).reshape(B, N, H, D).transpose(0, 2, 1, 3)
        out1 = _attn(q[0], k[0], v)
        out2 = _attn(q[1], k[1], v)
        lam = jnp.exp(lambda_p)
        out = out1 - lam * out2
        out = out.transpose(0, 2, 1, 3).reshape(B, N, C)
        return out @ Wo + bo

    def _L0_ffn_ref(x, router_w, probe_w, router_emb, fatigue, energy, w_fast1, w_slow1, h_fast1, m_gate1, b1, w_fast2, w_slow2, h_fast2, m_gate2, b2):
        import jax, jax.numpy as jnp
        import numpy as np
        B, T, C, H, E, TOPK, DR = (2, 512, 192, 768, 8, 2, 24)

        def _normalize(v, axis=-1, eps=1e-12):
            return v / jnp.maximum(jnp.linalg.norm(v, axis=axis, keepdims=True), eps)
        Bd, Td, Cd = x.shape
        logits = jnp.einsum('btc,ec->bte', x, router_w)
        tok_proxy = x.mean(axis=-1, keepdims=True)
        router_gain = jnp.linalg.norm(router_emb, axis=-1)
        base_bias = 0.02 * tok_proxy
        gain_bias = 0.02 * tok_proxy * router_gain
        tok_unit = _normalize(jnp.einsum('btc,dc->btd', x, probe_w))
        align_bias = 0.02 * jnp.einsum('btd,ed->bte', tok_unit, _normalize(router_emb))
        logits = logits + base_bias + gain_bias + align_bias + 0.1 * energy - 0.1 * fatigue
        g, idx = jax.lax.top_k(logits, TOPK)
        gates = jax.nn.softmax(g, axis=-1)
        N = Bd * Td
        gates_full = jnp.zeros((N, E), x.dtype).at[jnp.arange(N)[:, None], idx.reshape(N, TOPK)].set(gates.reshape(N, TOPK))
        flat_x = x.reshape(N, Cd)

        def body(acc, p):
            wf1, ws1, hf1, mg1, bb1, wf2, ws2, hf2, mg2, bb2, ge = p
            W1 = wf1 + mg1 * ws1 + hf1
            h = jnp.square(jnp.maximum(flat_x @ W1 + bb1, 0.0))
            W2 = wf2 + mg2 * ws2 + hf2
            y = h @ W2 + bb2
            return (acc + ge[:, None] * y, None)
        out, _ = jax.lax.scan(body, jnp.zeros((N, Cd), x.dtype), (w_fast1, w_slow1, h_fast1, m_gate1, b1, w_fast2, w_slow2, h_fast2, m_gate2, b2, gates_full.T))
        return out.reshape(Bd, Td, Cd)
    h = _L0_tok_ref(x, L0_tok_W_proj, L0_tok_b_proj, L0_tok_pos_table)
    h = h + _L0_attn_ref(_layernorm(h, axis=-1), L0_attn_Wq, L0_attn_Wk, L0_attn_Wv, L0_attn_lambda_p, L0_attn_Wo, L0_attn_bo)
    h = h + _L0_ffn_ref(_layernorm(h, axis=-1), L0_ffn_router_w, L0_ffn_probe_w, L0_ffn_router_emb, L0_ffn_fatigue, L0_ffn_energy, L0_ffn_w_fast1, L0_ffn_w_slow1, L0_ffn_h_fast1, L0_ffn_m_gate1, L0_ffn_b1, L0_ffn_w_fast2, L0_ffn_w_slow2, L0_ffn_h_fast2, L0_ffn_m_gate2, L0_ffn_b2)
    return h

_drawn_inputs = setup_inputs


def setup_inputs(seed=0):
    import zlib

    import numpy as np

    out = dict(_drawn_inputs(seed))
    spreads = {'L0_tok_b_proj': (0.0, 0.1),
     'L0_attn_lambda_p': (0.0, 0.8),
     'L0_attn_bo': (0.0, 0.517),
     'L0_ffn_fatigue': (0.0, 0.594),
     'L0_ffn_energy': (1.0, 0.555),
     'L0_ffn_b1': (0.0, 0.357),
     'L0_ffn_b2': (0.0, 0.8)}
    factors = {'L0_attn_Wq': 8.0,
     'L0_attn_Wk': 8.0,
     'L0_attn_Wv': 8.0,
     'L0_attn_Wo': 8.0,
     'L0_ffn_probe_w': 39.397,
     'L0_ffn_router_emb': 37.138,
     'L0_ffn_h_fast1': 3.737,
     'L0_ffn_m_gate1': 3.048,
     'L0_ffn_h_fast2': 4.38,
     'L0_ffn_m_gate2': 3.767}
    for name, (base, spread) in spreads.items():
        noise = np.random.default_rng([zlib.crc32(name.encode()), seed]).standard_normal(out[name].shape)
        drawn = base * np.exp(spread * noise) if base else spread * noise
        out[name] = jnp.asarray(drawn.astype(out[name].dtype))
    for name, factor in factors.items():
        out[name] = (out[name] * factor).astype(out[name].dtype)
    return out
```

```python
from contextlib import ExitStack

import numpy as np

import concourse.bass as bass
from concourse import mybir

F32 = mybir.dt.float32
F32R = mybir.dt.float32r
F16 = mybir.dt.float16
I32 = mybir.dt.int32
U32 = mybir.dt.uint32
ALU = mybir.AluOpType
ACT = mybir.ActivationFunctionType
AX = mybir.AxisListType.X

IMAGES, SIDE, CH, PATCH = 16, 96, 3, 16
GRID = SIDE // PATCH
KEYS = GRID * GRID
TOK = IMAGES * KEYS
C = 192
KP = C // 2
PK = PATCH * PATCH * CH // 128
GROUPS = 2
GI = IMAGES // GROUPS
GT = TOK // GROUPS
TT = 96
NT = TOK // TT
TG = NT // GROUPS
HEADS, D = 12, 16
TRI = 3
ROWS = TRI * KEYS
NTRI = HEADS // TRI
QC = 4
E, HID = 8, 768
HC = HID // 128
CAP = 256
ST = CAP // 128
ROUNDS = -(-TOK // CAP)
XROW = C + 4
DR = 24
EPS = 1e-5
BEYOND = 4096.0
FALLBACK_LINKS = 12
SBANK = (4, 0)
W1N, W2N = 2 * HID, HC * C

_cols = {}
_next = 0
for _name, _n in (("ident", 128), ("before", TT), ("qmask", TRI), ("hmask", TRI), ("lam", NTRI),
                  ("energy", E), ("fatigue", E), ("iota", E), ("token", NT),
                  ("slot", E * ST), ("expert", E * ST), ("bo", C), ("bp", C), ("rw", 2 * E),
                  ("probeT", 2 * DR), ("probe", C), ("embT", E)):
    _cols[_name] = (_next, _next + _n)
    _next += _n
SMALL = _next


def build(nc, patches, pos, wqk, wvo, small, w1, w2, wsmall, out):
    ctx = ExitStack()
    with ctx:
        def sb(name, shape, dt=F32):
            return ctx.enter_context(nc.sbuf_tensor(name, shape, dt))

        def sem(name):
            return ctx.enter_context(nc.semaphore(name))

        psum = ctx.enter_context(nc.psum_tensor("psum", [128, 8, 512], F32))
        bank = [psum[:, i, :] for i in range(8)]

        v_dram = nc.dram_tensor("v_rows", [TOK, C], F32, kind="Internal").ap()
        xs_dram = nc.dram_tensor("slot_rows", [E * CAP, XROW], F32, kind="Internal").ap()
        acc_dram = nc.dram_tensor("sum_rows", [TOK + CAP, C], F32, kind="Internal").ap()

        stage1 = sb("stage1", [128, 2, 3, W1N])
        stage2 = sb("stage2", [128, 2, 3, W2N])
        wsm = sb("wsm", [128, E, HC + 4])
        ready = sb("ready", [128, 2, 2 * W1N + 2 * W2N], F32R)
        w1h = [ready[0:KP, s, 0:W1N].rearrange("p (k n) -> p k n", k=2) for s in range(2)]
        w1l = [ready[0:KP, s, W1N:2 * W1N].rearrange("p (k n) -> p k n", k=2) for s in range(2)]
        w2h = [ready[:, s, 2 * W1N:2 * W1N + W2N].rearrange("p (k n) -> p k n", k=HC) for s in range(2)]
        w2l = [ready[:, s, 2 * W1N + W2N:].rearrange("p (k n) -> p k n", k=HC) for s in range(2)]
        PW = TOK + C
        pwraw = stage1[:, 1, :, :].rearrange("p a b -> p (a b)")[:, 0:PK * PW].rearrange("p (k n) -> p k n", k=PK)
        pwh = ready[:, 0, 0:PK * PW].rearrange("p (k n) -> p k n", k=PK)
        pwl = ready[:, 1, 0:PK * PW].rearrange("p (k n) -> p k n", k=PK)
        s2raw = stage2[0:KP, 1, :, :].rearrange("p a b -> p (a b)")
        QKN = 2 * 2 * QC * 128
        VON = 2 * 2 * C
        qkraw, voraw = s2raw[:, 0:QKN], s2raw[:, QKN:QKN + VON]
        fr = sb("fr", [128, 2, max(QKN + VON, 2 * HC * CAP)], F32R)
        wq = [fr[0:KP, s, 0:QKN].rearrange("p (k a c n) -> p k a c n", k=2, a=2, c=QC) for s in range(2)]
        wv = [fr[0:KP, s, QKN:QKN + VON].rearrange("p (k a n) -> p k a n", k=2, a=2) for s in range(2)]

        sm = sb("sm", [128, SMALL])

        def small_of(name, rows=128):
            a, b = _cols[name]
            return sm[0:rows, a:b]

        ones = sb("ones", [128, 128])
        ones16 = sb("ones16", [TT, 128], F16)
        before16 = sb("before16", [TT, TT], F16)
        nhalf = sb("nhalf", [128, E])
        phalf = sb("phalf", [128, E])
        zero = sb("zero", [128, XROW])
        held = sb("held", [1, E + 1])
        h = sb("h", [TT, NT, C])
        stats = sb("stats", [TT, 2, NT, 6])
        mv = sb("mv", [TT, 2, NT, 2])
        rstd = sb("rstd", [TT, 2, NT])
        xn = sb("xn", [128, TG * C])
        xnr = xn[0:TT, :].rearrange("p (t c) -> p t c", t=TG)
        xT = sb("xT", [KP, 2, 2, GT], F32R)
        qb = sb("qb", [128, 2, QC, GI, 128], F16)
        kT = sb("kT", [128, 2, QC, GT], F16)
        vrow = sb("vrow", [TT, TG, C])
        vb = sb("vb", [128, GROUPS * GI * 2 * 2 * TRI * D])
        vbd = vb[0:2 * KEYS, :].rearrange("p (g b a n) -> p g b a n", g=GROUPS, b=GI, a=2)
        ex = sb("ex", [ROWS, 3, 2 * NTRI, KEYS])
        dif = sb("dif", [ROWS, 4, NTRI, KEYS])
        mx = sb("mx", [ROWS, 2, 2 * NTRI])
        den = sb("den", [ROWS, 2, 2 * NTRI])
        rec = sb("rec", [ROWS, 3, 2 * NTRI])
        lam = sb("lam", [ROWS, NTRI])
        dT = sb("dT", [2 * KEYS, 2, 4, ROWS])
        oacc = sb("oacc", [KP, 2, 4, KEYS])
        oT = sb("oT", [KP, 2, 2, GT], F32R)
        xrow = sb("xrow", [TT, NT, XROW])
        x2T = sb("x2T", [KP, 2, 2, TT])
        rmat = sb("rmat", [KP, 2, 2 * E + DR])
        gain = sb("gain", [KP, 4, E])
        embsq = sb("embsq", [DR, E])
        lconst = sb("lconst", [TT, E])
        rsc = sb("rsc", [TT, TG, 2 * E + DR])
        usq = sb("usq", [TT, TG, DR])
        un = sb("un", [TT, 2, TG])
        logit = sb("logit", [TT, TG, E])
        top = sb("top", [TT, TG, 8])
        topi = sb("topi", [TT, TG, 8], U32)
        topf = sb("topf", [TT, NT, 2])
        gt = sb("gt", [TT, 4, TG])
        hot = sb("hot", [TT, TG * 2, E])
        hots = sb("hots", [TT, NT, E], F16)
        rk = sb("rk", [TT, TG, 2, E])
        rank = sb("rank", [TT, NT, 2])
        base = sb("base", [TT, NT, 2])
        live = sb("live", [TT, 2, NT, 2])
        place = sb("place", [TT, NT, 2])
        idx = sb("idx", [TT, NT, 2], U32)
        cnt = sb("cnt", [128, E])
        rounds_f = sb("rounds_f", [128, 3])
        rounds_i = sb("rounds_i", [128, 1], I32)
        slive = sb("slive", [128, E * ST])
        stok = sb("stok", [128, E * ST])
        sgate = sb("sgate", [128, E * ST])
        sidx = sb("sidx", [128, E * ST], U32)

        xs = qb[:, :, :, :, :].rearrange("p a c b n -> p (a c b n)").bitcast(F32)[:, 0:E * ST * XROW] \
            .rearrange("p (n c) -> p n c", c=XROW)
        hh = [fr[:, :, :].rearrange("p a n -> p (a n)")[:, (2 * s) * HC * CAP:(2 * s + 1) * HC * CAP]
              .rearrange("p (k n) -> p k n", k=HC) for s in range(2)]
        hl = [fr[:, :, :].rearrange("p a n -> p (a n)")[:, (2 * s + 1) * HC * CAP:(2 * s + 2) * HC * CAP]
              .rearrange("p (k n) -> p k n", k=HC) for s in range(2)]
        xg = [xT[:, :, :, 0:CAP], oT[:, :, :, 0:CAP]]
        relu = [vb[:, s * 2 * CAP:(s + 1) * 2 * CAP] for s in range(2)]
        hsq = [vb[:, (2 + s) * 2 * CAP:(3 + s) * 2 * CAP] for s in range(2)]
        yg = [vb[:, 8 * CAP + s * ST * C:8 * CAP + (s + 1) * ST * C].rearrange("p (s c) -> p s c", s=ST)
              for s in range(2)]
        yT = xn[0:KP, 0:2 * CAP].rearrange("p (m n) -> p m n", m=2)

        patch_in = [sem(f"patch_in{k}") for k in range(PK)]
        small_in, pos_in, qk_in, vo_in = sem("small_in"), sem("pos_in"), sem("qk_in"), sem("vo_in")
        st1_in = [sem(f"st1_in{s}") for s in range(2)]
        st2_in = [sem(f"st2_in{s}") for s in range(2)]
        zero_out, v_out, v_in = sem("zero_out"), [sem("v_out0"), sem("v_out1")], [sem("v_in0"), sem("v_in1")]
        acc_init, scattered = sem("acc_init"), sem("scattered")
        xs_in = [sem(f"xs_in{j}") for j in range(4)]
        added, out_done = sem("added"), sem("out_done")
        memset_done, v_zeroed, q_zeroed, pos_biased, h_biased = (
            sem("memset_done"), sem("v_zeroed"), sem("q_zeroed"), sem("pos_biased"), sem("h_biased"))
        pw_hi, pw_lo, qk_hi0, qk_lo0, vo_hi, vo_lo = (
            sem("pw_hi"), sem("pw_lo"), sem("qkw_hi"), sem("qkw_lo"), sem("vow_hi"), sem("vow_lo"))
        lam_done, consts16, emb_sq, gain_ps, gain_n2, gain_pow, rmat_done = (
            sem("lam_done"), sem("consts16"), sem("emb_sq"), sem("gain_ps"), sem("gain_n2"),
            sem("gain_pow"), sem("rmat_done"))
        emb_ready, emb_taken, mv_done, rstd_done, xn_done = (
            sem("emb_ready"), sem("emb_taken"), sem("mv_done"), sem("rstd_done"), sem("xn_done"))
        xT_ready, xT_hi, xT_lo = sem("xT_ready"), sem("xT_hi"), sem("xT_lo")
        qk_ready, qk_hi, qk_lo = sem("qk_ready"), sem("qk_hi"), sem("qk_lo")
        v_ready, v_taken = sem("v_ready"), sem("v_taken")
        s_ready, s_taken, mx_done, exp_done, den_done, rec_done, dif_done = (
            sem("s_ready"), sem("s_taken"), sem("mx_done"), sem("exp_done"), sem("den_done"),
            sem("rec_done"), sem("dif_done"))
        dT_ready, dT_taken, pv_ready, pv_taken, oT_done = (
            sem("dT_ready"), sem("dT_taken"), sem("pv_ready"), sem("pv_taken"), sem("oT_done"))
        wo_ready, h2_done, x2_done = sem("wo_ready"), sem("h2_done"), sem("x2_done")
        x2T_ready, x2T_taken, rt_ready, rt_taken = (
            sem("x2T_ready"), sem("x2T_taken"), sem("rt_ready"), sem("rt_taken"))
        un_clamped, un_pow, gap_done, gexp_done, row_done = (
            sem("un_clamped"), sem("un_pow"), sem("gap_done"), sem("gexp_done"), sem("row_done"))
        hots_done, rank_ready, rank_taken, count_ready = (
            sem("hots_done"), sem("rank_ready"), sem("rank_taken"), sem("count_ready"))
        count_taken = sem("count_taken")
        idx_done, rounds_done, sidx_done = sem("idx_done"), sem("rounds_done"), sem("sidx_done")
        w_added = [sem("w1_added"), sem("w2_added")]
        w_sum = [sem("w1_sum"), sem("w2_sum")]
        w_hi = [sem("w1_hi"), sem("w2_hi")]
        w_lo = [sem("w1_lo"), sem("w2_lo")]
        xg_ready, xg_hi, xg_lo = sem("xg_ready"), sem("xg_hi"), sem("xg_lo")
        l1_ready, relu_done, sq_done, h_hi, h_lo = (
            sem("l1_ready"), sem("relu_done"), sem("sq_done"), sem("h_hi"), sem("h_lo"))
        y_ready, yT_done, yb_ready, yg_done = sem("y_ready"), sem("yT_done"), sem("yb_ready"), sem("yg_done")
        dve_self = sem("dve_self")
        pool_self = sem("pool_self")

        def at(eng, s, value):
            if not isinstance(value, int) or value > 0:
                eng.wait_ge(s, value)

        ident = small_of("ident")
        identR = ident[0:ROWS, 0:ROWS]
        qmask = small_of("qmask")
        hmask = small_of("hmask", KP)

        def group(i):
            return i // TG, i % TG

        def bc(ap, axis, n):
            a = ap.unsqueeze(axis)
            shape = list(a.shape)
            shape[axis] = n
            return a.to_broadcast(shape)

        def gain_w(n, part):
            return wsm[0:(KP if part == 0 else 128), n % E, HC + 2 + part:HC + 3 + part]

        def rounds_of(eng):
            eng.wait_ge(rounds_done, 1)
            return eng.value_load(rounds_i[0:1, 0:1], min_val=1, max_val=ROUNDS)

        def more_rounds(eng, body):
            n = rounds_of(eng)
            with eng.If(n > 1):
                with eng.Fori(1, n) as r:
                    body(r)
            return n

        block = ctx.enter_context(nc.Block())

        @block.sync
        def _(sp):
            for k in range(PK):
                sp.dma_start(pwraw[:, k, :], patches[:, k, :]).then_inc(patch_in[k], 16)
            sp.dma_start(qkraw, wqk).then_inc(qk_in, 16)
            sp.dma_start(voraw, wvo).then_inc(vo_in, 16)

            def load1(r, e):
                at(sp, w_lo[0], E * r + e - 1)
                if isinstance(r, int) and r == 0 and e == 1:
                    sp.wait_ge(pw_lo, PK)
                sp.dma_start(stage1[0:KP, e % 2], w1[e]).then_inc(st1_in[e % 2], 16)

            def load2(r, e):
                at(sp, w_lo[1], E * r + e - 1)
                if isinstance(r, int) and r == 0 and e == 1:
                    sp.wait_ge(qk_lo0, 1)
                    sp.wait_ge(vo_lo, 1)
                sp.dma_start(stage2[:, e % 2], w2[e]).then_inc(st2_in[e % 2], 16)

            def load_slots(r):
                sp.wait_ge(scattered, (r + 1) * (2 * NT * 16))
                if isinstance(r, int):
                    sp.wait_ge(s_ready, IMAGES)
                for j in range(4):
                    sp.dma_start(xs[:, 4 * j:4 * j + 4, :],
                                 xs_dram.rearrange("(n p) c -> p n c", p=128)[:, 4 * j:4 * j + 4, :]) \
                      .then_inc(xs_in[j], 16)

            load1(0, 0)
            load2(0, 0)
            load1(0, 1)
            load2(0, 1)
            load1(0, 2)
            load2(0, 2)
            load1(0, 3)
            load2(0, 3)
            for g in range(GROUPS):
                sp.wait_ge(h2_done, TG * (g + 1))
                sp.dma_start(acc_dram[g * GT:(g + 1) * GT, :].rearrange("(t p) c -> p t c", p=TT),
                             h[:, TG * g:TG * (g + 1), :]).then_inc(acc_init, 16)
            load_slots(0)
            load1(0, 4)
            for e in range(4, E):
                if e + 1 < E:
                    load1(0, e + 1)
                load2(0, e)

            def fallback(r):
                sp.wait_ge(yg_done, E * r)
                load_slots(r)
                for e in range(E):
                    load1(r, e)
                    load2(r, e)

            n = more_rounds(sp, fallback)
            sp.wait_ge(added, n * (E * ST * 16))
            sp.dma_start(out, acc_dram[0:TOK, :]).then_inc(out_done, 16)
            sp.wait_ge(out_done, 16)

        @block.tensor
        def _(pe):
            mm = nc.tensor.matmul

            def three(out_, a, b, start, stop):
                mm(out_, a[0], b[0], start=start, stop=False)
                mm(out_, a[0], b[1], start=False, stop=False)
                return mm(out_, a[1], b[0], start=False, stop=stop)

            pe.wait_ge(small_in, 16)
            pe.wait_ge(memset_done, 1)
            pe.wait_ge(emb_sq, 1)
            for k in range(2):
                mm(bank[6][0:KP, k * E:(k + 1) * E], small_of("probe", DR)[:, k * KP:(k + 1) * KP],
                   small_of("embT", DR), start=True, stop=True)
            mm(bank[6][0:KP, 2 * E:3 * E], ones[0:DR, 0:KP], embsq[:, :], start=True, stop=True) \
                .then_inc(gain_ps, 1)

            for k in range(PK):
                pe.wait_ge(pw_lo, k + 1)
                for i in range(NT):
                    last = three(bank[i][0:TT, 0:C],
                                 [a[:, k, i * TT:(i + 1) * TT] for a in (pwh, pwl)],
                                 [a[:, k, TOK:] for a in (pwh, pwl)], k == 0, k == PK - 1)
                    if k == PK - 1:
                        last.then_inc(emb_ready, 1)

            def xT_tile(i):
                g, t = group(i)
                pe.wait_ge(xn_done, i + 1)
                at(pe, xT_lo, i - 1)
                if i == 0:
                    pe.wait_ge(rmat_done, 1)
                for k in range(2):
                    last = nc.tensor.transpose(bank[6 + i % 2][0:KP, k * TT:(k + 1) * TT],
                                               xnr[:, t, k * KP:(k + 1) * KP], ident[0:TT, 0:TT])
                last.then_inc(xT_ready, 1)

            def qk(g):
                pe.wait_ge(xT_lo, TG * (g + 1))
                pe.wait_ge(qk_lo0, 1)
                for m in range(2 * QC):
                    n = 2 * QC * g + m
                    if m >= 2:
                        pe.wait_ge(qk_lo, n - 1)
                    elif g:
                        pe.wait_ge(v_taken, TG * g)
                    else:
                        pe.wait_ge(emb_taken, 3 + m)
                    for k in range(2):
                        last = three(bank[2 + n % 2][:, 0:GT], [w[:, k, m % 2, m // 2, :] for w in wq],
                                     [xT[:, s, k, :] for s in range(2)], k == 0, k == 1)
                    last.then_inc(qk_ready, 1)

            def v(g):
                pe.wait_ge(vo_lo, 1)
                for t in range(TG):
                    i = TG * g + t
                    if t < 2:
                        pe.wait_ge(qk_lo, 2 * QC * (g + 1) - 1 + t)
                    else:
                        pe.wait_ge(v_taken, i - 1)
                    for k in range(2):
                        last = three(bank[2 + t % 2][0:TT, 0:C],
                                     [xT[:, s, k, t * TT:(t + 1) * TT] for s in range(2)],
                                     [w[:, k, 0, :] for w in wv], k == 0, k == 1)
                    last.then_inc(v_ready, 1)

            def scores(b):
                g, bi = b // GI, b % GI
                at(pe, s_taken, b - 1)
                if b < 2:
                    pe.wait_ge(emb_taken, NT)
                if bi == 0:
                    pe.wait_ge(qk_lo, 2 * QC * (g + 1))
                for c in range(QC):
                    for t in range(2):
                        rows = slice(64 * t, 64 * t + 64)
                        o = psum[:, SBANK[b % 2] + t, c * KEYS:(c + 1) * KEYS]
                        last = three(o, [qb[rows, s, c, bi, :] for s in range(2)],
                                     [kT[rows, s, c, bi * KEYS:(bi + 1) * KEYS] for s in range(2)],
                                     True, True)
                last.then_inc(s_ready, 1)

            def dT_pair(u):
                pe.wait_ge(dif_done, 2 * u + 2)
                at(pe, dT_taken, u)
                if u == 0:
                    pe.wait_ge(xT_lo, NT)
                for m in range(4):
                    b = 2 * u + m // 2
                    last = nc.tensor.transpose(
                        bank[6][0:2 * KEYS, m * ROWS:(m + 1) * ROWS],
                        dif[:, b % 4, 2 * (m % 2):2 * (m % 2) + 2, :].rearrange("p j n -> p (j n)"),
                        identR)
                last.then_inc(dT_ready, 1)

            def pv_pair(u):
                g = u // (GI // 2)
                pe.wait_ge(dT_taken, u + 1)
                pe.wait_ge(v_in[g], 64)
                at(pe, pv_taken, u)
                if u == 0:
                    pe.wait_ge(xT_lo, NT)
                for m in range(4):
                    bi = (2 * u + m // 2) % GI
                    last = mm(bank[7][0:KP, m * ROWS:(m + 1) * ROWS], vbd[:, g, bi, m % 2, :],
                              dT[:, u % 2, m, :], start=True, stop=True)
                last.then_inc(pv_ready, 1)

            def wo(g):
                pe.wait_ge(oT_done, GI // 2 * (g + 1))
                pe.wait_ge(v_taken, NT)
                for t in range(TG):
                    i = TG * g + t
                    at(pe, h2_done, i)
                    at(pe, rt_taken, g)
                    for k in range(2):
                        last = three(bank[2][0:TT, 0:C],
                                     [oT[:, s, k, t * TT:(t + 1) * TT] for s in range(2)],
                                     [w[:, k, 1, :] for w in wv], k == 0, k == 1)
                    last.then_inc(wo_ready, 1)

            def router(g):
                pe.wait_ge(h2_done, TG * (g + 1))
                for t in range(TG + 1):
                    if t < TG:
                        i = TG * g + t
                        pe.wait_ge(x2_done, i + 1)
                        at(pe, x2T_taken, i)
                        for k in range(2):
                            last = nc.tensor.transpose(bank[3][0:KP, k * TT:(k + 1) * TT],
                                                       xrow[:, i, k * KP:(k + 1) * KP],
                                                       ident[0:TT, 0:TT])
                        last.then_inc(x2T_ready, 1)
                    if t > 0:
                        i = TG * g + t - 1
                        pe.wait_ge(x2T_taken, i + 1)
                        for k in range(2):
                            last = mm(bank[2][0:TT, (t - 1) * (2 * E + DR):t * (2 * E + DR)],
                                      x2T[:, i % 2, k, :], rmat[:, k, :], start=(k == 0), stop=(k == 1))
                        last.then_inc(rt_ready, 1)

            def ranks(g):
                pe.wait_ge(consts16, 2)
                pe.wait_ge(hots_done, g + 1)
                pe.wait_ge(s_taken, IMAGES)
                at(pe, rank_taken, g)
                o = bank[1][0:TT, g * TG * E:(g + 1) * TG * E]
                mm(o, before16[:, :], hots[:, TG * g:TG * (g + 1), :].rearrange("p t e -> p (t e)"),
                   start=True, stop=False, skip_group_check=True)
                for j in range(TG * (g + 1) - 1):
                    first = max(j + 1, TG * g)
                    last = mm(bank[1][0:TT, first * E:(g + 1) * TG * E], ones16[:, 0:TT],
                              bc(hots[:, j, :], 1, TG * (g + 1) - first), start=False,
                              stop=(j == TG * (g + 1) - 2), skip_group_check=True)
                last.then_inc(rank_ready, 1)

            def counts():
                pe.wait_ge(pv_taken, IMAGES // 2)
                for i in range(NT):
                    last = mm(bank[7][:, 0:E], ones16[:, :], hots[:, i, :], start=(i == 0), stop=(i == NT - 1))
                last.then_inc(count_ready, 1)

            for i in range(TG):
                xT_tile(i)
            qk(0)
            v(0)
            for i in range(TG, NT):
                xT_tile(i)
            for b in range(IMAGES):
                scores(b)
                if b >= 3 and b % 2:
                    dT_pair((b - 3) // 2)
                if b >= 4 and b % 2 == 0:
                    pv_pair((b - 4) // 2)
                if b == GI - 1:
                    qk(1)
                    v(1)
                if b == GI + 3:
                    wo(0)
                if b == GI + 5:
                    router(0)
            pv_pair(IMAGES // 2 - 2)
            dT_pair(IMAGES // 2 - 1)
            ranks(0)
            pv_pair(IMAGES // 2 - 1)
            wo(1)
            router(1)
            ranks(1)
            counts()

            def slot_rows(r, e):
                pe.wait_ge(xs_in[e // 2], (r + 1) * 16)
                at(pe, xg_lo, E * r + e)
                if e == 0:
                    pe.wait_ge(s_taken, IMAGES)
                for k in range(2):
                    for s in range(ST):
                        last = nc.tensor.transpose(
                            bank[0][0:KP, k * CAP + s * 128:k * CAP + (s + 1) * 128],
                            xs[:, e * ST + s, k * KP:(k + 1) * KP], ident[:, :])
                last.then_inc(xg_ready, 1)

            def layer1(r, e, p):
                n = E * r + e
                if p == 0:
                    pe.wait_ge(xg_lo, n + 1)
                    pe.wait_ge(w_lo[0], n + 1)
                at(pe, relu_done, 3 * (n - 1) + p + 1)
                if isinstance(r, int) and n == 0:
                    pe.wait_ge(*((rank_taken, GROUPS), (rt_taken, GROUPS), (x2T_taken, NT))[p])
                for q in range(2):
                    for k in range(2):
                        last = three(bank[1 + p][:, q * CAP:(q + 1) * CAP],
                                     [w[e % 2][:, k, (2 * p + q) * 128:(2 * p + q + 1) * 128]
                                      for w in (w1h, w1l)],
                                     [xg[e % 2][:, s, k, :] for s in range(2)], k == 0, k == 1)
                last.then_inc(l1_ready, 1)

            def layer2(r, e, p):
                n = E * r + e
                pe.wait_ge(h_lo, 3 * n + p + 1)
                if p == 0:
                    pe.wait_ge(w_lo[1], n + 1)
                    at(pe, yT_done, n)
                    if isinstance(r, int) and n == 0:
                        pe.wait_ge(s_taken, IMAGES)
                for q in range(2):
                    for m in range(2):
                        c = 2 * p + q
                        last = three(bank[4 + m][0:KP, 0:CAP],
                                     [w[e % 2][:, c, m * KP:(m + 1) * KP] for w in (w2h, w2l)],
                                     [a[e % 2][:, c, :] for a in (hh, hl)], c == 0, c == HC - 1)
                if p == 2:
                    last.then_inc(y_ready, 1)

            def back(r, e):
                n = E * r + e
                pe.wait_ge(yT_done, n + 1)
                at(pe, yg_done, n)
                if isinstance(r, int) and n == 0:
                    pe.wait_ge(dT_taken, IMAGES // 2)
                for s in range(ST):
                    for m in range(2):
                        last = nc.tensor.transpose(
                            bank[6][:, s * C + m * KP:s * C + (m + 1) * KP],
                            yT[:, m, s * 128:(s + 1) * 128], ident[0:KP, 0:KP])
                last.then_inc(yb_ready, 1)

            slot_rows(0, 0)
            for s in range(E + 1):
                if s < E:
                    layer1(0, s, 0)
                if s >= 2:
                    back(0, s - 2)
                if s >= 1:
                    layer2(0, s - 1, 0)
                if s + 1 < E:
                    slot_rows(0, s + 1)
                for p in (1, 2):
                    if s < E:
                        layer1(0, s, p)
                    if s >= 1:
                        layer2(0, s - 1, p)
            back(0, E - 1)

            def fallback(r):
                for e in range(E):
                    slot_rows(r, e)
                    for p in range(3):
                        layer1(r, e, p)
                    for p in range(3):
                        layer2(r, e, p)
                    back(r, e)

            more_rounds(pe, fallback)

        @block.scalar
        def _(act):
            act.dma_start(sm[:, :], small).then_inc(small_in, 16)
            act.dma_start(wsm[:, :, :], wsmall).then_inc(small_in, 16)
            act.dma_start(h[:, :, :], pos).then_inc(pos_in, 16)
            for k in range(PK):
                act.wait_ge(patch_in[k], 16)
                nc.scalar.activation(pwh[:, k, :], pwraw[:, k, :], ACT.Copy).then_inc(pw_hi, 1)
            act.wait_ge(qk_in, 16)
            nc.scalar.activation(fr[0:KP, 0, 0:QKN], qkraw, ACT.Copy).then_inc(qk_hi0, 1)
            act.wait_ge(vo_in, 16)
            nc.scalar.activation(fr[0:KP, 0, QKN:QKN + VON], voraw, ACT.Copy).then_inc(vo_hi, 1)
            act.wait_ge(small_in, 32)
            nc.scalar.activation(lam[:, :], small_of("lam", ROWS), ACT.Exp).then_inc(lam_done, 1)

            def xT_high(i):
                g, t = group(i)
                act.wait_ge(xT_ready, i + 1)
                if i == TG:
                    act.wait_ge(v_ready, TG)
                nc.scalar.activation(xT[:, 0, :, t * TT:(t + 1) * TT],
                                     bank[6 + i % 2][0:KP, 0:2 * TT].rearrange("p (k n) -> p k n", k=2),
                                     ACT.Copy).then_inc(xT_hi, 1)

            def qk_high(g):
                if g:
                    act.wait_ge(s_ready, GI * g)
                else:
                    act.wait_ge(q_zeroed, 1)
                for m in range(2 * QC):
                    n, c = 2 * QC * g + m, m // 2
                    act.wait_ge(qk_ready, n + 1)
                    src = bank[2 + n % 2][:, 0:GT]
                    if m % 2:
                        nc.scalar.activation(kT[:, 0, c, :], src, ACT.Copy).then_inc(qk_hi, 1)
                    else:
                        src = src.rearrange("p (b n) -> p b n", b=GI)
                        for j in range(TRI):
                            last = nc.scalar.activation(
                                qb[:, 0, c, :, j * KEYS:(j + 1) * KEYS], src, ACT.Copy,
                                scale=qmask[:, j:j + 1])
                        last.then_inc(qk_hi, 1)

            def v_rows(g):
                for t in range(TG):
                    i = TG * g + t
                    act.wait_ge(v_ready, i + 1)
                    if g:
                        act.wait_ge(v_out[0], 16)
                    nc.scalar.activation(vrow[:, t, :], bank[2 + t % 2][0:TT, 0:C], ACT.Copy) \
                        .then_inc(v_taken, 1)
                act.wait_ge(v_taken, TG * (g + 1))
                act.dma_start(v_dram[g * GT:(g + 1) * GT, :].rearrange("(t p) c -> p t c", p=TT),
                              vrow[:, :, :]).then_inc(v_out[g], 16)

            def v_blocks(g):
                act.wait_ge(v_out[g], 16)
                act.wait_ge(v_zeroed, 1)
                n = TRI * D
                for j in range(2):
                    for a in range(2):
                        src = v_dram[g * GT:(g + 1) * GT, (2 * a + j) * n:(2 * a + j + 1) * n]
                        act.dma_start(vbd[j * KEYS:(j + 1) * KEYS, g, :, a, j * n:(j + 1) * n],
                                      src.rearrange("(b p) n -> p b n", p=KEYS)).then_inc(v_in[g], 16)

            def exps(b):
                act.wait_ge(s_taken, b + 1)
                nc.scalar.activation(ex[:, b % 3], ex[:, b % 3], ACT.Exp).then_inc(exp_done, 1)

            def dT_copy(u):
                act.wait_ge(dT_ready, u + 1)
                at(act, pv_ready, u - 1)
                nc.scalar.activation(dT[:, u % 2],
                                     bank[6][0:2 * KEYS, 0:4 * ROWS].rearrange("p (m n) -> p m n", m=4),
                                     ACT.Copy).then_inc(dT_taken, 1)

            def x2T_copy(i):
                act.wait_ge(x2T_ready, i + 1)
                at(act, rt_ready, i - 1)
                nc.scalar.activation(x2T[:, i % 2],
                                     bank[3][0:KP, 0:2 * TT].rearrange("p (k n) -> p k n", k=2),
                                     ACT.Copy).then_inc(x2T_taken, 1)

            def gap_exp(g):
                act.wait_ge(gap_done, g + 1)
                nc.scalar.activation(gt[:, 1, :], gt[:, 0, :], ACT.Exp).then_inc(gexp_done, 1)

            def w_high(r, e, part):
                n = E * r + e
                act.wait_ge(w_sum[part], n + 1)
                if isinstance(r, int) and n < 2:
                    act.wait_ge(emb_ready, NT)
                if part == 0:
                    at(act, l1_ready, 3 * (n - 1))
                    src = stage1[0:KP, e % 2, 0, :]
                    dst = w1h[e % 2].rearrange("p k n -> p (k n)")
                else:
                    at(act, y_ready, n - 1)
                    src = stage2[:, e % 2, 0, :]
                    dst = w2h[e % 2].rearrange("p k n -> p (k n)")
                nc.scalar.activation(dst, src, ACT.Copy).then_inc(w_hi[part], 1)

            for i in range(TG):
                xT_high(i)
            qk_high(0)
            v_rows(0)
            for i in range(TG, NT):
                xT_high(i)
            for b in range(IMAGES):
                exps(b)
                if b == 1:
                    v_blocks(0)
                if b >= 3 and b % 2:
                    dT_copy((b - 3) // 2)
                if b == GI - 1:
                    qk_high(1)
                    v_rows(1)
                if b == GI + 1:
                    v_blocks(1)
                if b == GI + 5:
                    for i in range(TG):
                        x2T_copy(i)
                if b == 4 or b == 6:
                    w_high(0, (b - 4) // 2, 0)
                    w_high(0, (b - 4) // 2, 1)
            gap_exp(0)
            dT_copy(IMAGES // 2 - 1)
            for i in range(TG, NT):
                x2T_copy(i)
            gap_exp(1)

            def slot_high(r, e):
                n = E * r + e
                act.wait_ge(xg_ready, n + 1)
                at(act, l1_ready, 3 * (n - 1))
                nc.scalar.activation(xg[e % 2][:, 0], bank[0][0:KP, :].rearrange("p (k n) -> p k n", k=2),
                                     ACT.Copy).then_inc(xg_hi, 1)

            def hidden(r, e, p):
                n = E * r + e
                j = 3 * n + p
                slot = (3 * e + p) % 2
                act.wait_ge(l1_ready, j + 1)
                at(act, sq_done, j - 1)
                for q in range(2):
                    last = nc.scalar.activation(
                        relu[slot][:, q * CAP:(q + 1) * CAP], bank[1 + p][:, q * CAP:(q + 1) * CAP],
                        ACT.Relu, bias=wsm[:, e, 2 * p + q:2 * p + q + 1])
                last.then_inc(relu_done, 1)
                act.wait_ge(relu_done, j + 1)
                at(act, h_lo, j - 1)
                nc.scalar.activation(hsq[slot], relu[slot], ACT.Square).then_inc(sq_done, 1)

            def y_bias(r, e):
                n = E * r + e
                act.wait_ge(y_ready, n + 1)
                at(act, yb_ready, n)
                for m in range(2):
                    last = nc.scalar.activation(yT[:, m, :], bank[4 + m][0:KP, 0:CAP], ACT.Identity,
                                                bias=wsm[0:KP, e, HC + m:HC + m + 1])
                last.then_inc(yT_done, 1)

            slot_high(0, 0)
            for s in range(E + 1):
                if s >= 2:
                    y_bias(0, s - 2)
                if s < E:
                    hidden(0, s, 0)
                if s + 1 < E:
                    slot_high(0, s + 1)
                    if s >= 1:
                        w_high(0, s + 1, 0)
                if s < E:
                    hidden(0, s, 1)
                    if s >= 2:
                        w_high(0, s, 1)
                    hidden(0, s, 2)
            y_bias(0, E - 1)

            def fallback(r):
                for e in range(E):
                    w_high(r, e, 0)
                    w_high(r, e, 1)
                    slot_high(r, e)
                    for p in range(3):
                        hidden(r, e, p)
                    y_bias(r, e)

            more_rounds(act, fallback)

        @block.vector
        def _(dve):
            vec = nc.vector
            links = [0]

            def link(ins, r=0):
                links[0] += 1
                ins.then_inc(dve_self, 1)
                dve.wait_ge(dve_self, links[0] + (0 if isinstance(r, int) else (r - 1) * FALLBACK_LINKS))

            dve.wait_ge(small_in, 32)
            vec.tensor_copy(before16[:, :], small_of("before", TT)).then_inc(consts16, 1)
            dve.wait_ge(memset_done, 1)
            vec.tensor_copy(ones16[:, :], ones[0:TT, :]).then_inc(consts16, 1)
            vec.tensor_tensor(embsq[:, :], small_of("embT", DR), small_of("embT", DR), ALU.mult) \
                .then_inc(emb_sq, 1)
            vec.tensor_tensor(lconst[:, :], small_of("energy", TT), small_of("fatigue", TT), ALU.subtract) \
                .then_inc(dve_self, 1)
            links[0] += 1
            for i in range(NT):
                vec.tensor_copy(xrow[:, i, C:C + 1], small_of("token", TT)[:, i:i + 1])
            dve.wait_ge(gain_ps, 1)
            link(vec.tensor_copy(gain[:, 0, :], bank[6][0:KP, 2 * E:3 * E]))
            vec.tensor_scalar(gain[:, 1, :], gain[:, 0, :], 1e-24, None, ALU.max).then_inc(gain_n2, 1)
            link(vec.tensor_scalar(lconst[:, :], lconst[:, :], 0.1, None, ALU.mult))

            def low(dst, src, hi):
                return vec.tensor_tensor(dst, src, hi.bitcast(F32), ALU.subtract)

            for k in range(PK):
                dve.wait_ge(pw_hi, k + 1)
                low(pwl[:, k, :], pwraw[:, k, :], pwh[:, k, :]).then_inc(pw_lo, 1)
            dve.wait_ge(qk_hi0, 1)
            low(fr[0:KP, 1, 0:QKN], qkraw, fr[0:KP, 0, 0:QKN]).then_inc(qk_lo0, 1)
            dve.wait_ge(vo_hi, 1)
            low(fr[0:KP, 1, QKN:QKN + VON], voraw, fr[0:KP, 0, QKN:QKN + VON]).then_inc(vo_lo, 1)
            dve.wait_ge(gain_pow, 2)
            link(vec.tensor_scalar(gain[:, 2, :], gain[:, 2, :], 1.0, 0.02 / C, ALU.add, ALU.mult))
            for k in range(2):
                vec.tensor_tensor(rmat[:, k, 0:E], small_of("rw", KP)[:, k * E:(k + 1) * E],
                                  gain[:, 2, :], ALU.add)
                vec.scalar_tensor_tensor(rmat[:, k, E:2 * E], bank[6][0:KP, k * E:(k + 1) * E], 0.02,
                                         gain[:, 3, :], ALU.mult, ALU.mult)
                last = vec.tensor_copy(rmat[:, k, 2 * E:], small_of("probeT", KP)[:, k * DR:(k + 1) * DR])
            last.then_inc(rmat_done, 1)

            def row_stats(ln, i, bnk, done):
                vec.tensor_tensor(h[:, i, :], bnk[0:TT, 0:C], h[:, i, :], ALU.add).then_inc(done, 1)

            def stats1(ln, i):
                vec.bn_stats(stats[:, ln, i, :], h[:, i, :]).then_inc(dve_self, 1)
                links[0] += 1

            def stats2(ln, i):
                vec.bn_aggr(mv[:, ln, i, :], stats[:, ln, i, :]).then_inc(mv_done, 1)

            def normalise(dst, ln, i):
                return vec.tensor_scalar(dst, h[:, i, :], mv[:, ln, i, 0:1], rstd[:, ln, i:i + 1],
                                         ALU.subtract, ALU.mult)

            dve.wait_ge(pos_biased, 1)
            for g in range(GROUPS):
                for i in range(TG * g, TG * g + TG):
                    dve.wait_ge(emb_ready, i + 1)
                    row_stats(0, i, bank[i], emb_taken)
                dve.wait_ge(emb_taken, TG * (g + 1))
                for i in range(TG * g, TG * g + TG):
                    stats1(0, i)
                dve.wait_ge(dve_self, links[0])
                for i in range(TG * g, TG * g + TG):
                    stats2(0, i)

            def ln1(g):
                dve.wait_ge(rstd_done, g + 1)
                if g:
                    dve.wait_ge(xT_ready, TG)
                for t in range(TG):
                    normalise(xnr[:, t, :], 0, TG * g + t).then_inc(xn_done, 1)

            def xT_low(i):
                g, t = group(i)
                dve.wait_ge(xT_hi, i + 1)
                vec.tensor_tensor(xT[:, 1, :, t * TT:(t + 1) * TT],
                                  bank[6 + i % 2][0:KP, 0:2 * TT].rearrange("p (k n) -> p k n", k=2),
                                  xT[:, 0, :, t * TT:(t + 1) * TT].bitcast(F32), ALU.subtract) \
                    .then_inc(xT_lo, 1)

            def qk_low(g):
                for m in range(2 * QC):
                    n, c = 2 * QC * g + m, m // 2
                    dve.wait_ge(qk_hi, n + 1)
                    src = bank[2 + n % 2][:, 0:GT]
                    if m % 2:
                        vec.tensor_tensor(kT[:, 1, c, :], src, kT[:, 0, c, :], ALU.subtract) \
                            .then_inc(qk_lo, 1)
                    else:
                        src = src.rearrange("p (b n) -> p b n", b=GI)
                        for j in range(TRI):
                            cols = slice(j * KEYS, (j + 1) * KEYS)
                            last = vec.scalar_tensor_tensor(
                                qb[:, 1, c, :, cols], src, qmask[:, j:j + 1], qb[:, 0, c, :, cols],
                                ALU.mult, ALU.subtract)
                        last.then_inc(qk_lo, 1)

            def softmax_top(b):
                s = psum[0:ROWS, SBANK[b % 2]:SBANK[b % 2] + 2, 0:QC * KEYS] \
                    .rearrange("p t (c n) -> p c t n", c=QC)
                dve.wait_ge(s_ready, b + 1)
                vec.reduce_max(mx[:, b % 2, :].rearrange("p (c t) -> p c t", t=2), s, AX).then_inc(mx_done, 1)
                if b >= 1:
                    softmax_sum(b - 1)
                dve.wait_ge(mx_done, b + 1)
                at(dve, dif_done, b - 2)
                vec.tensor_tensor(ex[:, b % 3].rearrange("p (c t) n -> p c t n", t=2), s,
                                  bc(mx[:, b % 2, :].rearrange("p (c t) -> p c t", t=2), 3, KEYS),
                                  ALU.subtract) \
                    .then_inc(s_taken, 1)
                if b >= 1:
                    softmax_scale(b - 1)

            def softmax_sum(b):
                dve.wait_ge(exp_done, b + 1)
                vec.reduce_sum(den[:, b % 2, :], ex[:, b % 3], AX).then_inc(den_done, 1)

            def softmax_scale(b):
                dve.wait_ge(den_done, b + 1)
                link(vec.reciprocal(rec[:, b % 3, :], den[:, b % 2, :]))
                if b == 0:
                    dve.wait_ge(lam_done, 1)
                vec.tensor_tensor(rec[:, b % 3, NTRI:], rec[:, b % 3, NTRI:], lam[:, :], ALU.mult) \
                    .then_inc(rec_done, 1)

            def diagonal(u):
                g = u // (GI // 2)
                o = bank[7][0:KP, 0:4 * ROWS].rearrange("p (m j n) -> p m j n", m=4, j=TRI)
                dve.wait_ge(pv_ready, u + 1)
                a = oacc[:, u % 2]
                link(vec.tensor_scalar(a, o[:, :, 0, :], hmask[:, 0:1], None, ALU.mult))
                link(vec.scalar_tensor_tensor(a, o[:, :, 1, :], hmask[:, 1:2], a, ALU.mult, ALU.add))
                vec.scalar_tensor_tensor(a, o[:, :, 2, :], hmask[:, 2:3], a, ALU.mult, ALU.add) \
                    .then_inc(pv_taken, 1)
                dve.wait_ge(pv_taken, u + 1)
                if u == GI // 2:
                    dve.wait_ge(wo_ready, TG)
                first = 2 * u * KEYS - g * GT
                src = a.rearrange("p (b k) n -> p k b n", b=2)
                halves = [oT[:, s, :, first:first + 2 * KEYS].rearrange("p k (b n) -> p k b n", b=2)
                          for s in range(2)]
                link(vec.tensor_copy(halves[0], src))
                vec.tensor_tensor(halves[1], src, halves[0].bitcast(F32), ALU.subtract) \
                    .then_inc(oT_done, 1)

            def residual(g):
                if g == 0:
                    dve.wait_ge(h_biased, 1)
                for i in range(TG * g, TG * g + TG):
                    dve.wait_ge(wo_ready, i + 1)
                    row_stats(1, i, bank[2], h2_done)
                dve.wait_ge(h2_done, TG * (g + 1))
                for i in range(TG * g, TG * g + TG):
                    stats1(1, i)
                dve.wait_ge(dve_self, links[0])
                for i in range(TG * g, TG * g + TG):
                    stats2(1, i)

            def ln2(g):
                dve.wait_ge(rstd_done, GROUPS + g + 1)
                for i in range(TG * g, TG * g + TG):
                    normalise(xrow[:, i, 0:C], 1, i).then_inc(x2_done, 1)

            def route_probe(g):
                dve.wait_ge(rt_ready, TG * (g + 1))
                vec.tensor_copy(rsc[:, :, :], bank[2][0:TT, 0:TG * (2 * E + DR)]
                                .rearrange("p (t n) -> p t n", t=TG)).then_inc(rt_taken, 1)
                dve.wait_ge(rt_taken, g + 1)
                link(vec.tensor_tensor(usq[:, :, :], rsc[:, :, 2 * E:], rsc[:, :, 2 * E:], ALU.mult))
                link(vec.reduce_sum(un[:, 0, :], usq[:, :, :], AX))
                vec.tensor_scalar(un[:, 1, :], un[:, 0, :], 1e-24, None, ALU.max).then_inc(un_clamped, 1)

            def route_choose(g):
                dve.wait_ge(un_pow, g + 1)
                link(vec.tensor_tensor(logit[:, :, :], rsc[:, :, E:2 * E], bc(un[:, 0, :], 2, E), ALU.mult))
                link(vec.tensor_tensor(logit[:, :, :], logit[:, :, :], rsc[:, :, 0:E], ALU.add))
                link(vec.tensor_tensor(logit[:, :, :], logit[:, :, :], bc(lconst[:, :], 1, TG), ALU.add))
                for t in range(TG):
                    vec.max(top[:, t, :], logit[:, t, :]).then_inc(dve_self, 1)
                links[0] += TG
                dve.wait_ge(dve_self, links[0])
                vec.tensor_tensor(gt[:, 0, :], top[:, :, 1], top[:, :, 0], ALU.subtract).then_inc(gap_done, 1)
                for t in range(TG):
                    vec.max_index(topi[:, t, :], top[:, t, :], logit[:, t, :]).then_inc(dve_self, 1)
                links[0] += TG
                dve.wait_ge(dve_self, links[0])
                tiles = slice(TG * g, TG * (g + 1))
                link(vec.tensor_copy(topf[:, tiles, :], topi[:, :, 0:2]))
                link(vec.tensor_tensor(
                    hot[:, :, :], bc(small_of("iota", TT), 1, 2 * TG),
                    bc(topf[:, tiles, :].rearrange("p t k -> p (t k)"), 2, E), ALU.is_equal))
                two = hot[:, :, :].rearrange("p (t k) e -> p t k e", k=2)
                vec.tensor_tensor(hots[:, tiles, :], two[:, :, 0, :], two[:, :, 1, :], ALU.add) \
                    .then_inc(hots_done, 1)
                link(vec.tensor_scalar(base[:, tiles, :], topf[:, tiles, :], float(CAP), None, ALU.mult))
                dve.wait_ge(gexp_done, g + 1)
                link(vec.tensor_scalar(gt[:, 2, :], gt[:, 1, :], 1.0, None, ALU.add))
                link(vec.reciprocal(gt[:, 3, :], gt[:, 2, :]))
                link(vec.tensor_tensor(xrow[:, tiles, C + 1], gt[:, 1, :], gt[:, 3, :], ALU.mult))
                vec.tensor_copy(xrow[:, tiles, C + 3], topf[:, tiles, 0])
                vec.tensor_tensor(xrow[:, tiles, C + 2], gt[:, 3, :], xrow[:, tiles, C + 1], ALU.subtract) \
                    .then_inc(row_done, 1)

            def route_rank(g):
                tiles = slice(TG * g, TG * (g + 1))
                dve.wait_ge(rank_ready, g + 1)
                src = bank[1][0:TT, g * TG * E:(g + 1) * TG * E].rearrange("p (t e) -> p t e", t=TG)
                vec.tensor_tensor(rk[:, :, :, :], hot[:, :, :].rearrange("p (t k) e -> p t k e", k=2),
                                  bc(src, 2, 2), ALU.mult).then_inc(rank_taken, 1)
                dve.wait_ge(rank_taken, g + 1)
                link(vec.reduce_sum(rank[:, tiles, :], rk[:, :, :, :], AX))
                place_rows(tiles, 0)

            def place_rows(tiles, r):
                a, b = rank[:, tiles, :], base[:, tiles, :]
                link(vec.tensor_scalar(live[:, 0, tiles, :], a, 0.0, None, ALU.is_ge), r)
                link(vec.scalar_tensor_tensor(live[:, 1, tiles, :], a, float(CAP), live[:, 0, tiles, :],
                                              ALU.is_lt, ALU.mult), r)
                link(vec.scalar_tensor_tensor(place[:, tiles, :], a, -BEYOND, b, ALU.add, ALU.add), r)
                link(vec.tensor_tensor(place[:, tiles, :], place[:, tiles, :], live[:, 1, tiles, :],
                                       ALU.mult), r)
                vec.tensor_scalar(idx[:, tiles, :], place[:, tiles, :], BEYOND, None, ALU.add) \
                    .then_inc(idx_done, 1)

            def count_rounds():
                dve.wait_ge(count_ready, 1)
                vec.tensor_copy(cnt[:, :], bank[7][:, 0:E]).then_inc(count_taken, 1)
                dve.wait_ge(count_taken, 1)
                link(vec.reduce_max(rounds_f[:, 0:1], cnt[:, :], AX))
                link(vec.tensor_scalar(rounds_f[:, 1:2], rounds_f[:, 0:1], float(CAP), 1.0,
                                       ALU.is_gt, ALU.add))
                for k in range(2, ROUNDS):
                    link(vec.tensor_scalar(rounds_f[:, 2:3], rounds_f[:, 0:1], float(k * CAP), None,
                                           ALU.is_gt))
                    link(vec.tensor_tensor(rounds_f[:, 1:2], rounds_f[:, 1:2], rounds_f[:, 2:3], ALU.add))
                vec.tensor_copy(rounds_i[:, :], rounds_f[:, 1:2]).then_inc(rounds_done, 1)

            def slots(r):
                n = small_of("slot")
                for j in range(4):
                    dve.wait_ge(xs_in[j], (r + 1) * 16)
                link(vec.tensor_tensor(slive[:, :].rearrange("p (e s) -> p e s", e=E),
                                       n.rearrange("p (e s) -> p e s", e=E), bc(cnt[:, :], 2, ST),
                                       ALU.is_lt), r)
                link(vec.scalar_tensor_tensor(stok[:, :], xs[:, :, C], -float(TOK), n,
                                              ALU.add, ALU.subtract), r)
                link(vec.tensor_tensor(stok[:, :], stok[:, :], slive[:, :], ALU.mult), r)
                link(vec.scalar_tensor_tensor(sidx[:, :], stok[:, :], float(TOK), n, ALU.add, ALU.add), r)
                link(vec.tensor_tensor(sgate[:, :], xs[:, :, C + 3], small_of("expert"), ALU.is_equal), r)
                link(vec.tensor_tensor(sgate[:, :], sgate[:, :], xs[:, :, C + 2], ALU.mult), r)
                vec.tensor_tensor(sgate[:, :], sgate[:, :], xs[:, :, C + 1], ALU.add).then_inc(sidx_done, 1)

            def staged(e, part, row):
                return stage1[0:KP, e % 2, row, :] if part == 0 else stage2[:, e % 2, row, :]

            def w_total(r, e, part):
                dve.wait_ge(w_added[part], E * r + e + 1)
                vec.scalar_tensor_tensor(staged(e, part, 0), staged(e, part, 0), gain_w(e, part),
                                         staged(e, part, 1), ALU.mult, ALU.add).then_inc(w_sum[part], 1)

            def w_low(r, e, part):
                dve.wait_ge(w_hi[part], E * r + e + 1)
                hi, lo = ((w1h, w1l), (w2h, w2l))[part]
                flat = "p k n -> p (k n)"
                low(lo[e % 2].rearrange(flat), staged(e, part, 0), hi[e % 2].rearrange(flat)) \
                    .then_inc(w_lo[part], 1)

            def slot_low(r, e):
                dve.wait_ge(xg_hi, E * r + e + 1)
                low(xg[e % 2][:, 1], bank[0][0:KP, :].rearrange("p (k n) -> p k n", k=2),
                    xg[e % 2][:, 0]).then_inc(xg_lo, 1)

            def hidden_halves(r, e, p):
                n = E * r + e
                j = 3 * n + p
                src = hsq[(3 * e + p) % 2].rearrange("p (q n) -> p q n", q=2)
                cs = slice(2 * p, 2 * p + 2)
                dve.wait_ge(sq_done, j + 1)
                at(dve, y_ready, n - 1)
                vec.tensor_copy(hh[e % 2][:, cs, :], src).then_inc(h_hi, 1)
                dve.wait_ge(h_hi, j + 1)
                low(hl[e % 2][:, cs, :], src, hh[e % 2][:, cs, :]).then_inc(h_lo, 1)

            def gated(r, e):
                n = E * r + e
                dve.wait_ge(yb_ready, n + 1)
                dve.wait_ge(sidx_done, r + 1)
                at(dve, added, (n - 1) * ST * 16)
                for s in range(ST):
                    last = vec.tensor_scalar(yg[e % 2][:, s, :], bank[6][:, s * C:(s + 1) * C],
                                             sgate[:, e * ST + s:e * ST + s + 1], None, ALU.mult)
                last.then_inc(yg_done, 1)

            ln1(0)
            for i in range(TG):
                xT_low(i)
            ln1(1)
            qk_low(0)
            for i in range(TG, NT):
                xT_low(i)
            for b in range(IMAGES):
                softmax_top(b)
                if b >= 4 and b % 2 == 0:
                    diagonal((b - 4) // 2)
                if b == GI - 1:
                    qk_low(1)
                if b in (3, 5):
                    w_total(0, (b - 3) // 2, 0)
                    w_total(0, (b - 3) // 2, 1)
                if b in (5, 7):
                    w_low(0, (b - 5) // 2, 0)
                    w_low(0, (b - 5) // 2, 1)
                if b == GI + 3:
                    residual(0)
                if b == GI + 4:
                    ln2(0)
                if b == GI + 6:
                    route_probe(0)
            softmax_sum(IMAGES - 1)
            softmax_scale(IMAGES - 1)
            diagonal(IMAGES // 2 - 2)
            route_choose(0)
            route_rank(0)
            diagonal(IMAGES // 2 - 1)
            residual(1)
            ln2(1)
            route_probe(1)
            route_choose(1)
            route_rank(1)
            count_rounds()
            slots(0)
            slot_low(0, 0)
            for s in range(E + 1):
                if 1 <= s and s + 1 < E:
                    w_total(0, s + 1, 0)
                if s < E:
                    hidden_halves(0, s, 0)
                if s >= 2:
                    gated(0, s - 2)
                if s + 1 < E:
                    slot_low(0, s + 1)
                if 2 <= s < E:
                    w_total(0, s, 1)
                if 1 <= s and s + 1 < E:
                    w_low(0, s + 1, 0)
                if s < E:
                    hidden_halves(0, s, 1)
                if 2 <= s < E:
                    w_low(0, s, 1)
                if s < E:
                    hidden_halves(0, s, 2)
            gated(0, E - 1)
            before = links[0]

            def fallback(r):
                dve.wait_ge(scattered, r * (2 * NT * 16))
                link(vec.tensor_scalar(rank[:, :, :], rank[:, :, :], -float(CAP), None, ALU.add), r)
                place_rows(slice(0, NT), r)
                dve.wait_ge(added, r * (E * ST * 16))
                link(vec.tensor_scalar(cnt[:, :], cnt[:, :], -float(CAP), None, ALU.add), r)
                slots(r)
                for e in range(E):
                    w_total(r, e, 0)
                    w_total(r, e, 1)
                    w_low(r, e, 0)
                    w_low(r, e, 1)
                    slot_low(r, e)
                    for p in range(3):
                        hidden_halves(r, e, p)
                    gated(r, e)
                assert links[0] - before == FALLBACK_LINKS

            more_rounds(dve, fallback)

        @block.gpsimd
        def _(pool):
            gp = nc.gpsimd
            links = [0]

            def link(ins):
                links[0] += 1
                ins.then_inc(pool_self, 1)
                pool.wait_ge(pool_self, links[0])

            gp.memset(ones[:, :], 1.0).then_inc(memset_done, 1)
            gp.memset(nhalf[:, :], -0.5)
            link(gp.memset(phalf[:, :], 0.5))
            link(gp.memset(zero[:, :], 0.0))
            pool.dma_start(xs_dram.rearrange("(n p) c -> p n c", p=128), bc(zero[:, :], 1, E * ST)) \
                .then_inc(zero_out, 16)
            pool.dma_start(acc_dram[TOK:, :].rearrange("(n p) c -> p n c", p=128),
                           bc(zero[:, 0:C], 1, ST)).then_inc(zero_out, 16)
            pool.wait_ge(gain_n2, 1)
            gp.tensor_tensor(gain[:, 2, :], gain[:, 0, :], phalf[0:KP, :], ALU.pow).then_inc(gain_pow, 1)
            gp.tensor_tensor(gain[:, 3, :], gain[:, 1, :], nhalf[0:KP, :], ALU.pow).then_inc(gain_pow, 1)
            pool.wait_ge(pos_in, 16)
            gp.tensor_tensor(h[:, :, :], h[:, :, :], bc(small_of("bp", TT), 1, NT), ALU.add) \
                .then_inc(pos_biased, 1)
            gp.memset(qb[:, :, :, :, ROWS:].rearrange("p a c b n -> p (a c b) n"), 0.0).then_inc(q_zeroed, 1)
            gp.memset(vb[0:2 * KEYS, :], 0.0).then_inc(v_zeroed, 1)

            def hold(k):
                gp.tensor_tensor(held[:, k:k + 1], zero[0:1, 0:1], zero[0:1, 1:2], ALU.add)

            def inverse_std(ln, g):
                tiles = slice(TG * g, TG * (g + 1))
                pool.wait_ge(mv_done, (ln * GROUPS + g + 1) * TG)
                link(gp.tensor_scalar(rstd[:, ln, tiles], mv[:, ln, tiles, 1], EPS, 1.0, ALU.add, ALU.mult))
                gp.tensor_tensor(rstd[:, ln, tiles], rstd[:, ln, tiles], nhalf[0:TT, 0:TG], ALU.pow) \
                    .then_inc(rstd_done, 1)

            def difference(b):
                pool.wait_ge(rec_done, b + 1)
                link(gp.tensor_tensor(ex[:, b % 3], ex[:, b % 3], bc(rec[:, b % 3, :], 2, KEYS), ALU.mult))
                at(pool, dT_ready, (b - 4) // 2 + 1 if b >= 4 else 0)
                gp.tensor_tensor(dif[:, b % 4], ex[:, b % 3, 0:NTRI], ex[:, b % 3, NTRI:], ALU.subtract) \
                    .then_inc(dif_done, 1)

            def w_add(r, e, part):
                s = (st1_in, st2_in)[part][e % 2]
                pool.wait_ge(s, (E // 2 * r + e // 2 + 1) * 16)
                a = stage1[0:KP, e % 2] if part == 0 else stage2[:, e % 2]
                gp.tensor_tensor(a[:, 1, :], a[:, 1, :], a[:, 2, :], ALU.add).then_inc(w_added[part], 1)

            def probe_norm(g):
                pool.wait_ge(un_clamped, g + 1)
                gp.tensor_tensor(un[:, 0, :], un[:, 1, :], nhalf[0:TT, 0:TG], ALU.pow).then_inc(un_pow, 1)

            def scatter(i, k):
                pool.indirect_dma_start(
                    xs_dram, bass.IndirectOffsetOnAxis(ap=idx[:, i, k:k + 1], axis=0), xrow[:, i, :], None,
                    bounds_check=E * CAP - 1, oob_is_err=False).then_inc(scattered, 16)

            def add_rows(r, e):
                n = E * r + e
                pool.wait_ge(yg_done, n + 1)
                at(pool, added, n * ST * 16)
                pool.wait_ge(acc_init, GROUPS * 16)
                if not isinstance(r, int):
                    hold(e)
                for s in range(ST):
                    j = e * ST + s
                    pool.indirect_dma_start(
                        acc_dram, bass.IndirectOffsetOnAxis(ap=sidx[:, j:j + 1], axis=0),
                        yg[e % 2][:, s, :], None, compute_op=ALU.add).then_inc(added, 16)

            inverse_std(0, 0)
            inverse_std(0, 1)
            w_add(0, 0, 0)
            w_add(0, 0, 1)
            pool.wait_ge(xn_done, NT)
            gp.tensor_tensor(h[:, :, :], h[:, :, :], bc(small_of("bo", TT), 1, NT), ALU.add) \
                .then_inc(h_biased, 1)
            for b in range(IMAGES):
                difference(b)
                if b == 2:
                    w_add(0, 1, 0)
                    w_add(0, 1, 1)
                if b == GI + 2:
                    inverse_std(1, 0)
                if b == GI + 5:
                    probe_norm(0)
            for e in (2, 3):
                for part in range(2):
                    w_add(0, e, part)
            pool.wait_ge(zero_out, 32)
            for g in range(GROUPS):
                if g:
                    inverse_std(1, 1)
                    probe_norm(1)
                pool.wait_ge(idx_done, g + 1)
                pool.wait_ge(row_done, g + 1)
                for i in range(TG * g, TG * (g + 1)):
                    for k in range(2):
                        scatter(i, k)
            for s in range(E + 2):
                if 4 <= s + 2 < E:
                    w_add(0, s + 2, 0)
                if s >= 2:
                    add_rows(0, s - 2)
                if 4 <= s + 1 < E:
                    w_add(0, s + 1, 1)

            def fallback(r):
                pool.wait_ge(idx_done, GROUPS + r)
                for j in range(4):
                    pool.wait_ge(xs_in[j], r * 16)
                hold(E)
                for i in range(NT):
                    for k in range(2):
                        scatter(i, k)
                for e in range(E):
                    w_add(r, e, 0)
                    w_add(r, e, 1)
                    add_rows(r, e)

            more_rounds(pool, fallback)


_INPUTS = ("patches", "pos", "wqk", "wvo", "small", "w1", "w2", "wsmall")


def kernel(**inputs):
    import concourse.bacc as bacc
    from concourse.bass_utils import run_bass_kernel_spmd as run

    a = {k: np.asarray(v) for k, v in inputs.items()}
    f = "L0_ffn_"
    x = a["x"].reshape(IMAGES, GRID, PATCH, GRID, PATCH, CH).transpose(2, 4, 5, 0, 1, 3)
    chunks = lambda m, n: m.reshape(n, m.shape[0] // n, *m.shape[1:]).swapaxes(0, 1)
    arrays = {}
    arrays["patches"] = np.concatenate([chunks(x.reshape(PATCH * PATCH * CH, TOK), PK),
                                        chunks(a["L0_tok_W_proj"], PK)], axis=2)
    arrays["pos"] = chunks(np.tile(a["L0_tok_pos_table"], (IMAGES, 1)), NT)
    wqk = np.zeros((KP, 2, 2, QC, 128), np.float32)
    for j, name in enumerate(("L0_attn_Wq", "L0_attn_Wk")):
        w = chunks(a[name], 2).reshape(KP, 2, QC, 2, TRI * D)
        for t in range(2):
            wqk[:, :, j, :, 64 * t:64 * t + TRI * D] = w[:, :, :, t, :]
    arrays["wqk"] = wqk.reshape(KP, -1)
    arrays["wvo"] = np.stack([chunks(a["L0_attn_Wv"], 2), chunks(a["L0_attn_Wo"], 2)], 2).reshape(KP, -1)
    arrays["w1"] = np.stack([a[f + n].reshape(E, 2, KP, HID).swapaxes(1, 2).reshape(E, KP, W1N)
                             for n in ("w_slow1", "w_fast1", "h_fast1")], 2)
    arrays["w2"] = np.stack([a[f + n].reshape(E, HC, 128, C).swapaxes(1, 2).reshape(E, 128, W2N)
                             for n in ("w_slow2", "w_fast2", "h_fast2")], 2)
    ws = np.zeros((128, E, HC + 4), np.float32)
    ws[:, :, 0:HC] = a[f + "b1"].reshape(E, HC, 128).transpose(2, 0, 1)
    ws[0:KP, :, HC:HC + 2] = a[f + "b2"].reshape(E, 2, KP).transpose(2, 0, 1)
    ws[:, :, HC + 2] = a[f + "m_gate1"]
    ws[:, :, HC + 3] = a[f + "m_gate2"]
    arrays["wsmall"] = ws

    s = np.zeros((128, SMALL), np.float32)

    def put(name, value):
        lo, hi = _cols[name]
        s[0:value.shape[0], lo:hi] = value.reshape(value.shape[0], -1)

    p = np.arange(128)[:, None]
    put("ident", np.eye(128, dtype=np.float32))
    put("before", np.triu(np.ones((TT, TT), np.float32), 1))
    head = lambda q, n: (q // D == n) & (q < TRI * D)
    put("qmask", np.where(head(p % 64, np.arange(TRI)), np.float32(D ** -0.5), np.float32(0)))
    put("hmask", head(p[0:KP] % (TRI * D), np.arange(TRI)).astype(np.float32))
    put("lam", np.repeat(a["L0_attn_lambda_p"].reshape(NTRI, TRI).T, KEYS, axis=0))
    put("energy", np.tile(a[f + "energy"], (128, 1)))
    put("fatigue", np.tile(a[f + "fatigue"], (128, 1)))
    put("iota", np.tile(np.arange(E, dtype=np.float32), (128, 1)))
    put("token", (p[0:TT] + TT * np.arange(NT)).astype(np.float32))
    n = np.arange(E * ST)
    put("slot", (p + 128 * (n % ST)).astype(np.float32))
    put("expert", np.tile((n // ST).astype(np.float32), (128, 1)))
    put("bo", np.tile(a["L0_attn_bo"], (128, 1)))
    put("bp", np.tile(a["L0_tok_b_proj"], (128, 1)))
    put("rw", chunks(a[f + "router_w"].T, 2))
    put("probeT", chunks(a[f + "probe_w"].T, 2))
    put("probe", a[f + "probe_w"])
    put("embT", a[f + "router_emb"].T)
    arrays["small"] = s
    arrays = {f"in_{k}": np.ascontiguousarray(arrays[k]) for k in _INPUTS}

    nc = bacc.Bacc("TRN2", target_bir_lowering=False, num_devices=1)
    ins = [nc.dram_tensor(k, v.shape, mybir.dt.from_np(v.dtype), kind="ExternalInput").ap()
           for k, v in arrays.items()]
    out = nc.dram_tensor("out_rows", (TOK, C), F32, kind="ExternalOutput").ap()
    build(nc, *ins, out)
    r = run(nc, [arrays], core_ids=[0])
    return r.results[0]["out_rows"].reshape(IMAGES, KEYS, C)
```

```python
from contextlib import ExitStack

import numpy as np

import concourse.bass as bass
from concourse import mybir

F32 = mybir.dt.float32
F32R = mybir.dt.float32r
F16 = mybir.dt.float16
I32 = mybir.dt.int32
U32 = mybir.dt.uint32
ALU = mybir.AluOpType
ACT = mybir.ActivationFunctionType
AX = mybir.AxisListType.X

IMAGES, SIDE, CH, PATCH = 16, 96, 3, 16
GRID = SIDE // PATCH
KEYS = GRID * GRID
TOK = IMAGES * KEYS
C = 192
KP = C // 2
PK = PATCH * PATCH * CH // 128
GROUPS = 2
GI = IMAGES // GROUPS
GT = TOK // GROUPS
TT = 96
NT = TOK // TT
TG = NT // GROUPS
HEADS, D = 12, 16
TRI = 3
ROWS = TRI * KEYS
NTRI = HEADS // TRI
QC = 4
E, HID = 8, 768
HC = HID // 128
CAP = 256
ST = CAP // 128
ROUNDS = -(-TOK // CAP)
XROW = C + 4
DR = 24
EPS = 1e-5
XS_PARTS = ((0, 1), (1, 2), (2, 4), (4, 8))
STAGES = 3
BEYOND = 4096.0
FALLBACK_LINKS = 12
SBANK = (4, 0)
QKBANK = (2, 3, 0, 1)
RANKBANK = (3, 1)
W1N, W2N = 2 * HID, HC * C

_cols = {}
_next = 0
for _name, _n in (("ident", 128), ("before", TT), ("qmask", TRI), ("lam", NTRI),
                  ("energy", E), ("fatigue", E), ("iota", E), ("token", NT),
                  ("slot", E * ST), ("expert", E * ST), ("bo", C), ("bp", C), ("rw", 2 * E),
                  ("probeT", 2 * DR), ("probe", C), ("embT", E)):
    _cols[_name] = (_next, _next + _n)
    _next += _n
SMALL = _next


def build(nc, patches, pos, wqk, wvo, small, w1, w2, wsmall, out):
    ctx = ExitStack()
    with ctx:
        def sb(name, shape, dt=F32):
            return ctx.enter_context(nc.sbuf_tensor(name, shape, dt))

        def sem(name):
            return ctx.enter_context(nc.semaphore(name))

        psum = ctx.enter_context(nc.psum_tensor("psum", [128, 8, 512], F32))
        bank = [psum[:, i, :] for i in range(8)]

        v_dram = nc.dram_tensor("v_rows", [2, TOK, C], F32, kind="Internal").ap()
        xs_dram = nc.dram_tensor("slot_rows", [E * CAP, XROW], F32, kind="Internal").ap()

        stage1 = sb("stage1", [128, STAGES, 2, W1N])
        stage2 = sb("stage2", [128, STAGES, 2, W2N])
        wsm = sb("wsm", [128, E, HC + 4])
        ready = sb("ready", [128, 2, 2 * W1N + 2 * W2N], F32R)
        w1h = [ready[0:KP, s, 0:W1N].rearrange("p (k n) -> p k n", k=2) for s in range(2)]
        w1l = [ready[0:KP, s, W1N:2 * W1N].rearrange("p (k n) -> p k n", k=2) for s in range(2)]
        w2h = [ready[:, s, 2 * W1N:2 * W1N + W2N].rearrange("p (k n) -> p k n", k=HC) for s in range(2)]
        w2l = [ready[:, s, 2 * W1N + W2N:].rearrange("p (k n) -> p k n", k=HC) for s in range(2)]
        PW = TOK + C
        pwraw = stage1[:, 1:, :, :].rearrange("p s a b -> p (s a b)")[:, 0:PK * PW].rearrange("p (k n) -> p k n", k=PK)
        pwh = ready[:, 0, 0:PK * PW].rearrange("p (k n) -> p k n", k=PK)
        pwl = ready[:, 1, 0:PK * PW].rearrange("p (k n) -> p k n", k=PK)
        s2raw = stage2[0:KP, 1:, :, :].rearrange("p s a b -> p (s a b)")
        QKN = 2 * 2 * QC * 128
        VON = 2 * 2 * C
        qkraw, voraw = s2raw[:, 0:QKN], s2raw[:, QKN:QKN + VON]
        fr = sb("fr", [128, 2, max(QKN + VON, 2 * HC * CAP)], F32R)
        wq = [fr[0:KP, s, 0:QKN].rearrange("p (k a c n) -> p k a c n", k=2, a=2, c=QC) for s in range(2)]
        wv = [fr[0:KP, s, QKN:QKN + VON].rearrange("p (k a n) -> p k a n", k=2, a=2) for s in range(2)]

        sm = sb("sm", [128, SMALL])

        def small_of(name, rows=128):
            a, b = _cols[name]
            return sm[0:rows, a:b]

        ones = sb("ones", [128, 128])
        ones16 = sb("ones16", [TT, 128], F16)
        before16 = sb("before16", [TT, TT], F16)
        nhalf = sb("nhalf", [128, E])
        phalf = sb("phalf", [128, E])
        zero = sb("zero", [128, XROW])
        held = sb("held", [1, 3 * E + 2])
        h = sb("h", [TT, NT, C])
        stats = sb("stats", [TT, 2, NT, 6])
        mv = sb("mv", [TT, 2, NT, 2])
        rstd = sb("rstd", [TT, 2, NT])
        xn = sb("xn", [128, TG * C])
        xnr = xn[0:TT, :].rearrange("p (t c) -> p t c", t=TG)
        xT = sb("xT", [KP, 2, 2, GT], F32R)
        qb = sb("qb", [128, 2, QC, GI, 128], F16)
        kT = sb("kT", [128, 2, QC, GT], F16)
        vrow = sb("vrow", [TT, TG, 2, C])
        vb = sb("vb", [128, GROUPS * GI * 2 * 2 * TRI * D])
        vbd = vb[0:2 * KEYS, :].rearrange("p (g b a j n) -> p g b a j n", g=GROUPS, b=GI, a=2, j=TRI)
        ex = sb("ex", [ROWS, 3, 2 * NTRI, KEYS])
        dif = sb("dif", [ROWS, 4, NTRI, KEYS])
        mx = sb("mx", [ROWS, 2, 2 * NTRI])
        den = sb("den", [ROWS, 2, 2 * NTRI])
        rec = sb("rec", [ROWS, 3, 2 * NTRI])
        lam = sb("lam", [ROWS, NTRI])
        dT = sb("dT", [2 * KEYS, 2, 4, ROWS])
        oT = sb("oT", [KP, 2, 2, GT], F32R)
        xrow = sb("xrow", [TT, NT, XROW])
        x2T = sb("x2T", [KP, 2, 2, TT])
        rmat = sb("rmat", [KP, 2, 2 * E + DR])
        gain = sb("gain", [KP, 4, E])
        embsq = sb("embsq", [DR, E])
        lconst = sb("lconst", [TT, E])
        rsc = sb("rsc", [TT, TG, 2 * E + DR])
        usq = sb("usq", [TT, TG, DR])
        un = sb("un", [TT, 2, TG])
        logit = sb("logit", [TT, TG, E])
        top = sb("top", [TT, TG, 8])
        topi = sb("topi", [TT, TG, 8], U32)
        topf = sb("topf", [TT, NT, 2])
        gt = sb("gt", [TT, 4, TG])
        hot = sb("hot", [TT, TG * 2, E])
        hots = sb("hots", [TT, NT, E], F16)
        rk = sb("rk", [TT, TG, 2, E])
        rank = sb("rank", [TT, NT, 2])
        base = sb("base", [TT, NT, 2])
        live = sb("live", [TT, 2, NT, 2])
        place = sb("place", [TT, NT, 2])
        idx = sb("idx", [TT, NT, 2], U32)
        cnt = sb("cnt", [128, E])
        rounds_f = sb("rounds_f", [128, 3])
        rounds_i = sb("rounds_i", [128, 1], I32)
        slive = sb("slive", [128, E * ST])
        stok = sb("stok", [128, E * ST])
        sgate = sb("sgate", [128, E * ST])
        sidx = sb("sidx", [128, E * ST], U32)

        xs = qb[:, :, :, :, :].rearrange("p a c b n -> p (a c b n)").bitcast(F32)[:, 0:E * ST * XROW] \
            .rearrange("p (n c) -> p n c", c=XROW)
        hh = [fr[:, :, :].rearrange("p a n -> p (a n)")[:, (2 * s) * HC * CAP:(2 * s + 1) * HC * CAP]
              .rearrange("p (k n) -> p k n", k=HC) for s in range(2)]
        hl = [fr[:, :, :].rearrange("p a n -> p (a n)")[:, (2 * s + 1) * HC * CAP:(2 * s + 2) * HC * CAP]
              .rearrange("p (k n) -> p k n", k=HC) for s in range(2)]
        xg = [xT[:, :, :, 0:CAP], oT[:, :, :, 0:CAP]]
        relu = [vb[:, s * 2 * CAP:(s + 1) * 2 * CAP] for s in range(2)]
        hsq = [vb[:, (2 + s) * 2 * CAP:(3 + s) * 2 * CAP] for s in range(2)]
        yg = [vb[:, 8 * CAP + s * ST * C:8 * CAP + (s + 1) * ST * C].rearrange("p (s c) -> p s c", s=ST)
              for s in range(2)]
        yT = xn[0:KP, 0:2 * CAP].rearrange("p (m n) -> p m n", m=2)

        patch_in = [sem(f"patch_in{k}") for k in range(PK)]
        small_in, pos_in, qk_in, vo_in, wsmall_in = (
            sem("small_in"), sem("pos_in"), sem("qk_in"), sem("vo_in"), sem("wsmall_in"))
        slow_in = [[sem(f"slow{p}_in{s}") for s in range(STAGES)] for p in (1, 2)]
        fast_in = [[sem(f"fast{p}_in{s}") for s in range(STAGES)] for p in (1, 2)]
        zero_out, v_out, v_in = sem("zero_out"), [sem("v_out0"), sem("v_out1")], [sem("v_in0"), sem("v_in1")]
        acc_init, scattered = sem("acc_init"), sem("scattered")
        xs_in = [sem(f"xs_in{j}") for j in range(len(XS_PARTS))]
        added = sem("added")
        memset_done, v_zeroed, q_zeroed, pos_biased, h_biased = (
            sem("memset_done"), sem("v_zeroed"), sem("q_zeroed"), sem("pos_biased"), sem("h_biased"))
        pw_hi, pw_lo, qk_hi0, qk_lo0, vo_hi, vo_lo = (
            sem("pw_hi"), sem("pw_lo"), sem("qkw_hi"), sem("qkw_lo"), sem("vow_hi"), sem("vow_lo"))
        lam_done, consts16, emb_sq, gain_ps, gain_n2, gain_pow, rmat_done = (
            sem("lam_done"), sem("consts16"), sem("emb_sq"), sem("gain_ps"), sem("gain_n2"),
            sem("gain_pow"), sem("rmat_done"))
        emb_ready, emb_taken, mv_done, rstd_done, xn_done = (
            sem("emb_ready"), sem("emb_taken"), sem("mv_done"), sem("rstd_done"), sem("xn_done"))
        xT_ready, xT_hi, xT_lo = sem("xT_ready"), sem("xT_hi"), sem("xT_lo")
        qk_ready, qk_hi, qk_lo = sem("qk_ready"), sem("qk_hi"), sem("qk_lo")
        v_ready, v_taken = sem("v_ready"), sem("v_taken")
        s_ready, s_taken, mx_done, exp_done, den_done, rec_done, dif_done = (
            sem("s_ready"), sem("s_taken"), sem("mx_done"), sem("exp_done"), sem("den_done"), sem("rec_done"),
            sem("dif_done"))
        dT_ready, dT_taken, pv_ready, oT_hi, oT_done = (
            sem("dT_ready"), sem("dT_taken"), sem("pv_ready"), sem("oT_hi"), sem("oT_done"))
        wo_ready, h2_done, x2_done = sem("wo_ready"), sem("h2_done"), sem("x2_done")
        x2T_ready, x2T_taken, rt_ready, rt_taken = (
            sem("x2T_ready"), sem("x2T_taken"), sem("rt_ready"), sem("rt_taken"))
        un_clamped, un_pow, gap_done, gexp_done, row_done = (
            sem("un_clamped"), sem("un_pow"), sem("gap_done"), sem("gexp_done"), sem("row_done"))
        hots_done, rank_ready, rank_taken, count_ready = (
            sem("hots_done"), sem("rank_ready"), sem("rank_taken"), sem("count_ready"))
        count_taken = sem("count_taken")
        idx_done, rounds_done, sidx_done = sem("idx_done"), sem("rounds_done"), sem("sidx_done")
        w_added = [[sem(f"w{p}_added{s}") for s in range(STAGES)] for p in (1, 2)]
        w_sum = [sem("w1_sum"), sem("w2_sum")]
        w_hi = [sem("w1_hi"), sem("w2_hi")]
        w_lo = [sem("w1_lo"), sem("w2_lo")]
        xg_ready, xg_hi, xg_lo = sem("xg_ready"), sem("xg_hi"), sem("xg_lo")
        l1_ready, relu_done, sq_done, h_hi, h_lo = (
            sem("l1_ready"), sem("relu_done"), sem("sq_done"), sem("h_hi"), sem("h_lo"))
        y_ready, yT_done, yb_ready, yg_done = sem("y_ready"), sem("yT_done"), sem("yb_ready"), sem("yg_done")
        dve_self = sem("dve_self")
        pool_self = sem("pool_self")

        def at(eng, s, value):
            if not isinstance(value, int) or value > 0:
                eng.wait_ge(s, value)

        ident = small_of("ident")
        identR = ident[0:ROWS, 0:ROWS]
        qmask = small_of("qmask")

        def group(i):
            return i // TG, i % TG

        def bc(ap, axis, n):
            a = ap.unsqueeze(axis)
            shape = list(a.shape)
            shape[axis] = n
            return a.to_broadcast(shape)

        def outputs(u):
            first = 2 * u * KEYS - u // (GI // 2) * GT
            src = bank[7][0:KP, 0:4 * KEYS].rearrange("p (b k n) -> p k b n", b=2, k=2)
            return src, [oT[:, s, :, first:first + 2 * KEYS].rearrange("p k (b n) -> p k b n", b=2)
                         for s in range(2)]

        def staged(e, part):
            return stage1[0:KP, e % STAGES] if part == 0 else stage2[:, e % STAGES]

        def staged_count(r, e):
            return ((E - 1 - e % STAGES) // STAGES + 1) * 16 * r + (e // STAGES + 1) * 16

        def gain_w(n, part):
            return wsm[0:(KP if part == 0 else 128), n % E, HC + 2 + part:HC + 3 + part]

        def rounds_of(eng):
            eng.wait_ge(rounds_done, 1)
            return eng.value_load(rounds_i[0:1, 0:1], min_val=1, max_val=ROUNDS)

        def more_rounds(eng, body):
            n = rounds_of(eng)
            with eng.If(n > 1):
                with eng.Fori(1, n) as r:
                    body(r)
            return n

        block = ctx.enter_context(nc.Block())

        @block.sync
        def _(sp):
            for k in range(PK):
                sp.dma_start(pwraw[:, k, :], patches[:, k, :]).then_inc(patch_in[k], 16)
            sp.dma_start(qkraw, wqk).then_inc(qk_in, 16)
            sp.dma_start(voraw, wvo).then_inc(vo_in, 16)
            sp.dma_start(wsm[:, :, :], wsmall).then_inc(wsmall_in, 16)

            def load(r, e, part):
                if isinstance(r, int):
                    at(sp, w_lo[part], e - STAGES + 1)
                    if 0 < e < STAGES:
                        sp.wait_ge(*((pw_lo, PK), (vo_lo, 1))[part])
                        sp.wait_ge(*((pw_lo, PK), (qk_lo0, 1))[part])
                else:
                    sp.wait_ge(w_lo[part], E * r + (e - STAGES + 1 if e >= STAGES else 0))
                for row in (1, 0):
                    sp.dma_start(staged(e, part)[:, row, :], (w1, w2)[part][e, :, row]) \
                      .then_inc((slow_in, fast_in)[row][part][e % STAGES], 16)

            for e in range(E):
                if e == 1:
                    sp.wait_ge(v_in[1], 32)
                if e == STAGES + 1:
                    sp.wait_ge(xs_in[-1], 16)
                for part in range(2):
                    load(0, e, part)

            def fallback(r):
                for e in range(E):
                    for part in range(2):
                        load(r, e, part)

            more_rounds(sp, fallback)

        @block.tensor
        def _(pe):
            mm = nc.tensor.matmul

            def three(out_, a, b, start, stop):
                mm(out_, a[0], b[0], start=start, stop=False)
                mm(out_, a[0], b[1], start=False, stop=False)
                return mm(out_, a[1], b[0], start=False, stop=stop)

            pe.wait_ge(small_in, 16)
            pe.wait_ge(memset_done, 1)
            pe.wait_ge(emb_sq, 1)
            for k in range(2):
                mm(bank[6][0:KP, k * E:(k + 1) * E], small_of("probe", DR)[:, k * KP:(k + 1) * KP],
                   small_of("embT", DR), start=True, stop=True)
            mm(bank[6][0:KP, 2 * E:3 * E], ones[0:DR, 0:KP], embsq[:, :], start=True, stop=True) \
                .then_inc(gain_ps, 1)

            for k in range(PK):
                pe.wait_ge(pw_lo, k + 1)
                for i in range(NT):
                    last = three(bank[i][0:TT, 0:C],
                                 [a[:, k, i * TT:(i + 1) * TT] for a in (pwh, pwl)],
                                 [a[:, k, TOK:] for a in (pwh, pwl)], k == 0, k == PK - 1)
                    if k == PK - 1:
                        last.then_inc(emb_ready, 1)

            def xT_tile(i):
                g, t = group(i)
                pe.wait_ge(xn_done, i + 1)
                at(pe, xT_lo, i - 1)
                if i == 0:
                    pe.wait_ge(rmat_done, 1)
                for k in range(2):
                    last = nc.tensor.transpose(bank[6 + i % 2][0:KP, k * TT:(k + 1) * TT],
                                               xnr[:, t, k * KP:(k + 1) * KP], ident[0:TT, 0:TT])
                last.then_inc(xT_ready, 1)

            def qk(g, chunks):
                pe.wait_ge(xT_lo, TG * (g + 1))
                pe.wait_ge(qk_lo0, 1)
                for m in chunks:
                    n = 2 * QC * g + m
                    if m >= 4:
                        pe.wait_ge(qk_lo, n - 3)
                    elif g and m < 2:
                        pe.wait_ge(v_taken, NT)
                    elif g:
                        pe.wait_ge(s_taken, GI)
                    else:
                        pe.wait_ge(emb_taken, QKBANK[m] + 1)
                    for k in range(2):
                        last = three(bank[QKBANK[n % 4]][:, 0:GT], [w[:, k, m % 2, m // 2, :] for w in wq],
                                     [xT[:, s, k, :] for s in range(2)], k == 0, k == 1)
                    last.then_inc(qk_ready, 1)

            def v(g):
                pe.wait_ge(vo_lo, 1)
                pe.wait_ge(xT_lo, TG * (g + 1))
                for t in range(TG):
                    i = TG * g + t
                    if i < 2:
                        pe.wait_ge(qk_lo, 2 * QC - 3 + i)
                    else:
                        pe.wait_ge(v_taken, i - 1)
                    for k in range(2):
                        last = three(bank[2 + i % 2][0:TT, 0:C],
                                     [xT[:, s, k, t * TT:(t + 1) * TT] for s in range(2)],
                                     [w[:, k, 0, :] for w in wv], k == 0, k == 1)
                    last.then_inc(v_ready, 1)

            def scores(b):
                g, bi = b // GI, b % GI
                at(pe, s_taken, b - 1)
                if b < 2:
                    pe.wait_ge(emb_taken, NT)
                if bi == 0:
                    pe.wait_ge(qk_lo, 2 * QC * (g + 1))
                for c in range(QC):
                    for t in range(2):
                        rows = slice(64 * t, 64 * t + 64)
                        o = psum[:, SBANK[b % 2] + t, c * KEYS:(c + 1) * KEYS]
                        last = three(o, [qb[rows, s, c, bi, :] for s in range(2)],
                                     [kT[rows, s, c, bi * KEYS:(bi + 1) * KEYS] for s in range(2)],
                                     True, True)
                last.then_inc(s_ready, 1)

            def dT_pair(u):
                pe.wait_ge(dif_done, 2 * u + 2)
                at(pe, dT_taken, u)
                if u == 0:
                    pe.wait_ge(xT_lo, NT)
                for m in range(4):
                    b = 2 * u + m // 2
                    last = nc.tensor.transpose(
                        bank[6][0:2 * KEYS, m * ROWS:(m + 1) * ROWS],
                        dif[:, b % 4, 2 * (m % 2):2 * (m % 2) + 2, :].rearrange("p j n -> p (j n)"),
                        identR)
                last.then_inc(dT_ready, 1)

            def pv_pair(u):
                g = u // (GI // 2)
                pe.wait_ge(dT_taken, u + 1)
                pe.wait_ge(v_in[g], 32)
                at(pe, oT_done, u)
                if u == 0:
                    pe.wait_ge(xT_lo, NT)
                for m in range(4):
                    bi = (2 * u + m // 2) % GI
                    for j in range(TRI):
                        last = mm(bank[7][2 * D * j:2 * D * (j + 1), m * KEYS:(m + 1) * KEYS],
                                  vbd[:, g, bi, m % 2, j, :],
                                  dT[:, u % 2, m, j * KEYS:(j + 1) * KEYS], start=True, stop=True)
                last.then_inc(pv_ready, 1)

            def wo(g, tiles):
                pe.wait_ge(oT_done, GI // 2 * (g + 1))
                pe.wait_ge(v_taken, NT)
                for t in tiles:
                    i = TG * g + t
                    at(pe, h2_done, i - 1)
                    at(pe, rt_taken, g)
                    at(pe, rank_taken, g)
                    for k in range(2):
                        last = three(bank[2 + i % 2][0:TT, 0:C],
                                     [oT[:, s, k, t * TT:(t + 1) * TT] for s in range(2)],
                                     [w[:, k, 1, :] for w in wv], k == 0, k == 1)
                    last.then_inc(wo_ready, 1)

            def router(g):
                pe.wait_ge(h2_done, TG * (g + 1))
                at(pe, rank_taken, g)
                for t in range(TG + 1):
                    if t < TG:
                        i = TG * g + t
                        pe.wait_ge(x2_done, i + 1)
                        at(pe, x2T_taken, i)
                        for k in range(2):
                            last = nc.tensor.transpose(bank[3][0:KP, k * TT:(k + 1) * TT],
                                                       xrow[:, i, k * KP:(k + 1) * KP],
                                                       ident[0:TT, 0:TT])
                        last.then_inc(x2T_ready, 1)
                    if t > 0:
                        i = TG * g + t - 1
                        pe.wait_ge(x2T_taken, i + 1)
                        for k in range(2):
                            last = mm(bank[2][0:TT, (t - 1) * (2 * E + DR):t * (2 * E + DR)],
                                      x2T[:, i % 2, k, :], rmat[:, k, :], start=(k == 0), stop=(k == 1))
                        last.then_inc(rt_ready, 1)

            def ranks(g):
                pe.wait_ge(consts16, 2)
                pe.wait_ge(hots_done, g + 1)
                if g:
                    pe.wait_ge(s_taken, IMAGES)
                else:
                    pe.wait_ge(x2T_taken, TG)
                rb = bank[RANKBANK[g]]
                o = rb[0:TT, g * TG * E:(g + 1) * TG * E]
                mm(o, before16[:, :], hots[:, TG * g:TG * (g + 1), :].rearrange("p t e -> p (t e)"),
                   start=True, stop=False, skip_group_check=True)
                for j in range(TG * (g + 1) - 1):
                    first = max(j + 1, TG * g)
                    last = mm(rb[0:TT, first * E:(g + 1) * TG * E], ones16[:, 0:TT],
                              bc(hots[:, j, :], 1, TG * (g + 1) - first), start=False,
                              stop=(j == TG * (g + 1) - 2), skip_group_check=True)
                last.then_inc(rank_ready, 1)

            def counts():
                pe.wait_ge(oT_done, IMAGES // 2)
                for i in range(NT):
                    last = mm(bank[7][:, 0:E], ones16[:, :], hots[:, i, :], start=(i == 0), stop=(i == NT - 1))
                last.then_inc(count_ready, 1)

            for i in range(TG):
                xT_tile(i)
            qk(0, range(2 * QC))
            v(0)
            for b in range(IMAGES):
                if b == GI - 1:
                    qk(1, range(0, 2))
                scores(b)
                if b < TG:
                    xT_tile(TG + b)
                if b == TG:
                    v(1)
                if b >= 5 and b % 2:
                    pv_pair((b - 5) // 2)
                if b >= 4 and b % 2 == 0:
                    dT_pair((b - 4) // 2)
                if b == GI - 1:
                    qk(1, range(2, 2 * QC))
                if b == GI + 4:
                    wo(0, range(0, 2))
                if b == GI + 5:
                    wo(0, range(2, TG))
            dT_pair(IMAGES // 2 - 2)
            router(0)
            pv_pair(IMAGES // 2 - 2)
            dT_pair(IMAGES // 2 - 1)
            ranks(0)
            pv_pair(IMAGES // 2 - 1)
            wo(1, range(TG))
            router(1)
            ranks(1)
            counts()

            def slot_rows(r, e):
                j = [a <= e < b for a, b in XS_PARTS].index(True)
                pe.wait_ge(xs_in[j], (r + 1) * 16)
                at(pe, xg_lo, E * r + e)
                if e == 0:
                    pe.wait_ge(s_taken, IMAGES)
                for k in range(2):
                    for s in range(ST):
                        last = nc.tensor.transpose(
                            bank[0][0:KP, k * CAP + s * 128:k * CAP + (s + 1) * 128],
                            xs[:, e * ST + s, k * KP:(k + 1) * KP], ident[:, :])
                last.then_inc(xg_ready, 1)

            def layer1(r, e, p):
                n = E * r + e
                if p == 0:
                    pe.wait_ge(xg_lo, n + 1)
                    pe.wait_ge(w_lo[0], n + 1)
                at(pe, relu_done, 3 * (n - 1) + p + 1)
                if isinstance(r, int) and n == 0:
                    pe.wait_ge(*((rank_taken, GROUPS), (rt_taken, GROUPS), (x2T_taken, NT))[p])
                for q in range(2):
                    for k in range(2):
                        last = three(bank[1 + p][:, q * CAP:(q + 1) * CAP],
                                     [w[e % 2][:, k, (2 * p + q) * 128:(2 * p + q + 1) * 128]
                                      for w in (w1h, w1l)],
                                     [xg[e % 2][:, s, k, :] for s in range(2)], k == 0, k == 1)
                last.then_inc(l1_ready, 1)

            def layer2(r, e, p):
                n = E * r + e
                pe.wait_ge(h_lo, 3 * n + p + 1)
                if p == 0:
                    pe.wait_ge(w_lo[1], n + 1)
                    at(pe, yT_done, n)
                    if isinstance(r, int) and n == 0:
                        pe.wait_ge(s_taken, IMAGES)
                for q in range(2):
                    for m in range(2):
                        c = 2 * p + q
                        last = three(bank[4 + m][0:KP, 0:CAP],
                                     [w[e % 2][:, c, m * KP:(m + 1) * KP] for w in (w2h, w2l)],
                                     [a[e % 2][:, c, :] for a in (hh, hl)], c == 0, c == HC - 1)
                if p == 2:
                    last.then_inc(y_ready, 1)

            def back(r, e):
                n = E * r + e
                pe.wait_ge(yT_done, n + 1)
                at(pe, yg_done, n)
                if isinstance(r, int) and n == 0:
                    pe.wait_ge(dT_taken, IMAGES // 2)
                for s in range(ST):
                    for m in range(2):
                        last = nc.tensor.transpose(
                            bank[6][:, s * C + m * KP:s * C + (m + 1) * KP],
                            yT[:, m, s * 128:(s + 1) * 128], ident[0:KP, 0:KP])
                last.then_inc(yb_ready, 1)

            slot_rows(0, 0)
            for s in range(E + 1):
                if s < E:
                    layer1(0, s, 0)
                if s >= 2:
                    back(0, s - 2)
                if s >= 1:
                    layer2(0, s - 1, 0)
                if s + 1 < E:
                    slot_rows(0, s + 1)
                for p in (1, 2):
                    if s < E:
                        layer1(0, s, p)
                    if s >= 1:
                        layer2(0, s - 1, p)
            back(0, E - 1)

            def fallback(r):
                for e in range(E):
                    slot_rows(r, e)
                    for p in range(3):
                        layer1(r, e, p)
                    for p in range(3):
                        layer2(r, e, p)
                    back(r, e)

            more_rounds(pe, fallback)

        @block.scalar
        def _(act):
            act.dma_start(sm[:, :], small).then_inc(small_in, 16)
            act.dma_start(h[:, :, :], pos).then_inc(pos_in, 16)
            for k in range(PK):
                act.wait_ge(patch_in[k], 16)
                nc.scalar.activation(pwh[:, k, :], pwraw[:, k, :], ACT.Copy).then_inc(pw_hi, 1)
            act.wait_ge(qk_in, 16)
            nc.scalar.activation(fr[0:KP, 0, 0:QKN], qkraw, ACT.Copy).then_inc(qk_hi0, 1)
            act.wait_ge(vo_in, 16)
            nc.scalar.activation(fr[0:KP, 0, QKN:QKN + VON], voraw, ACT.Copy).then_inc(vo_hi, 1)
            act.wait_ge(small_in, 16)
            nc.scalar.activation(lam[:, :], small_of("lam", ROWS), ACT.Exp).then_inc(lam_done, 1)

            def xT_high(i):
                g, t = group(i)
                act.wait_ge(xT_ready, i + 1)
                if i == TG:
                    act.wait_ge(v_ready, TG)
                nc.scalar.activation(xT[:, 0, :, t * TT:(t + 1) * TT],
                                     bank[6 + i % 2][0:KP, 0:2 * TT].rearrange("p (k n) -> p k n", k=2),
                                     ACT.Copy).then_inc(xT_hi, 1)

            def qk_high(g):
                if g:
                    act.wait_ge(s_ready, GI * g)
                else:
                    act.wait_ge(q_zeroed, 1)
                for m in range(2 * QC):
                    n, c = 2 * QC * g + m, m // 2
                    act.wait_ge(qk_ready, n + 1)
                    src = bank[QKBANK[n % 4]][:, 0:GT]
                    if m % 2:
                        nc.scalar.activation(kT[:, 0, c, :], src, ACT.Copy).then_inc(qk_hi, 1)
                    else:
                        src = src.rearrange("p (b n) -> p b n", b=GI)
                        for j in range(TRI):
                            last = nc.scalar.activation(
                                qb[:, 0, c, :, j * KEYS:(j + 1) * KEYS], src, ACT.Copy,
                                scale=qmask[:, j:j + 1])
                        last.then_inc(qk_hi, 1)

            def v_rows(g):
                for t in range(TG):
                    i = TG * g + t
                    act.wait_ge(v_ready, i + 1)
                    if g:
                        act.wait_ge(v_out[0], 32)
                    if i == 0:
                        act.wait_ge(v_zeroed, 1)
                    for s in range(2):
                        last = nc.scalar.activation(
                            vrow[:, t, s, :].rearrange("p (m t n) -> p m t n", t=2, n=D)[:, :, s, :],
                            bank[2 + i % 2][0:TT, s * KP:(s + 1) * KP].rearrange("p (m n) -> p m n", n=D),
                            ACT.Copy)
                    last.then_inc(v_taken, 1)
                act.wait_ge(v_taken, TG * (g + 1))
                for s in range(2):
                    act.dma_start(v_dram[s, g * GT:(g + 1) * GT, :].rearrange("(t p) c -> p t c", p=TT),
                                  vrow[:, :, s, :]).then_inc(v_out[g], 16)

            def v_blocks(g):
                act.wait_ge(v_out[g], 32)
                for s in range(2):
                    act.dma_start(vbd[s * KEYS:(s + 1) * KEYS, g].rearrange("p b a j n -> p b (a j n)"),
                                  v_dram[s, g * GT:(g + 1) * GT, :].rearrange("(b p) n -> p b n", p=KEYS)) \
                       .then_inc(v_in[g], 16)

            def exps(b):
                act.wait_ge(s_taken, b + 1)
                nc.scalar.activation(ex[:, b % 3], ex[:, b % 3], ACT.Exp).then_inc(exp_done, 1)

            def dT_copy(u):
                act.wait_ge(dT_ready, u + 1)
                at(act, pv_ready, u - 1)
                nc.scalar.activation(dT[:, u % 2],
                                     bank[6][0:2 * KEYS, 0:4 * ROWS].rearrange("p (m n) -> p m n", m=4),
                                     ACT.Copy).then_inc(dT_taken, 1)

            def output_high(u):
                act.wait_ge(pv_ready, u + 1)
                if u == GI // 2:
                    act.wait_ge(wo_ready, TG)
                src, halves = outputs(u)
                nc.scalar.activation(halves[0], src, ACT.Copy).then_inc(oT_hi, 1)

            def x2T_copy(i):
                act.wait_ge(x2T_ready, i + 1)
                at(act, rt_ready, i - 1)
                nc.scalar.activation(x2T[:, i % 2],
                                     bank[3][0:KP, 0:2 * TT].rearrange("p (k n) -> p k n", k=2),
                                     ACT.Copy).then_inc(x2T_taken, 1)

            def gap_exp(g):
                act.wait_ge(gap_done, g + 1)
                nc.scalar.activation(gt[:, 1, :], gt[:, 0, :], ACT.Exp).then_inc(gexp_done, 1)

            def w_high(r, e, part):
                n = E * r + e
                act.wait_ge(w_sum[part], n + 1)
                if isinstance(r, int) and n < 2:
                    act.wait_ge(emb_ready, NT)
                if part == 0:
                    at(act, l1_ready, 3 * (n - 1))
                    src = staged(e, 0)[:, 0, :]
                    dst = w1h[e % 2].rearrange("p k n -> p (k n)")
                else:
                    at(act, y_ready, n - 1)
                    src = staged(e, 1)[:, 0, :]
                    dst = w2h[e % 2].rearrange("p k n -> p (k n)")
                nc.scalar.activation(dst, src, ACT.Copy).then_inc(w_hi[part], 1)

            for i in range(TG):
                xT_high(i)
            qk_high(0)
            v_rows(0)
            for b in range(IMAGES):
                if b < TG:
                    xT_high(TG + b)
                exps(b)
                if b == 1:
                    v_blocks(0)
                if b == TG:
                    v_rows(1)
                if b == TG + 2:
                    v_blocks(1)
                if b >= 4 and b % 2 == 0:
                    dT_copy((b - 4) // 2)
                if b >= 5 and b % 2:
                    output_high((b - 5) // 2)
                if b == GI - 1:
                    qk_high(1)
            dT_copy(IMAGES // 2 - 2)
            for i in range(TG):
                x2T_copy(i)
            output_high(IMAGES // 2 - 2)
            w_high(0, 0, 0)
            dT_copy(IMAGES // 2 - 1)
            gap_exp(0)
            output_high(IMAGES // 2 - 1)
            w_high(0, 0, 1)
            w_high(0, 1, 0)
            for i in range(TG, NT):
                x2T_copy(i)
            w_high(0, 1, 1)
            gap_exp(1)

            def sum_init(g):
                act.wait_ge(h2_done, TG * (g + 1))
                act.dma_start(out[g * GT:(g + 1) * GT, :].rearrange("(t p) c -> p t c", p=TT),
                              h[:, TG * g:TG * (g + 1), :]).then_inc(acc_init, 16)

            def load_slots(r):
                act.wait_ge(scattered, (r + 1) * (2 * NT * 16))
                if isinstance(r, int):
                    act.wait_ge(s_ready, IMAGES)
                for j, (a, b) in enumerate(XS_PARTS):
                    part = slice(a * ST, b * ST)
                    act.dma_start(xs[:, part, :], xs_dram.rearrange("(n p) c -> p n c", p=128)[:, part, :]) \
                       .then_inc(xs_in[j], 16)

            def slot_high(r, e):
                n = E * r + e
                act.wait_ge(xg_ready, n + 1)
                at(act, l1_ready, 3 * (n - 1))
                nc.scalar.activation(xg[e % 2][:, 0], bank[0][0:KP, :].rearrange("p (k n) -> p k n", k=2),
                                     ACT.Copy).then_inc(xg_hi, 1)

            def hidden(r, e, p):
                n = E * r + e
                j = 3 * n + p
                slot = (3 * e + p) % 2
                act.wait_ge(l1_ready, j + 1)
                at(act, sq_done, j - 1)
                if isinstance(r, int) and j == 0:
                    act.wait_ge(wsmall_in, 16)
                for q in range(2):
                    last = nc.scalar.activation(
                        relu[slot][:, q * CAP:(q + 1) * CAP], bank[1 + p][:, q * CAP:(q + 1) * CAP],
                        ACT.Relu, bias=wsm[:, e, 2 * p + q:2 * p + q + 1])
                last.then_inc(relu_done, 1)
                act.wait_ge(relu_done, j + 1)
                at(act, h_lo, j - 1)
                nc.scalar.activation(hsq[slot], relu[slot], ACT.Square).then_inc(sq_done, 1)

            def y_bias(r, e):
                n = E * r + e
                act.wait_ge(y_ready, n + 1)
                at(act, yb_ready, n)
                for m in range(2):
                    last = nc.scalar.activation(yT[:, m, :], bank[4 + m][0:KP, 0:CAP], ACT.Identity,
                                                bias=wsm[0:KP, e, HC + m:HC + m + 1])
                last.then_inc(yT_done, 1)

            for g in range(GROUPS):
                sum_init(g)
            load_slots(0)
            slot_high(0, 0)
            for s in range(E + 1):
                if s >= 2:
                    y_bias(0, s - 2)
                if 2 <= s + 1 < E:
                    w_high(0, s + 1, 0)
                if s < E:
                    hidden(0, s, 0)
                if s + 1 < E:
                    slot_high(0, s + 1)
                if s < E:
                    hidden(0, s, 1)
                    if s >= 2:
                        w_high(0, s, 1)
                    hidden(0, s, 2)
            y_bias(0, E - 1)

            def fallback(r):
                act.wait_ge(yg_done, E * r)
                load_slots(r)
                for e in range(E):
                    w_high(r, e, 0)
                    w_high(r, e, 1)
                    slot_high(r, e)
                    for p in range(3):
                        hidden(r, e, p)
                    y_bias(r, e)

            more_rounds(act, fallback)

        @block.vector
        def _(dve):
            vec = nc.vector
            links = [0]

            def link(ins, r=0):
                links[0] += 1
                ins.then_inc(dve_self, 1)
                dve.wait_ge(dve_self, links[0] + (0 if isinstance(r, int) else (r - 1) * FALLBACK_LINKS))

            dve.wait_ge(small_in, 16)
            vec.tensor_copy(before16[:, :], small_of("before", TT)).then_inc(consts16, 1)
            dve.wait_ge(memset_done, 1)
            vec.tensor_copy(ones16[:, :], ones[0:TT, :]).then_inc(consts16, 1)
            vec.tensor_tensor(embsq[:, :], small_of("embT", DR), small_of("embT", DR), ALU.mult) \
                .then_inc(emb_sq, 1)
            vec.tensor_tensor(lconst[:, :], small_of("energy", TT), small_of("fatigue", TT), ALU.subtract) \
                .then_inc(dve_self, 1)
            links[0] += 1
            for i in range(NT):
                vec.tensor_copy(xrow[:, i, C:C + 1], small_of("token", TT)[:, i:i + 1])
            dve.wait_ge(gain_ps, 1)
            link(vec.tensor_copy(gain[:, 0, :], bank[6][0:KP, 2 * E:3 * E]))
            vec.tensor_scalar(gain[:, 1, :], gain[:, 0, :], 1e-24, None, ALU.max).then_inc(gain_n2, 1)
            link(vec.tensor_scalar(lconst[:, :], lconst[:, :], 0.1, None, ALU.mult))

            def low(dst, src, hi):
                return vec.tensor_tensor(dst, src, hi.bitcast(F32), ALU.subtract)

            for k in range(PK):
                dve.wait_ge(pw_hi, k + 1)
                low(pwl[:, k, :], pwraw[:, k, :], pwh[:, k, :]).then_inc(pw_lo, 1)
            dve.wait_ge(gain_pow, 2)
            link(vec.tensor_scalar(gain[:, 2, :], gain[:, 2, :], 1.0, 0.02 / C, ALU.add, ALU.mult))
            for k in range(2):
                vec.tensor_tensor(rmat[:, k, 0:E], small_of("rw", KP)[:, k * E:(k + 1) * E],
                                  gain[:, 2, :], ALU.add)
                vec.scalar_tensor_tensor(rmat[:, k, E:2 * E], bank[6][0:KP, k * E:(k + 1) * E], 0.02,
                                         gain[:, 3, :], ALU.mult, ALU.mult)
                last = vec.tensor_copy(rmat[:, k, 2 * E:], small_of("probeT", KP)[:, k * DR:(k + 1) * DR])
            last.then_inc(rmat_done, 1)
            dve.wait_ge(qk_hi0, 1)
            low(fr[0:KP, 1, 0:QKN], qkraw, fr[0:KP, 0, 0:QKN]).then_inc(qk_lo0, 1)
            dve.wait_ge(vo_hi, 1)
            low(fr[0:KP, 1, QKN:QKN + VON], voraw, fr[0:KP, 0, QKN:QKN + VON]).then_inc(vo_lo, 1)

            def row_stats(ln, i, bnk, done):
                vec.tensor_tensor(h[:, i, :], bnk[0:TT, 0:C], h[:, i, :], ALU.add).then_inc(done, 1)

            def stats1(ln, i):
                vec.bn_stats(stats[:, ln, i, :], h[:, i, :]).then_inc(dve_self, 1)
                links[0] += 1

            def stats2(ln, i):
                vec.bn_aggr(mv[:, ln, i, :], stats[:, ln, i, :]).then_inc(mv_done, 1)

            def normalise(dst, ln, i):
                return vec.tensor_scalar(dst, h[:, i, :], mv[:, ln, i, 0:1], rstd[:, ln, i:i + 1],
                                         ALU.subtract, ALU.mult)

            def embedded(g):
                for i in range(TG * g, TG * g + TG):
                    dve.wait_ge(emb_ready, i + 1)
                    row_stats(0, i, bank[i], emb_taken)
                if g == 0:
                    embedded_stats(0)

            def embedded_stats(g):
                dve.wait_ge(emb_taken, TG * (g + 1))
                for i in range(TG * g, TG * g + TG):
                    stats1(0, i)
                dve.wait_ge(dve_self, links[0])
                for i in range(TG * g, TG * g + TG):
                    stats2(0, i)

            def ln1(g):
                dve.wait_ge(rstd_done, g + 1)
                if g:
                    dve.wait_ge(xT_ready, TG)
                for t in range(TG):
                    normalise(xnr[:, t, :], 0, TG * g + t).then_inc(xn_done, 1)

            def xT_low(i):
                g, t = group(i)
                dve.wait_ge(xT_hi, i + 1)
                vec.tensor_tensor(xT[:, 1, :, t * TT:(t + 1) * TT],
                                  bank[6 + i % 2][0:KP, 0:2 * TT].rearrange("p (k n) -> p k n", k=2),
                                  xT[:, 0, :, t * TT:(t + 1) * TT].bitcast(F32), ALU.subtract) \
                    .then_inc(xT_lo, 1)

            def qk_low(g):
                for m in range(2 * QC):
                    n, c = 2 * QC * g + m, m // 2
                    dve.wait_ge(qk_hi, n + 1)
                    src = bank[QKBANK[n % 4]][:, 0:GT]
                    if m % 2:
                        vec.tensor_tensor(kT[:, 1, c, :], src, kT[:, 0, c, :], ALU.subtract) \
                            .then_inc(qk_lo, 1)
                    else:
                        src = src.rearrange("p (b n) -> p b n", b=GI)
                        for j in range(TRI):
                            cols = slice(j * KEYS, (j + 1) * KEYS)
                            last = vec.scalar_tensor_tensor(
                                qb[:, 1, c, :, cols], src, qmask[:, j:j + 1], qb[:, 0, c, :, cols],
                                ALU.mult, ALU.subtract)
                        last.then_inc(qk_lo, 1)

            def softmax_top(b):
                s = psum[0:ROWS, SBANK[b % 2]:SBANK[b % 2] + 2, 0:QC * KEYS] \
                    .rearrange("p t (c n) -> p c t n", c=QC)
                dve.wait_ge(s_ready, b + 1)
                vec.reduce_max(mx[:, b % 2, :].rearrange("p (c t) -> p c t", t=2), s, AX).then_inc(mx_done, 1)
                if b >= 1 and b != GI:
                    softmax_sum(b - 1)
                dve.wait_ge(mx_done, b + 1)
                at(dve, dif_done, b - 2)
                vec.tensor_tensor(ex[:, b % 3].rearrange("p (c t) n -> p c t n", t=2), s,
                                  bc(mx[:, b % 2, :].rearrange("p (c t) -> p c t", t=2), 3, KEYS),
                                  ALU.subtract) \
                    .then_inc(s_taken, 1)
                if b >= 1 and b != GI:
                    softmax_scale(b - 1)

            def softmax_sum(b):
                dve.wait_ge(exp_done, b + 1)
                vec.reduce_sum(den[:, b % 2, :], ex[:, b % 3], AX).then_inc(den_done, 1)

            def softmax_scale(b):
                dve.wait_ge(den_done, b + 1)
                at(dve, dif_done, b - 2)
                vec.reciprocal(rec[:, b % 3, :], den[:, b % 2, :]).then_inc(rec_done, 1)

            def output_low(u):
                dve.wait_ge(oT_hi, u + 1)
                src, halves = outputs(u)
                vec.tensor_tensor(halves[1], src, halves[0].bitcast(F32), ALU.subtract).then_inc(oT_done, 1)

            def residual(g):
                if g == 0:
                    dve.wait_ge(h_biased, 1)
                for i in range(TG * g, TG * g + TG):
                    dve.wait_ge(wo_ready, i + 1)
                    row_stats(1, i, bank[2 + i % 2], h2_done)
                dve.wait_ge(h2_done, TG * (g + 1))
                for i in range(TG * g, TG * g + TG):
                    stats1(1, i)
                dve.wait_ge(dve_self, links[0])
                for i in range(TG * g, TG * g + TG):
                    stats2(1, i)

            def ln2(g):
                dve.wait_ge(rstd_done, GROUPS + g + 1)
                for i in range(TG * g, TG * g + TG):
                    normalise(xrow[:, i, 0:C], 1, i).then_inc(x2_done, 1)

            def route_probe(g):
                dve.wait_ge(rt_ready, TG * (g + 1))
                vec.tensor_copy(rsc[:, :, :], bank[2][0:TT, 0:TG * (2 * E + DR)]
                                .rearrange("p (t n) -> p t n", t=TG)).then_inc(rt_taken, 1)
                dve.wait_ge(rt_taken, g + 1)
                link(vec.tensor_tensor(usq[:, :, :], rsc[:, :, 2 * E:], rsc[:, :, 2 * E:], ALU.mult))
                link(vec.reduce_sum(un[:, 0, :], usq[:, :, :], AX))
                vec.tensor_scalar(un[:, 1, :], un[:, 0, :], 1e-24, None, ALU.max).then_inc(un_clamped, 1)

            def route_choose(g):
                dve.wait_ge(un_pow, g + 1)
                link(vec.tensor_tensor(logit[:, :, :], rsc[:, :, E:2 * E], bc(un[:, 0, :], 2, E), ALU.mult))
                link(vec.tensor_tensor(logit[:, :, :], logit[:, :, :], rsc[:, :, 0:E], ALU.add))
                link(vec.tensor_tensor(logit[:, :, :], logit[:, :, :], bc(lconst[:, :], 1, TG), ALU.add))
                for t in range(TG):
                    vec.max(top[:, t, :], logit[:, t, :]).then_inc(dve_self, 1)
                links[0] += TG
                dve.wait_ge(dve_self, links[0])
                vec.tensor_tensor(gt[:, 0, :], top[:, :, 1], top[:, :, 0], ALU.subtract).then_inc(gap_done, 1)
                for t in range(TG):
                    vec.max_index(topi[:, t, :], top[:, t, :], logit[:, t, :]).then_inc(dve_self, 1)
                links[0] += TG
                dve.wait_ge(dve_self, links[0])
                tiles = slice(TG * g, TG * (g + 1))
                link(vec.tensor_copy(topf[:, tiles, :], topi[:, :, 0:2]))
                link(vec.tensor_tensor(
                    hot[:, :, :], bc(small_of("iota", TT), 1, 2 * TG),
                    bc(topf[:, tiles, :].rearrange("p t k -> p (t k)"), 2, E), ALU.is_equal))
                two = hot[:, :, :].rearrange("p (t k) e -> p t k e", k=2)
                vec.tensor_tensor(hots[:, tiles, :], two[:, :, 0, :], two[:, :, 1, :], ALU.add) \
                    .then_inc(hots_done, 1)
                link(vec.tensor_scalar(base[:, tiles, :], topf[:, tiles, :], float(CAP), None, ALU.mult))
                dve.wait_ge(gexp_done, g + 1)
                link(vec.tensor_scalar(gt[:, 2, :], gt[:, 1, :], 1.0, None, ALU.add))
                link(vec.reciprocal(gt[:, 3, :], gt[:, 2, :]))
                link(vec.tensor_tensor(xrow[:, tiles, C + 1], gt[:, 1, :], gt[:, 3, :], ALU.mult))
                vec.tensor_copy(xrow[:, tiles, C + 3], topf[:, tiles, 0])
                vec.tensor_tensor(xrow[:, tiles, C + 2], gt[:, 3, :], xrow[:, tiles, C + 1], ALU.subtract) \
                    .then_inc(row_done, 1)

            def route_rank(g):
                tiles = slice(TG * g, TG * (g + 1))
                dve.wait_ge(rank_ready, g + 1)
                src = bank[RANKBANK[g]][0:TT, g * TG * E:(g + 1) * TG * E].rearrange("p (t e) -> p t e", t=TG)
                vec.tensor_tensor(rk[:, :, :, :], hot[:, :, :].rearrange("p (t k) e -> p t k e", k=2),
                                  bc(src, 2, 2), ALU.mult).then_inc(rank_taken, 1)
                dve.wait_ge(rank_taken, g + 1)
                link(vec.reduce_sum(rank[:, tiles, :], rk[:, :, :, :], AX))
                place_rows(tiles, 0)

            def place_rows(tiles, r):
                a, b = rank[:, tiles, :], base[:, tiles, :]
                link(vec.tensor_scalar(live[:, 0, tiles, :], a, 0.0, None, ALU.is_ge), r)
                link(vec.scalar_tensor_tensor(live[:, 1, tiles, :], a, float(CAP), live[:, 0, tiles, :],
                                              ALU.is_lt, ALU.mult), r)
                link(vec.scalar_tensor_tensor(place[:, tiles, :], a, -BEYOND, b, ALU.add, ALU.add), r)
                link(vec.tensor_tensor(place[:, tiles, :], place[:, tiles, :], live[:, 1, tiles, :],
                                       ALU.mult), r)
                vec.tensor_scalar(idx[:, tiles, :], place[:, tiles, :], BEYOND, None, ALU.add) \
                    .then_inc(idx_done, 1)

            def count_rounds():
                dve.wait_ge(count_ready, 1)
                vec.tensor_copy(cnt[:, :], bank[7][:, 0:E]).then_inc(count_taken, 1)
                dve.wait_ge(count_taken, 1)
                link(vec.reduce_max(rounds_f[:, 0:1], cnt[:, :], AX))
                link(vec.tensor_scalar(rounds_f[:, 1:2], rounds_f[:, 0:1], float(CAP), 1.0,
                                       ALU.is_gt, ALU.add))
                for k in range(2, ROUNDS):
                    link(vec.tensor_scalar(rounds_f[:, 2:3], rounds_f[:, 0:1], float(k * CAP), None,
                                           ALU.is_gt))
                    link(vec.tensor_tensor(rounds_f[:, 1:2], rounds_f[:, 1:2], rounds_f[:, 2:3], ALU.add))
                vec.tensor_copy(rounds_i[:, :], rounds_f[:, 1:2]).then_inc(rounds_done, 1)

            def slots(r):
                n = small_of("slot")
                for j in range(len(XS_PARTS)):
                    dve.wait_ge(xs_in[j], (r + 1) * 16)
                link(vec.tensor_tensor(slive[:, :].rearrange("p (e s) -> p e s", e=E),
                                       n.rearrange("p (e s) -> p e s", e=E), bc(cnt[:, :], 2, ST),
                                       ALU.is_lt), r)
                link(vec.scalar_tensor_tensor(stok[:, :], xs[:, :, C], -float(TOK), n,
                                              ALU.add, ALU.subtract), r)
                link(vec.tensor_tensor(stok[:, :], stok[:, :], slive[:, :], ALU.mult), r)
                link(vec.scalar_tensor_tensor(sidx[:, :], stok[:, :], float(TOK), n, ALU.add, ALU.add), r)
                link(vec.tensor_tensor(sgate[:, :], xs[:, :, C + 3], small_of("expert"), ALU.is_equal), r)
                link(vec.tensor_tensor(sgate[:, :], sgate[:, :], xs[:, :, C + 2], ALU.mult), r)
                vec.tensor_tensor(sgate[:, :], sgate[:, :], xs[:, :, C + 1], ALU.add).then_inc(sidx_done, 1)

            def w_total(r, e, part):
                dve.wait_ge(slow_in[part][e % STAGES], staged_count(r, e))
                dve.wait_ge(w_added[part][e % STAGES], staged_count(r, e))
                if isinstance(r, int) and e == 0:
                    dve.wait_ge(wsmall_in, 16)
                w = staged(e, part)
                vec.scalar_tensor_tensor(w[:, 0, :], w[:, 0, :], gain_w(e, part), w[:, 1, :],
                                         ALU.mult, ALU.add).then_inc(w_sum[part], 1)

            def w_low(r, e, part):
                dve.wait_ge(w_hi[part], E * r + e + 1)
                hi, lo = ((w1h, w1l), (w2h, w2l))[part]
                flat = "p k n -> p (k n)"
                low(lo[e % 2].rearrange(flat), staged(e, part)[:, 0, :], hi[e % 2].rearrange(flat)) \
                    .then_inc(w_lo[part], 1)

            def slot_low(r, e):
                dve.wait_ge(xg_hi, E * r + e + 1)
                low(xg[e % 2][:, 1], bank[0][0:KP, :].rearrange("p (k n) -> p k n", k=2),
                    xg[e % 2][:, 0]).then_inc(xg_lo, 1)

            def hidden_halves(r, e, p):
                n = E * r + e
                j = 3 * n + p
                src = hsq[(3 * e + p) % 2].rearrange("p (q n) -> p q n", q=2)
                cs = slice(2 * p, 2 * p + 2)
                dve.wait_ge(sq_done, j + 1)
                at(dve, y_ready, n - 1)
                vec.tensor_copy(hh[e % 2][:, cs, :], src).then_inc(h_hi, 1)
                dve.wait_ge(h_hi, j + 1)
                low(hl[e % 2][:, cs, :], src, hh[e % 2][:, cs, :]).then_inc(h_lo, 1)

            def gated(r, e):
                n = E * r + e
                dve.wait_ge(yb_ready, n + 1)
                dve.wait_ge(sidx_done, r + 1)
                at(dve, added, (n - 1) * ST * 16)
                for s in range(ST):
                    last = vec.tensor_scalar(yg[e % 2][:, s, :], bank[6][:, s * C:(s + 1) * C],
                                             sgate[:, e * ST + s:e * ST + s + 1], None, ALU.mult)
                last.then_inc(yg_done, 1)

            dve.wait_ge(pos_biased, 1)
            embedded(0)
            embedded(1)
            ln1(0)
            embedded_stats(1)
            for i in range(TG):
                xT_low(i)
            ln1(1)
            qk_low(0)
            w_total(0, 0, 0)
            w_total(0, 0, 1)
            for b in range(IMAGES):
                softmax_top(b)
                if b < TG:
                    xT_low(TG + b)
                if b >= 6 and b % 2 == 0:
                    output_low((b - 6) // 2)
                if b == GI - 1:
                    softmax_sum(b)
                    softmax_scale(b)
                    qk_low(1)
                if b == GI + 5:
                    residual(0)
                if b == GI + 6:
                    ln2(0)
            softmax_sum(IMAGES - 1)
            softmax_scale(IMAGES - 1)
            output_low(IMAGES // 2 - 3)
            route_probe(0)
            route_choose(0)
            output_low(IMAGES // 2 - 2)
            route_rank(0)
            output_low(IMAGES // 2 - 1)
            w_low(0, 0, 0)
            residual(1)
            w_total(0, 1, 0)
            ln2(1)
            w_low(0, 0, 1)
            w_total(0, 1, 1)
            route_probe(1)
            route_choose(1)
            route_rank(1)
            count_rounds()
            w_low(0, 1, 0)
            w_low(0, 1, 1)
            for e in range(2, STAGES + 1):
                for part in range(2):
                    w_total(0, e, part)
            slot_low(0, 0)
            for s in range(E + 1):
                if s < E:
                    hidden_halves(0, s, 0)
                if s == 0:
                    slots(0)
                if s >= 2:
                    gated(0, s - 2)
                if s + 1 < E:
                    slot_low(0, s + 1)
                if STAGES < s + 2 < E:
                    w_total(0, s + 2, 0)
                if s < E:
                    hidden_halves(0, s, 1)
                if STAGES < s + 1 < E:
                    w_total(0, s + 1, 1)
                if 2 <= s < E:
                    w_low(0, s, 1)
                if s < E:
                    hidden_halves(0, s, 2)
            gated(0, E - 1)
            before = links[0]

            def fallback(r):
                dve.wait_ge(scattered, r * (2 * NT * 16))
                link(vec.tensor_scalar(rank[:, :, :], rank[:, :, :], -float(CAP), None, ALU.add), r)
                place_rows(slice(0, NT), r)
                dve.wait_ge(added, r * (E * ST * 16))
                link(vec.tensor_scalar(cnt[:, :], cnt[:, :], -float(CAP), None, ALU.add), r)
                slots(r)
                for e in range(E):
                    w_total(r, e, 0)
                    w_total(r, e, 1)
                    w_low(r, e, 1)
                    slot_low(r, e)
                    for p in range(3):
                        hidden_halves(r, e, p)
                    gated(r, e)
                assert links[0] - before == FALLBACK_LINKS

            more_rounds(dve, fallback)

        @block.gpsimd
        def _(pool):
            gp = nc.gpsimd
            links = [0]

            def link(ins):
                links[0] += 1
                ins.then_inc(pool_self, 1)
                pool.wait_ge(pool_self, links[0])

            gp.memset(ones[:, :], 1.0).then_inc(memset_done, 1)
            gp.memset(nhalf[:, :], -0.5)
            link(gp.memset(phalf[:, :], 0.5))
            link(gp.memset(zero[:, :], 0.0))
            pool.wait_ge(gain_n2, 1)
            gp.tensor_tensor(gain[:, 2, :], gain[:, 0, :], phalf[0:KP, :], ALU.pow).then_inc(gain_pow, 1)
            gp.tensor_tensor(gain[:, 3, :], gain[:, 1, :], nhalf[0:KP, :], ALU.pow).then_inc(gain_pow, 1)
            pool.wait_ge(pos_in, 16)
            gp.tensor_tensor(h[:, :, :], h[:, :, :], bc(small_of("bp", TT), 1, NT), ALU.add) \
                .then_inc(pos_biased, 1)
            gp.memset(qb[:, :, :, :, ROWS:].rearrange("p a c b n -> p (a c b) n"), 0.0).then_inc(q_zeroed, 1)
            gp.memset(vrow[:, :, :, :], 0.0).then_inc(v_zeroed, 1)

            def hold(k):
                gp.tensor_tensor(held[:, k:k + 1], zero[0:1, 0:1], zero[0:1, 1:2], ALU.add)

            def inverse_std(ln, g):
                tiles = slice(TG * g, TG * (g + 1))
                pool.wait_ge(mv_done, (ln * GROUPS + g + 1) * TG)
                link(gp.tensor_scalar(rstd[:, ln, tiles], mv[:, ln, tiles, 1], EPS, 1.0, ALU.add, ALU.mult))
                gp.tensor_tensor(rstd[:, ln, tiles], rstd[:, ln, tiles], nhalf[0:TT, 0:TG], ALU.pow) \
                    .then_inc(rstd_done, 1)

            def difference(b):
                pool.wait_ge(rec_done, b + 1)
                if b == 0:
                    pool.wait_ge(lam_done, 1)
                link(gp.tensor_tensor(rec[:, b % 3, NTRI:], rec[:, b % 3, NTRI:], lam[:, :], ALU.mult))
                link(gp.tensor_tensor(ex[:, b % 3], ex[:, b % 3], bc(rec[:, b % 3, :], 2, KEYS), ALU.mult))
                at(pool, dT_ready, (b - 4) // 2 + 1 if b >= 4 else 0)
                gp.tensor_tensor(dif[:, b % 4], ex[:, b % 3, 0:NTRI], ex[:, b % 3, NTRI:], ALU.subtract) \
                    .then_inc(dif_done, 1)

            def w_add(r, e, part):
                pool.wait_ge(fast_in[part][e % STAGES], staged_count(r, e))
                if not isinstance(r, int):
                    hold((part + 1) * E + e)
                pool.dma_start(staged(e, part)[:, 1, :], (w1, w2)[part][e, :, 2], accum_op=ALU.add) \
                    .then_inc(w_added[part][e % STAGES], 16)

            def w_low(r, e, part):
                pool.wait_ge(w_hi[part], E * r + e + 1)
                hi, lo = ((w1h, w1l), (w2h, w2l))[part]
                flat = "p k n -> p (k n)"
                gp.tensor_tensor(lo[e % 2].rearrange(flat), staged(e, part)[:, 0, :],
                                 hi[e % 2].rearrange(flat).bitcast(F32), ALU.subtract).then_inc(w_lo[part], 1)

            def probe_norm(g):
                pool.wait_ge(un_clamped, g + 1)
                gp.tensor_tensor(un[:, 0, :], un[:, 1, :], nhalf[0:TT, 0:TG], ALU.pow).then_inc(un_pow, 1)

            def scatter(i, k):
                pool.indirect_dma_start(
                    xs_dram, bass.IndirectOffsetOnAxis(ap=idx[:, i, k:k + 1], axis=0), xrow[:, i, :], None,
                    bounds_check=E * CAP - 1, oob_is_err=False).then_inc(scattered, 16)

            def add_rows(r, e):
                n = E * r + e
                pool.wait_ge(yg_done, n + 1)
                at(pool, added, n * ST * 16)
                pool.wait_ge(acc_init, GROUPS * 16)
                if not isinstance(r, int):
                    hold(e)
                for s in range(ST):
                    j = e * ST + s
                    pool.indirect_dma_start(
                        out, bass.IndirectOffsetOnAxis(ap=sidx[:, j:j + 1], axis=0),
                        yg[e % 2][:, s, :], None, bounds_check=TOK - 1, oob_is_err=False,
                        compute_op=ALU.add).then_inc(added, 16)

            def scatter_rows(g):
                pool.wait_ge(idx_done, g + 1)
                pool.wait_ge(row_done, g + 1)
                for i in range(TG * g, TG * (g + 1)):
                    for k in range(2):
                        scatter(i, k)

            inverse_std(0, 0)
            w_add(0, 0, 0)
            inverse_std(0, 1)
            w_add(0, 0, 1)
            pool.dma_start(xs_dram.rearrange("(n p) c -> p n c", p=128), bc(zero[:, :], 1, E * ST)) \
                .then_inc(zero_out, 16)
            pool.wait_ge(xn_done, NT)
            gp.tensor_tensor(h[:, :, :], h[:, :, :], bc(small_of("bo", TT), 1, NT), ALU.add) \
                .then_inc(h_biased, 1)
            for b in range(IMAGES):
                difference(b)
                if b in (GI + 2, GI + 3):
                    for part in range(2):
                        w_add(0, b - GI - 1, part)
                if b == GI + 4:
                    inverse_std(1, 0)
            probe_norm(0)
            pool.wait_ge(zero_out, 16)
            scatter_rows(0)
            inverse_std(1, 1)
            probe_norm(1)
            for part in range(2):
                w_add(0, STAGES, part)
            scatter_rows(1)
            for s in range(E + 2):
                if STAGES < s + 1 < E:
                    w_add(0, s + 1, 1)
                if STAGES < s + 2 < E:
                    w_add(0, s + 2, 0)
                if 2 <= s + 1 < E:
                    w_low(0, s + 1, 0)
                if s >= 2:
                    add_rows(0, s - 2)

            def fallback(r):
                pool.wait_ge(idx_done, GROUPS + r)
                for j in range(len(XS_PARTS)):
                    pool.wait_ge(xs_in[j], r * 16)
                hold(3 * E)
                for i in range(NT):
                    for k in range(2):
                        scatter(i, k)
                for e in range(E):
                    w_add(r, e, 0)
                    w_add(r, e, 1)
                    w_low(r, e, 0)
                    add_rows(r, e)

            n = more_rounds(pool, fallback)
            pool.wait_ge(added, n * (E * ST * 16))
            hold(3 * E + 1)


_INPUTS = ("patches", "pos", "wqk", "wvo", "small", "w1", "w2", "wsmall")


def kernel(**inputs):
    import concourse.bacc as bacc
    from concourse.bass_utils import run_bass_kernel_spmd as run

    a = {k: np.asarray(v) for k, v in inputs.items()}
    f = "L0_ffn_"
    x = a["x"].reshape(IMAGES, GRID, PATCH, GRID, PATCH, CH).transpose(2, 4, 5, 0, 1, 3)
    chunks = lambda m, n: m.reshape(n, m.shape[0] // n, *m.shape[1:]).swapaxes(0, 1)
    arrays = {}
    arrays["patches"] = np.concatenate([chunks(x.reshape(PATCH * PATCH * CH, TOK), PK),
                                        chunks(a["L0_tok_W_proj"], PK)], axis=2)
    arrays["pos"] = chunks(np.tile(a["L0_tok_pos_table"], (IMAGES, 1)), NT)
    wqk = np.zeros((KP, 2, 2, QC, 128), np.float32)
    for j, name in enumerate(("L0_attn_Wq", "L0_attn_Wk")):
        w = chunks(a[name], 2).reshape(KP, 2, QC, 2, TRI * D)
        for t in range(2):
            wqk[:, :, j, :, 64 * t:64 * t + TRI * D] = w[:, :, :, t, :]
    arrays["wqk"] = wqk.reshape(KP, -1)
    wo = chunks(a["L0_attn_Wo"], 2).reshape(2, TRI, D, 2, C).swapaxes(0, 1).reshape(KP, 2, C)
    wvc = a["L0_attn_Wv"].reshape(C, 2, 2, TRI * D).swapaxes(1, 2).reshape(C, C)
    arrays["wvo"] = np.stack([chunks(wvc, 2), wo], 2).reshape(KP, -1)
    arrays["w1"] = np.stack([a[f + n].reshape(E, 2, KP, HID).swapaxes(1, 2).reshape(E, KP, W1N)
                             for n in ("w_slow1", "w_fast1", "h_fast1")], 2)
    arrays["w2"] = np.stack([a[f + n].reshape(E, HC, 128, C).swapaxes(1, 2).reshape(E, 128, W2N)
                             for n in ("w_slow2", "w_fast2", "h_fast2")], 2)
    ws = np.zeros((128, E, HC + 4), np.float32)
    ws[:, :, 0:HC] = a[f + "b1"].reshape(E, HC, 128).transpose(2, 0, 1)
    ws[0:KP, :, HC:HC + 2] = a[f + "b2"].reshape(E, 2, KP).transpose(2, 0, 1)
    ws[:, :, HC + 2] = a[f + "m_gate1"]
    ws[:, :, HC + 3] = a[f + "m_gate2"]
    arrays["wsmall"] = ws

    s = np.zeros((128, SMALL), np.float32)

    def put(name, value):
        lo, hi = _cols[name]
        s[0:value.shape[0], lo:hi] = value.reshape(value.shape[0], -1)

    p = np.arange(128)[:, None]
    put("ident", np.eye(128, dtype=np.float32))
    put("before", np.triu(np.ones((TT, TT), np.float32), 1))
    head = lambda q, n: (q // D == n) & (q < TRI * D)
    put("qmask", np.where(head(p % 64, np.arange(TRI)), np.float32(D ** -0.5), np.float32(0)))
    put("lam", np.repeat(a["L0_attn_lambda_p"].reshape(NTRI, TRI).T, KEYS, axis=0))
    put("energy", np.tile(a[f + "energy"], (128, 1)))
    put("fatigue", np.tile(a[f + "fatigue"], (128, 1)))
    put("iota", np.tile(np.arange(E, dtype=np.float32), (128, 1)))
    put("token", (p[0:TT] + TT * np.arange(NT)).astype(np.float32))
    n = np.arange(E * ST)
    put("slot", (p + 128 * (n % ST)).astype(np.float32))
    put("expert", np.tile((n // ST).astype(np.float32), (128, 1)))
    put("bo", np.tile(a["L0_attn_bo"], (128, 1)))
    put("bp", np.tile(a["L0_tok_b_proj"], (128, 1)))
    put("rw", chunks(a[f + "router_w"].T, 2))
    put("probeT", chunks(a[f + "probe_w"].T, 2))
    put("probe", a[f + "probe_w"])
    put("embT", a[f + "router_emb"].T)
    arrays["small"] = s
    arrays = {f"in_{k}": np.ascontiguousarray(arrays[k]) for k in _INPUTS}

    nc = bacc.Bacc("TRN2", target_bir_lowering=False, num_devices=1)
    ins = [nc.dram_tensor(k, v.shape, mybir.dt.from_np(v.dtype), kind="ExternalInput").ap()
           for k, v in arrays.items()]
    out = nc.dram_tensor("out_rows", (TOK, C), F32, kind="ExternalOutput").ap()
    build(nc, *ins, out)
    r = run(nc, [arrays], core_ids=[0])
    return r.results[0]["out_rows"].reshape(IMAGES, KEYS, C)
```

```python
from contextlib import ExitStack

import numpy as np

import concourse.bass as bass
from concourse import mybir

F32 = mybir.dt.float32
F32R = mybir.dt.float32r
F16 = mybir.dt.float16
I32 = mybir.dt.int32
U32 = mybir.dt.uint32
ALU = mybir.AluOpType
ACT = mybir.ActivationFunctionType
AX = mybir.AxisListType.X

IMAGES, SIDE, CH, PATCH = 16, 96, 3, 16
GRID = SIDE // PATCH
KEYS = GRID * GRID
TOK = IMAGES * KEYS
C = 192
KP = C // 2
PK = PATCH * PATCH * CH // 128
GROUPS = 2
GI = IMAGES // GROUPS
GT = TOK // GROUPS
TT = 96
NT = TOK // TT
TG = NT // GROUPS
HEADS, D = 12, 16
TRI = 3
ROWS = TRI * KEYS
NTRI = HEADS // TRI
QC = 4
E, HID = 8, 768
HC = HID // 128
CAP = 256
ST = CAP // 128
ROUNDS = -(-TOK // CAP)
XROW = C + 4
DR = 24
EPS = 1e-5
XS_PARTS = ((0, 1), (1, 2), (2, 4), (4, 8))
STAGES = 3
TOTALS_AT = ({1: 4, 2: 5, 4: 6, 5: 7}, {2: 4, 3: 5, 5: 6, 6: 7})
WARM = 10
BEYOND = 4096.0
FALLBACK_LINKS = 12
SBANK = (4, 0)
QKBANK = ((2, 3, 0, 1), (0, 1, 2, 3))
W1N, W2N = 2 * HID, HC * C

_cols = {}
_next = 0
for _name, _n in (("ident", 128), ("before", TT), ("qmask", TRI), ("lam", NTRI),
                  ("energy", E), ("fatigue", E), ("iota", E), ("token", NT),
                  ("slot", E * ST), ("expert", E * ST), ("bo", C), ("bp", C), ("rw", 2 * E),
                  ("probeT", 2 * DR), ("probe", C), ("embT", E)):
    _cols[_name] = (_next, _next + _n)
    _next += _n
SMALL = _next


def build(nc, patches, pos, wqk, wvo, small, w1, w2, wsmall, b2, out):
    ctx = ExitStack()
    with ctx:
        def sb(name, shape, dt=F32):
            return ctx.enter_context(nc.sbuf_tensor(name, shape, dt))

        def sem(name):
            return ctx.enter_context(nc.semaphore(name))

        psum = ctx.enter_context(nc.psum_tensor("psum", [128, 8, 512], F32))
        bank = [psum[:, i, :] for i in range(8)]

        v_dram = nc.dram_tensor("v_rows", [2, TOK, C], F32, kind="Internal").ap()
        xs_dram = nc.dram_tensor("slot_rows", [E * CAP, XROW], F32, kind="Internal").ap()

        stage = sb("stage", [128, STAGES, 2 * W1N + 2 * W2N])
        wsm = sb("wsm", [128, E, HC + 2])
        ready = sb("ready", [128, 2, 2 * W1N + 2 * W2N], F32R)
        w1h = [ready[0:KP, s, 0:W1N].rearrange("p (k n) -> p k n", k=2) for s in range(2)]
        w1l = [ready[0:KP, s, W1N:2 * W1N].rearrange("p (k n) -> p k n", k=2) for s in range(2)]
        w2h = [ready[:, s, 2 * W1N:2 * W1N + W2N].rearrange("p (k n) -> p k n", k=HC) for s in range(2)]
        w2l = [ready[:, s, 2 * W1N + W2N:].rearrange("p (k n) -> p k n", k=HC) for s in range(2)]
        PW = TOK + C
        later = stage[:, 1:, :].rearrange("p s n -> p (s n)")
        pwraw = later[:, 0:PK * PW].rearrange("p (k n) -> p k n", k=PK)
        pwh = ready[:, 0, 0:PK * PW].rearrange("p (k n) -> p k n", k=PK)
        pwl = ready[:, 1, 0:PK * PW].rearrange("p (k n) -> p k n", k=PK)
        QKN = 2 * 2 * QC * 128
        VON = 2 * 2 * C
        qkraw = later[0:KP, PK * PW:PK * PW + QKN]
        voraw = later[0:KP, PK * PW + QKN:PK * PW + QKN + VON]
        fr = sb("fr", [128, 2, max(QKN + VON, 2 * HC * CAP)], F32R)
        wq = [fr[0:KP, s, 0:QKN].rearrange("p (k a c n) -> p k a c n", k=2, a=2, c=QC) for s in range(2)]
        wv = [fr[0:KP, s, QKN:QKN + VON].rearrange("p (k a n) -> p k a n", k=2, a=2) for s in range(2)]

        sm = sb("sm", [128, SMALL])

        def small_of(name, rows=128):
            a, b = _cols[name]
            return sm[0:rows, a:b]

        ones = sb("ones", [128, 128])
        ones16 = sb("ones16", [TT, 128], F16)
        before16 = sb("before16", [TT, TT], F16)
        nhalf = sb("nhalf", [128, E])
        phalf = sb("phalf", [128, E])
        zero = sb("zero", [128, XROW])
        held = sb("held", [1, 3 * E + 2])
        h = sb("h", [TT, NT, C])
        stats = sb("stats", [TT, 2, NT, 6])
        mv = sb("mv", [TT, 2, NT, 2])
        rstd = sb("rstd", [TT, 2, NT])
        xn = sb("xn", [128, TG * C])
        xnr = xn[0:TT, :].rearrange("p (t c) -> p t c", t=TG)
        xT = sb("xT", [KP, 2, 2, GT], F32R)
        QBN, KTN = 2 * QC * GI * 128, 2 * QC * GT
        q0 = sb("q0", [128, QBN], F16)
        k0 = sb("k0", [128, KTN], F16)
        qk1 = stage[:, 2, :].bitcast(F16)
        qb = [a.rearrange("p (s c b n) -> p s c b n", s=2, c=QC, b=GI) for a in (q0[:, :], qk1[:, 0:QBN])]
        kT = [a.rearrange("p (s c n) -> p s c n", s=2, c=QC) for a in (k0[:, :], qk1[:, QBN:QBN + KTN])]
        vrow = sb("vrow", [TT, TG, 2, C])
        vb = sb("vb", [128, GROUPS * GI * 2 * 2 * TRI * D])
        vbd = vb[0:2 * KEYS, :].rearrange("p (g b a j n) -> p g b a j n", g=GROUPS, b=GI, a=2, j=TRI)
        ex = sb("ex", [ROWS, 3, 2 * NTRI, KEYS])
        dif = sb("dif", [ROWS, 4, NTRI, KEYS])
        mx = sb("mx", [ROWS, 2, 2 * NTRI])
        den = sb("den", [ROWS, 2, 2 * NTRI])
        rec = sb("rec", [ROWS, 3, 2 * NTRI])
        lam = sb("lam", [ROWS, NTRI])
        dT = sb("dT", [2 * KEYS, 2, 4, ROWS])
        oT = sb("oT", [KP, 2, 2, GT], F32R)
        xrow = sb("xrow", [TT, NT, XROW])
        x2T = sb("x2T", [KP, 2, 2, TT])
        rmat = sb("rmat", [KP, 2, 2 * E + DR])
        gain = sb("gain", [KP, 4, E])
        align = sb("align", [KP, 3, E])
        embsq = sb("embsq", [DR, E])
        lconst = sb("lconst", [TT, E])
        rsc = sb("rsc", [TT, TG, 2 * E + DR])
        usq = sb("usq", [TT, TG, DR])
        un = sb("un", [TT, 2, TG])
        logit = sb("logit", [TT, TG, E])
        top = sb("top", [TT, TG, 8])
        topi = sb("topi", [TT, TG, 8], U32)
        topf = sb("topf", [TT, NT, 2])
        gt = sb("gt", [TT, 4, TG])
        hot = sb("hot", [TT, TG * 2, E])
        hots = sb("hots", [TT, NT, E], F16)
        rk = sb("rk", [TT, TG, 2, E])
        rank = sb("rank", [TT, NT, 2])
        base = sb("base", [TT, NT, 2])
        live = sb("live", [TT, 2, NT, 2])
        place = sb("place", [TT, NT, 2])
        idx = sb("idx", [TT, NT, 2], U32)
        cnt = sb("cnt", [128, E])
        rounds_f = sb("rounds_f", [128, 3])
        rounds_i = sb("rounds_i", [128, 1], I32)
        slive = sb("slive", [128, E * ST])
        stok = sb("stok", [128, E * ST])
        sgate = sb("sgate", [128, E * ST])
        sidx = sb("sidx", [128, E * ST], U32)

        xs = q0[:, :].bitcast(F32)[:, 0:E * ST * XROW] \
            .rearrange("p (n c) -> p n c", c=XROW)
        hh = [fr[:, :, :].rearrange("p a n -> p (a n)")[:, (2 * s) * HC * CAP:(2 * s + 1) * HC * CAP]
              .rearrange("p (k n) -> p k n", k=HC) for s in range(2)]
        hl = [fr[:, :, :].rearrange("p a n -> p (a n)")[:, (2 * s + 1) * HC * CAP:(2 * s + 2) * HC * CAP]
              .rearrange("p (k n) -> p k n", k=HC) for s in range(2)]
        xg = [xT[:, :, :, 0:CAP], oT[:, :, :, 0:CAP]]
        relu = [vb[:, s * 2 * CAP:(s + 1) * 2 * CAP] for s in range(2)]
        hsq = [vb[:, (2 + s) * 2 * CAP:(3 + s) * 2 * CAP] for s in range(2)]
        yg = [vb[:, 8 * CAP + s * ST * C:8 * CAP + (s + 1) * ST * C].rearrange("p (s c) -> p s c", s=ST)
              for s in range(2)]
        yb = xn[:, 0:ST * C].rearrange("p (s c) -> p s c", s=ST)
        B2_EARLY = (QBN // 2 - E * ST * XROW) // C
        b2b = (q0[:, :].bitcast(F32)[:, E * ST * XROW:E * ST * XROW + B2_EARLY * C],
               k0[:, :].bitcast(F32)[:, 0:(E - B2_EARLY) * C])

        patch_in = [sem(f"patch_in{k}") for k in range(PK)]
        small_in, pos_in, qk_in, vo_in, wsmall_in = (
            sem("small_in"), sem("pos_in"), sem("qk_in"), sem("vo_in"), sem("wsmall_in"))
        slow_in = [[sem(f"slow{p}_in{s}") for s in range(STAGES)] for p in (1, 2)]
        fast_in = [[sem(f"fast{p}_in{s}") for s in range(STAGES)] for p in (1, 2)]
        zero_there = sem("zero_there")
        zero_out, v_out, v_in = sem("zero_out"), [sem("v_out0"), sem("v_out1")], [sem("v_in0"), sem("v_in1")]
        out_init, scattered = sem("out_init"), sem("scattered")
        xs_in = [sem(f"xs_in{j}") for j in range(len(XS_PARTS))]
        added = sem("added")
        memset_done, v_zeroed, q_zeroed, pos_biased, h_biased = (
            sem("memset_done"), sem("v_zeroed"), sem("q_zeroed"), sem("pos_biased"), sem("h_biased"))
        pw_hi, pw_lo, qk_hi0, qk_lo0, vo_hi, vo_lo = (
            sem("pw_hi"), sem("pw_lo"), sem("qkw_hi"), sem("qkw_lo"), sem("vow_hi"), sem("vow_lo"))
        lam_done, consts16, emb_sq, gain_ps, gain_n2, gain_pow, rmat_done = (
            sem("lam_done"), sem("consts16"), sem("emb_sq"), sem("gain_ps"), sem("gain_n2"),
            sem("gain_pow"), sem("rmat_done"))
        emb_ready, emb_taken, mv_done, rstd_done, xn_done = (
            sem("emb_ready"), sem("emb_taken"), sem("mv_done"), sem("rstd_done"), sem("xn_done"))
        xT_ready, xT_hi, xT_lo = sem("xT_ready"), sem("xT_hi"), sem("xT_lo")
        qk_ready, qk_hi, qk_lo = sem("qk_ready"), sem("qk_hi"), sem("qk_lo")
        v_ready, v_taken = sem("v_ready"), sem("v_taken")
        s_ready, s_taken, mx_done, exp_done, den_done, rec_done, dif_done = (
            sem("s_ready"), sem("s_taken"), sem("mx_done"), sem("exp_done"), sem("den_done"), sem("rec_done"),
            sem("dif_done"))
        dT_ready, dT_taken, pv_ready, oT_hi, oT_done = (
            sem("dT_ready"), sem("dT_taken"), sem("pv_ready"), sem("oT_hi"), sem("oT_done"))
        wo_ready, h2_done, x2_done = sem("wo_ready"), sem("h2_done"), sem("x2_done")
        x2T_ready, x2T_taken, rt_ready, rt_taken = (
            sem("x2T_ready"), sem("x2T_taken"), sem("rt_ready"), sem("rt_taken"))
        un_clamped, un_pow, gap_done, gexp_done, row_done = (
            sem("un_clamped"), sem("un_pow"), sem("gap_done"), sem("gexp_done"), sem("row_done"))
        hots_done, rank_ready, rank_taken, count_ready = (
            sem("hots_done"), sem("rank_ready"), sem("rank_taken"), sem("count_ready"))
        count_taken = sem("count_taken")
        idx_done, rounds_done, sidx_done = sem("idx_done"), sem("rounds_done"), sem("sidx_done")
        w_added = [[sem(f"w{p}_added{s}") for s in range(STAGES)] for p in (1, 2)]
        w_sum = [sem("w1_sum"), sem("w2_sum")]
        w_hi = [sem("w1_hi"), sem("w2_hi")]
        w_lo = [sem("w1_lo"), sem("w2_lo")]
        xg_ready, xg_hi, xg_lo = sem("xg_ready"), sem("xg_hi"), sem("xg_lo")
        l1_ready, relu_done, sq_done, h_hi, h_lo = (
            sem("l1_ready"), sem("relu_done"), sem("sq_done"), sem("h_hi"), sem("h_lo"))
        b2_in, y_ready, y_taken, yg_done = sem("b2_in"), sem("y_ready"), sem("y_taken"), sem("yg_done")
        dve_self = sem("dve_self")
        pool_self = sem("pool_self")

        def at(eng, s, value):
            if not isinstance(value, int) or value > 0:
                eng.wait_ge(s, value)

        ident = small_of("ident")
        identR = ident[0:ROWS, 0:ROWS]
        qmask = small_of("qmask")

        def group(i):
            return i // TG, i % TG

        def bc(ap, axis, n):
            a = ap.unsqueeze(axis)
            shape = list(a.shape)
            shape[axis] = n
            return a.to_broadcast(shape)

        def qk_bank(n):
            return bank[QKBANK[n // (2 * QC)][n % 4]]

        def x2T_bank(i):
            return bank[3 if i < TG else 3 * (i % 2)]

        def wo_place(i):
            t = i % TG
            return bank[2 + t // 2][0:TT, t % 2 * C:(t % 2 + 1) * C]

        def xT_bank(i):
            return bank[4 if i == NT - 1 else 6 + i % 2]

        def v_bank(i):
            return bank[(2 if i < TG else 6) + i % 2]

        def pair_banks(u):
            return (bank[5], bank[4]) if u == IMAGES // 2 - 1 else (bank[6], bank[7])

        def outputs(u):
            first = 2 * u * KEYS - u // (GI // 2) * GT
            src = pair_banks(u)[1][0:KP, 0:4 * KEYS].rearrange("p (b k n) -> p k b n", b=2, k=2)
            return src, [oT[:, s, :, first:first + 2 * KEYS].rearrange("p k (b n) -> p k b n", b=2)
                         for s in range(2)]

        def staged(e, part):
            a = stage[0:KP, e % STAGES, 0:2 * W1N] if part == 0 else stage[:, e % STAGES, 2 * W1N:]
            return a.rearrange("p (a n) -> p a n", a=2)

        def staged_count(r, e):
            return ((E - 1 - e % STAGES) // STAGES + 1) * 16 * r + (e // STAGES + 1) * 16

        def gain_w(n, part):
            return wsm[0:(KP if part == 0 else 128), n % E, HC + part:HC + 1 + part]

        def rounds_of(eng):
            eng.wait_ge(rounds_done, 1)
            return eng.value_load(rounds_i[0:1, 0:1], min_val=1, max_val=ROUNDS)

        def more_rounds(eng, body):
            n = rounds_of(eng)
            with eng.If(n > 1):
                with eng.Fori(1, n) as r:
                    body(r)
            return n

        block = ctx.enter_context(nc.Block())

        @block.sync
        def _(sp):
            for k in range(PK):
                sp.dma_start(pwraw[:, k, :], patches[:, k, :]).then_inc(patch_in[k], 16)
            sp.dma_start(h[:, :, :], pos).then_inc(pos_in, 16)
            sp.dma_start(sm[:, :], small).then_inc(small_in, 16)
            sp.dma_start(qkraw, wqk).then_inc(qk_in, 16)
            sp.dma_start(voraw, wvo).then_inc(vo_in, 16)
            sp.dma_start(wsm[:, :, :], wsmall).then_inc(wsmall_in, 16)

            def load(r, e, part, row):
                freed = (w_lo, w_sum)[row][part]
                if isinstance(r, int):
                    at(sp, freed, e - STAGES + 1)
                    if 0 < e < STAGES:
                        sp.wait_ge(pw_lo, PK)
                        sp.wait_ge(qk_lo0, 2)
                        sp.wait_ge(vo_lo, 1)
                    if e == 2:
                        sp.wait_ge(s_ready, IMAGES)
                else:
                    sp.wait_ge(freed, E * r + (e - STAGES + 1 if e >= STAGES else 0))
                sp.dma_start(staged(e, part)[:, row, :], (w1, w2)[part][e, :, row]) \
                  .then_inc((slow_in, fast_in)[row][part][e % STAGES], 16)

            def load_parts(e, *rows):
                for part in range(2):
                    for row in rows:
                        load(0, e, part, row)

            def v_store(g):
                sp.wait_ge(v_taken, TG * (g + 1))
                for s in range(2):
                    sp.dma_start(v_dram[s, g * GT:(g + 1) * GT, :].rearrange("(t p) c -> p t c", p=TT),
                                  vrow[:, :, s, :]).then_inc(v_out[g], 16)

            def v_blocks(g):
                sp.wait_ge(v_out[g], 32)
                for s in range(2):
                    sp.dma_start(vbd[s * KEYS:(s + 1) * KEYS, g].rearrange("p b a j n -> p b (a j n)"),
                                  v_dram[s, g * GT:(g + 1) * GT, :].rearrange("(b p) n -> p b n", p=KEYS)) \
                       .then_inc(v_in[g], 16)

            def residual_out(g):
                sp.wait_ge(h2_done, TG * (g + 1))
                sp.dma_start(out[g * GT:(g + 1) * GT, :].rearrange("(t p) c -> p t c", p=TT),
                              h[:, TG * g:TG * (g + 1), :]).then_inc(out_init, 16)

            def load_slots(r):
                sp.wait_ge(scattered, (r + 1) * (2 * NT * 16))
                if isinstance(r, int):
                    sp.wait_ge(s_ready, IMAGES)
                for j, (a, b) in enumerate(XS_PARTS):
                    part = slice(a * ST, b * ST)
                    sp.dma_start(xs[:, part, :], xs_dram.rearrange("(n p) c -> p n c", p=128)[:, part, :]) \
                       .then_inc(xs_in[j], 16)

            load_parts(0, 1, 0)
            sp.wait_ge(zero_there, 1)
            sp.dma_start(out[TOK:, :].rearrange("(s p) c -> p s c", p=128), bc(zero[:, 0:C], 1, ST)) \
              .then_inc(out_init, 16)
            for g in range(GROUPS):
                v_store(g)
                v_blocks(g)
            sp.wait_ge(v_in[1], 32)
            load_parts(1, 1, 0)
            load(0, 3, 0, 1)
            load(0, 3, 0, 0)
            sp.wait_ge(s_ready, GI)
            for place, first in ((b2b[0], 0), (b2b[1], B2_EARLY * C)):
                sp.dma_start(place, b2[:, first:first + place.shape[1]]
                             .to_broadcast([128, place.shape[1]])).then_inc(b2_in, 16)
            load_parts(2, 1, 0)
            load(0, 3, 1, 1)
            load(0, 3, 1, 0)
            residual_out(0)
            load(0, 4, 0, 1)
            residual_out(1)
            load_slots(0)
            sp.wait_ge(xs_in[-1], 16)
            load(0, 4, 0, 0)
            load(0, 4, 1, 1)
            load(0, 4, 1, 0)
            load_parts(5, 1)
            load_parts(6, 1)
            load(0, 5, 0, 0)
            load(0, 6, 0, 0)
            load(0, 7, 0, 1)
            load(0, 5, 1, 0)
            load(0, 7, 0, 0)
            load(0, 7, 1, 1)
            load(0, 6, 1, 0)
            load(0, 7, 1, 0)

            def fallback(r):
                sp.wait_ge(yg_done, E * r)
                load_slots(r)
                for e in range(E):
                    for part in range(2):
                        for row in (1, 0):
                            load(r, e, part, row)

            more_rounds(sp, fallback)

        @block.tensor
        def _(pe):
            mm = nc.tensor.matmul

            def three(out_, a, b, start, stop):
                mm(out_, a[0], b[0], start=start, stop=False)
                mm(out_, a[0], b[1], start=False, stop=False)
                return mm(out_, a[1], b[0], start=False, stop=stop)

            def router_gains():
                pe.wait_ge(small_in, 16)
                pe.wait_ge(memset_done, 1)
                pe.wait_ge(emb_sq, 1)
                for k in range(2):
                    mm(bank[6][0:KP, k * E:(k + 1) * E], small_of("probe", DR)[:, k * KP:(k + 1) * KP],
                       small_of("embT", DR), start=True, stop=True)
                mm(bank[6][0:KP, 2 * E:3 * E], ones[0:DR, 0:KP], embsq[:, :], start=True, stop=True) \
                    .then_inc(gain_ps, 1)

            pe.wait_ge(memset_done, 1)
            for _ in range(WARM):
                mm(bank[7][:, 0:128], ones[:, :], ones[:, :], start=True, stop=True)

            for k in range(PK):
                pe.wait_ge(pw_lo, k + 1)
                for i in range(NT):
                    last = three(bank[i][0:TT, 0:C],
                                 [a[:, k, i * TT:(i + 1) * TT] for a in (pwh, pwl)],
                                 [a[:, k, TOK:] for a in (pwh, pwl)], k == 0, k == PK - 1)
                    if k == PK - 1:
                        last.then_inc(emb_ready, 1)
                if k == PK - 2:
                    router_gains()

            def xT_tile(i):
                g, t = group(i)
                pe.wait_ge(xn_done, i + 1)
                if i < NT - 1:
                    at(pe, xT_lo, i - 1)
                if i == 0:
                    pe.wait_ge(gain_n2, 1)
                for k in range(2):
                    last = nc.tensor.transpose(xT_bank(i)[0:KP, k * TT:(k + 1) * TT],
                                               xnr[:, t, k * KP:(k + 1) * KP], ident[0:TT, 0:TT])
                last.then_inc(xT_ready, 1)

            def qk(g, m):
                n = 2 * QC * g + m
                if m == 0:
                    pe.wait_ge(xT_lo, TG * (g + 1))
                    pe.wait_ge(qk_lo0, 2)
                if m >= 4:
                    pe.wait_ge(qk_lo, n - 3)
                elif g:
                    pe.wait_ge(v_taken, TG)
                else:
                    pe.wait_ge(emb_taken, QKBANK[0][m] + 1)
                for k in range(2):
                    last = three(qk_bank(n)[:, 0:GT], [w[:, k, m % 2, m // 2, :] for w in wq],
                                 [xT[:, s, k, :] for s in range(2)], k == 0, k == 1)
                last.then_inc(qk_ready, 1)

            def v(i):
                t = i % TG
                pe.wait_ge(vo_lo, 1)
                pe.wait_ge(xT_lo, i + 1)
                if i < 2:
                    pe.wait_ge(qk_lo, 2 * QC - 3 + i)
                elif i < TG:
                    pe.wait_ge(v_taken, i - 1)
                else:
                    pe.wait_ge(xT_lo, NT)
                    pe.wait_ge(v_taken, i - 1)
                for k in range(2):
                    last = three(v_bank(i)[0:TT, 0:C],
                                 [xT[:, s, k, t * TT:(t + 1) * TT] for s in range(2)],
                                 [w[:, k, 0, :] for w in wv], k == 0, k == 1)
                last.then_inc(v_ready, 1)

            def scores(b):
                g, bi = b // GI, b % GI
                at(pe, s_taken, b - 1)
                if b < 2:
                    pe.wait_ge(emb_taken, NT)
                if bi == 0:
                    pe.wait_ge(qk_lo, 2 * QC * (g + 1))
                    pe.wait_ge(q_zeroed, g + 1)
                if b == 1:
                    pe.wait_ge(qk_lo, 4 * QC - 2)
                for c in range(QC):
                    for t in range(2):
                        rows = slice(64 * t, 64 * t + 64)
                        o = psum[:, SBANK[b % 2] + t, c * KEYS:(c + 1) * KEYS]
                        last = three(o, [qb[g][rows, s, c, bi, :] for s in range(2)],
                                     [kT[g][rows, s, c, bi * KEYS:(bi + 1) * KEYS] for s in range(2)],
                                     True, True)
                last.then_inc(s_ready, 1)

            def dT_pair(u):
                pe.wait_ge(dif_done, 2 * u + 2)
                if u == IMAGES // 2 - 1:
                    pe.wait_ge(s_taken, IMAGES - 1)
                else:
                    at(pe, dT_taken, u)
                if u == 0:
                    pe.wait_ge(v_taken, NT)
                for m in range(4):
                    b = 2 * u + m // 2
                    last = nc.tensor.transpose(
                        pair_banks(u)[0][0:2 * KEYS, m * ROWS:(m + 1) * ROWS],
                        dif[:, b % 4, 2 * (m % 2):2 * (m % 2) + 2, :].rearrange("p j n -> p (j n)"),
                        identR)
                last.then_inc(dT_ready, 1)

            def pv_pair(u):
                g = u // (GI // 2)
                pe.wait_ge(dT_taken, u + 1)
                pe.wait_ge(v_in[g], 32)
                at(pe, oT_done, u if u < IMAGES // 2 - 1 else 0)
                if u == 0:
                    pe.wait_ge(v_taken, NT)
                for m in range(4):
                    bi = (2 * u + m // 2) % GI
                    for j in range(TRI):
                        last = mm(pair_banks(u)[1][2 * D * j:2 * D * (j + 1), m * KEYS:(m + 1) * KEYS],
                                  vbd[:, g, bi, m % 2, j, :],
                                  dT[:, u % 2, m, j * KEYS:(j + 1) * KEYS], start=True, stop=True)
                last.then_inc(pv_ready, 1)

            def wo(g):
                pe.wait_ge(oT_done, GI // 2 * (g + 1))
                at(pe, qk_lo, 4 * QC)
                at(pe, rt_taken, g)
                at(pe, x2T_taken, TG * g)
                for t in range(TG):
                    for k in range(2):
                        last = three(wo_place(t), [oT[:, s, k, t * TT:(t + 1) * TT] for s in range(2)],
                                     [w[:, k, 1, :] for w in wv], k == 0, k == 1)
                    if t:
                        last.then_inc(wo_ready, 1)

            def router(g):
                pe.wait_ge(h2_done, TG * (g + 1))
                pe.wait_ge(rmat_done, 1)
                if g:
                    pe.wait_ge(s_taken, IMAGES)
                for t in range(TG + 1):
                    if t < TG:
                        i = TG * g + t
                        pe.wait_ge(x2_done, i + 1)
                        at(pe, x2T_taken, i if i <= TG else i - 1)
                        for k in range(2):
                            last = nc.tensor.transpose(x2T_bank(i)[0:KP, k * TT:(k + 1) * TT],
                                                       xrow[:, i, k * KP:(k + 1) * KP],
                                                       ident[0:TT, 0:TT])
                        last.then_inc(x2T_ready, 1)
                    if t > 0:
                        i = TG * g + t - 1
                        pe.wait_ge(x2T_taken, i + 1)
                        for k in range(2):
                            last = mm(bank[2][0:TT, (t - 1) * (2 * E + DR):t * (2 * E + DR)],
                                      x2T[:, i % 2, k, :], rmat[:, k, :], start=(k == 0), stop=(k == 1))
                        last.then_inc(rt_ready, 1)

            def ranks(g):
                pe.wait_ge(consts16, 2)
                pe.wait_ge(hots_done, g + 1)
                pe.wait_ge(s_taken, IMAGES)
                at(pe, rank_taken, g)
                rb = bank[1]
                o = rb[0:TT, g * TG * E:(g + 1) * TG * E]
                mm(o, before16[:, :], hots[:, TG * g:TG * (g + 1), :].rearrange("p t e -> p (t e)"),
                   start=True, stop=False, skip_group_check=True)
                for j in range(TG * (g + 1) - 1):
                    first = max(j + 1, TG * g)
                    last = mm(rb[0:TT, first * E:(g + 1) * TG * E], ones16[:, 0:TT],
                              bc(hots[:, j, :], 1, TG * (g + 1) - first), start=False,
                              stop=(j == TG * (g + 1) - 2), skip_group_check=True)
                last.then_inc(rank_ready, 1)

            def counts():
                pe.wait_ge(oT_done, IMAGES // 2)
                for i in range(NT):
                    last = mm(bank[7][:, 0:E], ones16[:, :], hots[:, i, :], start=(i == 0), stop=(i == NT - 1))
                last.then_inc(count_ready, 1)

            for i in range(TG):
                xT_tile(i)
            for m in range(2 * QC):
                qk(0, m)
            for i in range(TG):
                v(i)
            for i in range(TG, NT):
                xT_tile(i)
            for m in range(2 * QC):
                qk(1, m)
                if m % 2 and m // 2 < TG:
                    v(TG + m // 2)
            scores(0)
            for b in range(IMAGES):
                if b + 1 < IMAGES:
                    scores(b + 1)
                if b >= 5 and b % 2:
                    pv_pair((b - 5) // 2)
                if b >= 4 and b % 2 == 0:
                    dT_pair((b - 4) // 2)
                if b == GI + 4:
                    wo(0)
            router(0)
            dT_pair(IMAGES // 2 - 2)
            dT_pair(IMAGES // 2 - 1)
            pv_pair(IMAGES // 2 - 2)
            pv_pair(IMAGES // 2 - 1)
            wo(1)
            ranks(0)
            router(1)
            ranks(1)
            counts()

            def slot_rows(r, e):
                j = [a <= e < b for a, b in XS_PARTS].index(True)
                pe.wait_ge(xs_in[j], (r + 1) * 16)
                at(pe, xg_lo, E * r + e)
                if e == 0:
                    pe.wait_ge(s_taken, IMAGES)
                for k in range(2):
                    for s in range(ST):
                        last = nc.tensor.transpose(
                            bank[0][0:KP, k * CAP + s * 128:k * CAP + (s + 1) * 128],
                            xs[:, e * ST + s, k * KP:(k + 1) * KP], ident[:, :])
                last.then_inc(xg_ready, 1)

            def layer1(r, e, p):
                n = E * r + e
                if p == 0:
                    pe.wait_ge(xg_lo, n + 1)
                    pe.wait_ge(w_lo[0], n + 1)
                at(pe, relu_done, 3 * (n - 1) + p + 1)
                if isinstance(r, int) and n == 0:
                    pe.wait_ge(*((rank_taken, GROUPS), (rt_taken, GROUPS), (x2T_taken, NT))[p])
                for q in range(2):
                    for k in range(2):
                        last = three(bank[1 + p][:, q * CAP:(q + 1) * CAP],
                                     [w[e % 2][:, k, (2 * p + q) * 128:(2 * p + q + 1) * 128]
                                      for w in (w1h, w1l)],
                                     [xg[e % 2][:, s, k, :] for s in range(2)], k == 0, k == 1)
                last.then_inc(l1_ready, 1)

            def layer2(r, e, p):
                n = E * r + e
                pe.wait_ge(h_lo, 3 * n + p + 1)
                if p == 0:
                    pe.wait_ge(w_lo[1], n + 1)
                    at(pe, y_taken, n - 1)
                    if isinstance(r, int) and n == 0:
                        pe.wait_ge(s_taken, IMAGES)
                        pe.wait_ge(oT_done, IMAGES // 2)
                        pe.wait_ge(count_taken, 1)
                for q in range(2):
                    for s in range(ST):
                        c = 2 * p + q
                        last = three(bank[4 + 2 * (e % 2) + s][:, 0:C],
                                     [a[e % 2][:, c, s * 128:(s + 1) * 128] for a in (hh, hl)],
                                     [w[e % 2][:, c, :] for w in (w2h, w2l)], c == 0, c == HC - 1)
                if p == 2:
                    last.then_inc(y_ready, 1)

            slot_rows(0, 0)
            for s in range(E + 1):
                if s < E:
                    layer1(0, s, 0)
                if s >= 1:
                    layer2(0, s - 1, 0)
                if s + 1 < E:
                    slot_rows(0, s + 1)
                for p in (1, 2):
                    if s < E:
                        layer1(0, s, p)
                    if s >= 1:
                        layer2(0, s - 1, p)

            def fallback(r):
                for e in range(E):
                    slot_rows(r, e)
                    for p in range(3):
                        layer1(r, e, p)
                    for p in range(3):
                        layer2(r, e, p)

            more_rounds(pe, fallback)

        @block.scalar
        def _(act):
            for k in range(PK):
                act.wait_ge(patch_in[k], 16)
                nc.scalar.activation(pwh[:, k, :], pwraw[:, k, :], ACT.Copy).then_inc(pw_hi, 1)
            act.wait_ge(qk_in, 16)
            for k in range(2):
                n = slice(k * (QKN // 2), (k + 1) * (QKN // 2))
                nc.scalar.activation(fr[0:KP, 0, n], qkraw[:, n], ACT.Copy).then_inc(qk_hi0, 1)
            act.wait_ge(vo_in, 16)
            nc.scalar.activation(fr[0:KP, 0, QKN:QKN + VON], voraw, ACT.Copy).then_inc(vo_hi, 1)
            act.wait_ge(small_in, 16)
            nc.scalar.activation(lam[:, :], small_of("lam", ROWS), ACT.Exp).then_inc(lam_done, 1)

            def xT_high(i):
                g, t = group(i)
                act.wait_ge(xT_ready, i + 1)
                if i == TG:
                    act.wait_ge(v_ready, TG)
                nc.scalar.activation(xT[:, 0, :, t * TT:(t + 1) * TT],
                                     xT_bank(i)[0:KP, 0:2 * TT].rearrange("p (k n) -> p k n", k=2),
                                     ACT.Copy).then_inc(xT_hi, 1)

            def qk_high(g, m):
                n, c = 2 * QC * g + m, m // 2
                if g:
                    act.wait_ge(qk_lo0, 2)
                    act.wait_ge(vo_lo, 1)
                act.wait_ge(qk_ready, n + 1)
                src = qk_bank(n)[:, 0:GT]
                if m % 2:
                    nc.scalar.activation(kT[g][:, 0, c, :], src, ACT.Copy).then_inc(qk_hi, 1)
                else:
                    src = src.rearrange("p (b n) -> p b n", b=GI)
                    for j in range(TRI):
                        last = nc.scalar.activation(
                            qb[g][:, 0, c, :, j * KEYS:(j + 1) * KEYS], src, ACT.Copy,
                            scale=qmask[:, j:j + 1])
                    last.then_inc(qk_hi, 1)

            def v_rows(i):
                t = i % TG
                act.wait_ge(v_ready, i + 1)
                if i >= TG:
                    act.wait_ge(v_out[0], 32)
                if i == 0:
                    act.wait_ge(v_zeroed, 1)
                for s in range(2):
                    last = nc.scalar.activation(
                        vrow[:, t, s, :].rearrange("p (m t n) -> p m t n", t=2, n=D)[:, :, s, :],
                        v_bank(i)[0:TT, s * KP:(s + 1) * KP].rearrange("p (m n) -> p m n", n=D),
                        ACT.Copy)
                last.then_inc(v_taken, 1)

            def exps(b):
                act.wait_ge(s_taken, b + 1)
                nc.scalar.activation(ex[:, b % 3], ex[:, b % 3], ACT.Exp).then_inc(exp_done, 1)

            def dT_copy(u):
                act.wait_ge(dT_ready, u + 1)
                at(act, pv_ready, u - 1)
                nc.scalar.activation(dT[:, u % 2],
                                     pair_banks(u)[0][0:2 * KEYS, 0:4 * ROWS].rearrange("p (m n) -> p m n", m=4),
                                     ACT.Copy).then_inc(dT_taken, 1)

            def output_high(u):
                act.wait_ge(pv_ready, u + 1)
                if u == GI // 2:
                    act.wait_ge(wo_ready, 2)
                src, halves = outputs(u)
                nc.scalar.activation(halves[0], src, ACT.Copy).then_inc(oT_hi, 1)

            def x2T_copy(i):
                act.wait_ge(x2T_ready, i + 1)
                at(act, rt_ready, i - 1)
                nc.scalar.activation(x2T[:, i % 2],
                                     x2T_bank(i)[0:KP, 0:2 * TT].rearrange("p (k n) -> p k n", k=2),
                                     ACT.Copy).then_inc(x2T_taken, 1)

            def gap_exp(g):
                act.wait_ge(gap_done, g + 1)
                nc.scalar.activation(gt[:, 1, :], gt[:, 0, :], ACT.Exp).then_inc(gexp_done, 1)

            def w_high(r, e, part):
                n = E * r + e
                act.wait_ge(w_sum[part], n + 1)
                if isinstance(r, int) and n < 2:
                    act.wait_ge(emb_ready, NT)
                if part == 0:
                    at(act, l1_ready, 3 * (n - 1))
                    src = staged(e, 0)[:, 0, :]
                    dst = w1h[e % 2].rearrange("p k n -> p (k n)")
                else:
                    at(act, y_ready, n - 1)
                    src = staged(e, 1)[:, 0, :]
                    dst = w2h[e % 2].rearrange("p k n -> p (k n)")
                nc.scalar.activation(dst, src, ACT.Copy).then_inc(w_hi[part], 1)

            for i in range(TG):
                xT_high(i)
            for m in range(2 * QC):
                qk_high(0, m)
            for i in range(TG):
                v_rows(i)
            for i in range(TG, NT):
                xT_high(i)
            w_high(0, 0, 0)
            for m in range(2 * QC):
                qk_high(1, m)
                if m % 2 and m // 2 < TG:
                    v_rows(TG + m // 2)
            w_high(0, 0, 1)
            for b in range(IMAGES):
                exps(b)
                if b >= 4 and b % 2 == 0:
                    dT_copy((b - 4) // 2)
                if b >= 5 and b % 2:
                    output_high((b - 5) // 2)
            for i in range(TG):
                x2T_copy(i)
            dT_copy(IMAGES // 2 - 2)
            dT_copy(IMAGES // 2 - 1)
            output_high(IMAGES // 2 - 2)
            output_high(IMAGES // 2 - 1)
            gap_exp(0)
            for i in range(TG, NT):
                x2T_copy(i)
            gap_exp(1)
            w_high(0, 1, 0)

            def slot_high(r, e):
                n = E * r + e
                act.wait_ge(xg_ready, n + 1)
                at(act, l1_ready, 3 * (n - 1))
                nc.scalar.activation(xg[e % 2][:, 0], bank[0][0:KP, :].rearrange("p (k n) -> p k n", k=2),
                                     ACT.Copy).then_inc(xg_hi, 1)

            def hidden(r, e, p):
                n = E * r + e
                j = 3 * n + p
                slot = (3 * e + p) % 2
                act.wait_ge(l1_ready, j + 1)
                at(act, sq_done, j - 1)
                if isinstance(r, int) and j == 0:
                    act.wait_ge(wsmall_in, 16)
                for q in range(2):
                    last = nc.scalar.activation(
                        relu[slot][:, q * CAP:(q + 1) * CAP], bank[1 + p][:, q * CAP:(q + 1) * CAP],
                        ACT.Relu, bias=wsm[:, e, 2 * p + q:2 * p + q + 1])
                last.then_inc(relu_done, 1)
                act.wait_ge(relu_done, j + 1)
                at(act, h_lo, j - 1)
                nc.scalar.activation(hsq[slot], relu[slot], ACT.Square).then_inc(sq_done, 1)

            def gated(r, e):
                n = E * r + e
                act.wait_ge(y_taken, n + 1)
                act.wait_ge(sidx_done, r + 1)
                at(act, added, (n - 1) * ST * 16)
                for s in range(ST):
                    last = nc.scalar.activation(yg[e % 2][:, s, :], yb[:, s, :], ACT.Copy,
                                                scale=sgate[:, e * ST + s:e * ST + s + 1])
                last.then_inc(yg_done, 1)

            w_high(0, 1, 1)
            slot_high(0, 0)
            for s in range(E + 1):
                if 2 <= s + 1 < E:
                    w_high(0, s + 1, 0)
                if s < E:
                    hidden(0, s, 0)
                if s >= 2:
                    gated(0, s - 2)
                if s + 1 < E:
                    slot_high(0, s + 1)
                if s < E:
                    hidden(0, s, 1)
                    if s >= 2:
                        w_high(0, s, 1)
                    hidden(0, s, 2)
            gated(0, E - 1)

            def fallback(r):
                for e in range(E):
                    w_high(r, e, 0)
                    w_high(r, e, 1)
                    slot_high(r, e)
                    for p in range(3):
                        hidden(r, e, p)
                    gated(r, e)

            more_rounds(act, fallback)

        @block.vector
        def _(dve):
            vec = nc.vector
            links = [0]

            def link(ins, r=0):
                links[0] += 1
                ins.then_inc(dve_self, 1)
                dve.wait_ge(dve_self, links[0] + (0 if isinstance(r, int) else (r - 1) * FALLBACK_LINKS))

            def low(dst, src, hi):
                return vec.tensor_tensor(dst, src, hi.bitcast(F32), ALU.subtract)

            for k in range(PK):
                dve.wait_ge(pw_hi, k + 1)
                low(pwl[:, k, :], pwraw[:, k, :], pwh[:, k, :]).then_inc(pw_lo, 1)

            dve.wait_ge(small_in, 16)
            vec.tensor_tensor(embsq[:, :], small_of("embT", DR), small_of("embT", DR), ALU.mult) \
                .then_inc(emb_sq, 1)
            vec.tensor_copy(before16[:, :], small_of("before", TT)).then_inc(consts16, 1)
            dve.wait_ge(memset_done, 1)
            vec.tensor_copy(ones16[:, :], ones[0:TT, :]).then_inc(consts16, 1)
            vec.tensor_tensor(lconst[:, :], small_of("energy", TT), small_of("fatigue", TT), ALU.subtract) \
                .then_inc(dve_self, 1)
            links[0] += 1
            for i in range(NT):
                vec.tensor_copy(xrow[:, i, C:C + 1], small_of("token", TT)[:, i:i + 1])
            dve.wait_ge(gain_ps, 1)
            link(vec.tensor_copy(align[:, :, :], bank[6][0:KP, 0:3 * E].rearrange("p (k e) -> p k e", k=3)))
            vec.tensor_scalar(gain[:, 1, :], align[:, 2, :], 1e-24, None, ALU.max).then_inc(gain_n2, 1)
            link(vec.tensor_scalar(lconst[:, :], lconst[:, :], 0.1, None, ALU.mult))

            def router_matrix():
                dve.wait_ge(gain_pow, 2)
                link(vec.tensor_scalar(gain[:, 2, :], gain[:, 2, :], 1.0, 0.02 / C, ALU.add, ALU.mult))
                for k in range(2):
                    vec.tensor_tensor(rmat[:, k, 0:E], small_of("rw", KP)[:, k * E:(k + 1) * E],
                                      gain[:, 2, :], ALU.add)
                    vec.scalar_tensor_tensor(rmat[:, k, E:2 * E], align[:, k, :], 0.02,
                                             gain[:, 3, :], ALU.mult, ALU.mult)
                    last = vec.tensor_copy(rmat[:, k, 2 * E:], small_of("probeT", KP)[:, k * DR:(k + 1) * DR])
                last.then_inc(rmat_done, 1)

            def projection_low(k):
                n = slice(k * (QKN // 2), (k + 1) * (QKN // 2))
                dve.wait_ge(qk_hi0, k + 1)
                low(fr[0:KP, 1, n], qkraw[:, n], fr[0:KP, 0, n]).then_inc(qk_lo0, 1)

            def add_rows(i, bnk, done):
                vec.tensor_tensor(h[:, i, :], bnk[0:TT, 0:C], h[:, i, :], ALU.add).then_inc(done, 1)

            def stats1(ln, i):
                vec.bn_stats(stats[:, ln, i, :], h[:, i, :]).then_inc(dve_self, 1)
                links[0] += 1

            def stats2(ln, i):
                vec.bn_aggr(mv[:, ln, i, :], stats[:, ln, i, :]).then_inc(mv_done, 1)

            def normalise(dst, ln, i):
                return vec.tensor_scalar(dst, h[:, i, :], mv[:, ln, i, 0:1], rstd[:, ln, i:i + 1],
                                         ALU.subtract, ALU.mult)

            def embedded(g):
                for i in range(TG * g, TG * g + TG):
                    dve.wait_ge(emb_ready, i + 1)
                    add_rows(i, bank[i], emb_taken)
                if g == 0:
                    embedded_stats(0)

            def embedded_stats(g):
                dve.wait_ge(emb_taken, TG * (g + 1))
                for i in range(TG * g, TG * g + TG):
                    stats1(0, i)
                dve.wait_ge(dve_self, links[0])
                for i in range(TG * g, TG * g + TG):
                    stats2(0, i)

            def ln1(g):
                dve.wait_ge(rstd_done, g + 1)
                if g:
                    dve.wait_ge(xT_ready, TG)
                for t in range(TG):
                    normalise(xnr[:, t, :], 0, TG * g + t).then_inc(xn_done, 1)

            def xT_low(i):
                g, t = group(i)
                dve.wait_ge(xT_hi, i + 1)
                vec.tensor_tensor(xT[:, 1, :, t * TT:(t + 1) * TT],
                                  xT_bank(i)[0:KP, 0:2 * TT].rearrange("p (k n) -> p k n", k=2),
                                  xT[:, 0, :, t * TT:(t + 1) * TT].bitcast(F32), ALU.subtract) \
                    .then_inc(xT_lo, 1)

            def qk_low(g, m):
                n, c = 2 * QC * g + m, m // 2
                dve.wait_ge(qk_hi, n + 1)
                src = qk_bank(n)[:, 0:GT]
                if m % 2:
                    vec.tensor_tensor(kT[g][:, 1, c, :], src, kT[g][:, 0, c, :], ALU.subtract) \
                        .then_inc(qk_lo, 1)
                else:
                    src = src.rearrange("p (b n) -> p b n", b=GI)
                    for j in range(TRI):
                        cols = slice(j * KEYS, (j + 1) * KEYS)
                        last = vec.scalar_tensor_tensor(
                            qb[g][:, 1, c, :, cols], src, qmask[:, j:j + 1], qb[g][:, 0, c, :, cols],
                            ALU.mult, ALU.subtract)
                    last.then_inc(qk_lo, 1)

            def softmax_top(b):
                s = psum[0:ROWS, SBANK[b % 2]:SBANK[b % 2] + 2, 0:QC * KEYS] \
                    .rearrange("p t (c n) -> p c t n", c=QC)
                dve.wait_ge(s_ready, b + 1)
                vec.reduce_max(mx[:, b % 2, :].rearrange("p (c t) -> p c t", t=2), s, AX).then_inc(mx_done, 1)
                if b >= 1:
                    softmax_sum(b - 1)
                dve.wait_ge(mx_done, b + 1)
                at(dve, dif_done, b - 2)
                vec.tensor_tensor(ex[:, b % 3].rearrange("p (c t) n -> p c t n", t=2), s,
                                  bc(mx[:, b % 2, :].rearrange("p (c t) -> p c t", t=2), 3, KEYS),
                                  ALU.subtract) \
                    .then_inc(s_taken, 1)
                if b >= 1:
                    softmax_scale(b - 1)

            def softmax_sum(b):
                dve.wait_ge(exp_done, b + 1)
                vec.reduce_sum(den[:, b % 2, :], ex[:, b % 3], AX).then_inc(den_done, 1)

            def softmax_scale(b):
                dve.wait_ge(den_done, b + 1)
                at(dve, dif_done, b - 2)
                vec.reciprocal(rec[:, b % 3, :], den[:, b % 2, :]).then_inc(rec_done, 1)

            def output_low(u):
                dve.wait_ge(oT_hi, u + 1)
                src, halves = outputs(u)
                vec.tensor_tensor(halves[1], src, halves[0].bitcast(F32), ALU.subtract).then_inc(oT_done, 1)

            def residual(g):
                if g == 0:
                    dve.wait_ge(h_biased, 1)
                for i in range(TG * g, TG * g + TG):
                    dve.wait_ge(wo_ready, 2 * g + 1 + i % TG // 2)
                    add_rows(i, wo_place(i), h2_done)
                dve.wait_ge(h2_done, TG * (g + 1))
                for i in range(TG * g, TG * g + TG):
                    stats1(1, i)
                dve.wait_ge(dve_self, links[0])
                for i in range(TG * g, TG * g + TG):
                    stats2(1, i)

            def ln2(g):
                dve.wait_ge(rstd_done, GROUPS + g + 1)
                for i in range(TG * g, TG * g + TG):
                    normalise(xrow[:, i, 0:C], 1, i).then_inc(x2_done, 1)

            def route_probe(g):
                dve.wait_ge(rt_ready, TG * (g + 1))
                vec.tensor_copy(rsc[:, :, :], bank[2][0:TT, 0:TG * (2 * E + DR)]
                                .rearrange("p (t n) -> p t n", t=TG)).then_inc(rt_taken, 1)
                dve.wait_ge(rt_taken, g + 1)
                link(vec.tensor_tensor(usq[:, :, :], rsc[:, :, 2 * E:], rsc[:, :, 2 * E:], ALU.mult))
                link(vec.reduce_sum(un[:, 0, :], usq[:, :, :], AX))
                vec.tensor_scalar(un[:, 1, :], un[:, 0, :], 1e-24, None, ALU.max).then_inc(un_clamped, 1)

            def route_choose(g):
                dve.wait_ge(un_pow, g + 1)
                link(vec.tensor_tensor(logit[:, :, :], rsc[:, :, E:2 * E], bc(un[:, 0, :], 2, E), ALU.mult))
                link(vec.tensor_tensor(logit[:, :, :], logit[:, :, :], rsc[:, :, 0:E], ALU.add))
                link(vec.tensor_tensor(logit[:, :, :], logit[:, :, :], bc(lconst[:, :], 1, TG), ALU.add))
                for t in range(TG):
                    vec.max(top[:, t, :], logit[:, t, :]).then_inc(dve_self, 1)
                links[0] += TG
                dve.wait_ge(dve_self, links[0])
                vec.tensor_tensor(gt[:, 0, :], top[:, :, 1], top[:, :, 0], ALU.subtract).then_inc(gap_done, 1)

            def route_experts(g):
                for t in range(TG):
                    vec.max_index(topi[:, t, :], top[:, t, :], logit[:, t, :]).then_inc(dve_self, 1)
                links[0] += TG
                dve.wait_ge(dve_self, links[0])
                tiles = slice(TG * g, TG * (g + 1))
                link(vec.tensor_copy(topf[:, tiles, :], topi[:, :, 0:2]))
                link(vec.tensor_tensor(
                    hot[:, :, :], bc(small_of("iota", TT), 1, 2 * TG),
                    bc(topf[:, tiles, :].rearrange("p t k -> p (t k)"), 2, E), ALU.is_equal))
                two = hot[:, :, :].rearrange("p (t k) e -> p t k e", k=2)
                vec.tensor_tensor(hots[:, tiles, :], two[:, :, 0, :], two[:, :, 1, :], ALU.add) \
                    .then_inc(hots_done, 1)
                link(vec.tensor_scalar(base[:, tiles, :], topf[:, tiles, :], float(CAP), None, ALU.mult))

            def route_gates(g):
                tiles = slice(TG * g, TG * (g + 1))
                dve.wait_ge(gexp_done, g + 1)
                link(vec.tensor_scalar(gt[:, 2, :], gt[:, 1, :], 1.0, None, ALU.add))
                link(vec.reciprocal(gt[:, 3, :], gt[:, 2, :]))
                link(vec.tensor_tensor(xrow[:, tiles, C + 1], gt[:, 1, :], gt[:, 3, :], ALU.mult))
                vec.tensor_copy(xrow[:, tiles, C + 3], topf[:, tiles, 0])
                vec.tensor_tensor(xrow[:, tiles, C + 2], gt[:, 3, :], xrow[:, tiles, C + 1], ALU.subtract) \
                    .then_inc(row_done, 1)

            def route_rank(g):
                tiles = slice(TG * g, TG * (g + 1))
                dve.wait_ge(rank_ready, g + 1)
                src = bank[1][0:TT, g * TG * E:(g + 1) * TG * E].rearrange("p (t e) -> p t e", t=TG)
                vec.tensor_tensor(rk[:, :, :, :], hot[:, :, :].rearrange("p (t k) e -> p t k e", k=2),
                                  bc(src, 2, 2), ALU.mult).then_inc(rank_taken, 1)
                dve.wait_ge(rank_taken, g + 1)
                link(vec.reduce_sum(rank[:, tiles, :], rk[:, :, :, :], AX))
                place_rows(tiles, 0)

            def place_rows(tiles, r):
                a, b = rank[:, tiles, :], base[:, tiles, :]
                link(vec.tensor_scalar(live[:, 0, tiles, :], a, 0.0, None, ALU.is_ge), r)
                link(vec.scalar_tensor_tensor(live[:, 1, tiles, :], a, float(CAP), live[:, 0, tiles, :],
                                              ALU.is_lt, ALU.mult), r)
                link(vec.scalar_tensor_tensor(place[:, tiles, :], a, -BEYOND, b, ALU.add, ALU.add), r)
                link(vec.tensor_tensor(place[:, tiles, :], place[:, tiles, :], live[:, 1, tiles, :],
                                       ALU.mult), r)
                vec.tensor_scalar(idx[:, tiles, :], place[:, tiles, :], BEYOND, None, ALU.add) \
                    .then_inc(idx_done, 1)

            def count_rounds():
                dve.wait_ge(count_ready, 1)
                vec.tensor_copy(cnt[:, :], bank[7][:, 0:E]).then_inc(count_taken, 1)
                dve.wait_ge(count_taken, 1)
                link(vec.reduce_max(rounds_f[:, 0:1], cnt[:, :], AX))
                link(vec.tensor_scalar(rounds_f[:, 1:2], rounds_f[:, 0:1], float(CAP), 1.0,
                                       ALU.is_gt, ALU.add))
                for k in range(2, ROUNDS):
                    link(vec.tensor_scalar(rounds_f[:, 2:3], rounds_f[:, 0:1], float(k * CAP), None,
                                           ALU.is_gt))
                    link(vec.tensor_tensor(rounds_f[:, 1:2], rounds_f[:, 1:2], rounds_f[:, 2:3], ALU.add))
                vec.tensor_copy(rounds_i[:, :], rounds_f[:, 1:2]).then_inc(rounds_done, 1)

            def slots(r):
                n = small_of("slot")
                for j in range(len(XS_PARTS)):
                    dve.wait_ge(xs_in[j], (r + 1) * 16)
                link(vec.tensor_tensor(slive[:, :].rearrange("p (e s) -> p e s", e=E),
                                       n.rearrange("p (e s) -> p e s", e=E), bc(cnt[:, :], 2, ST),
                                       ALU.is_lt), r)
                link(vec.scalar_tensor_tensor(stok[:, :], xs[:, :, C], -float(TOK), n,
                                              ALU.add, ALU.subtract), r)
                link(vec.tensor_tensor(stok[:, :], stok[:, :], slive[:, :], ALU.mult), r)
                link(vec.scalar_tensor_tensor(sidx[:, :], stok[:, :], float(TOK), n, ALU.add, ALU.add), r)
                link(vec.tensor_tensor(sgate[:, :], xs[:, :, C + 3], small_of("expert"), ALU.is_equal), r)
                link(vec.tensor_tensor(sgate[:, :], sgate[:, :], xs[:, :, C + 2], ALU.mult), r)
                vec.tensor_tensor(sgate[:, :], sgate[:, :], xs[:, :, C + 1], ALU.add).then_inc(sidx_done, 1)

            def w_total(r, e, part):
                dve.wait_ge(slow_in[part][e % STAGES], staged_count(r, e))
                dve.wait_ge(w_added[part][e % STAGES], staged_count(r, e))
                if isinstance(r, int) and e == 0:
                    dve.wait_ge(wsmall_in, 16)
                w = staged(e, part)
                vec.scalar_tensor_tensor(w[:, 0, :], w[:, 0, :], gain_w(e, part), w[:, 1, :],
                                         ALU.mult, ALU.add).then_inc(w_sum[part], 1)

            def w_low(r, e, part):
                dve.wait_ge(w_hi[part], E * r + e + 1)
                hi, lo = ((w1h, w1l), (w2h, w2l))[part]
                flat = "p k n -> p (k n)"
                low(lo[e % 2].rearrange(flat), staged(e, part)[:, 0, :], hi[e % 2].rearrange(flat)) \
                    .then_inc(w_lo[part], 1)

            def slot_low(r, e):
                dve.wait_ge(xg_hi, E * r + e + 1)
                low(xg[e % 2][:, 1], bank[0][0:KP, :].rearrange("p (k n) -> p k n", k=2),
                    xg[e % 2][:, 0]).then_inc(xg_lo, 1)

            def hidden_halves(r, e, p):
                n = E * r + e
                j = 3 * n + p
                src = hsq[(3 * e + p) % 2].rearrange("p (q n) -> p q n", q=2)
                cs = slice(2 * p, 2 * p + 2)
                dve.wait_ge(sq_done, j + 1)
                at(dve, y_ready, n - 1)
                vec.tensor_copy(hh[e % 2][:, cs, :], src).then_inc(h_hi, 1)
                dve.wait_ge(h_hi, j + 1)
                low(hl[e % 2][:, cs, :], src, hh[e % 2][:, cs, :]).then_inc(h_lo, 1)

            def output_biased(r, e):
                n = E * r + e
                dve.wait_ge(y_ready, n + 1)
                if isinstance(r, int) and n == 0:
                    dve.wait_ge(b2_in, 32)
                at(dve, yg_done, n)
                late = e >= B2_EARLY
                first = (e - late * B2_EARLY) * C
                both = slice(4 + 2 * (e % 2), 4 + 2 * (e % 2) + ST)
                vec.tensor_tensor(yb, psum[:, both, 0:C], bc(b2b[late][:, first:first + C], 1, ST), ALU.add) \
                    .then_inc(y_taken, 1)

            dve.wait_ge(pos_biased, 1)
            embedded(0)
            projection_low(1)
            ln1(0)
            xT_low(0)
            xT_low(1)
            xT_low(2)
            embedded(1)
            embedded_stats(1)
            for m in range(2 * QC):
                qk_low(0, m)
                if m == 1:
                    w_total(0, 0, 0)
                if m == 3:
                    ln1(1)
                if m == 5:
                    router_matrix()
            for i in range(TG, NT):
                xT_low(i)
            w_total(0, 0, 1)
            w_low(0, 0, 0)
            for m in range(2 * QC):
                qk_low(1, m)
            for b in range(IMAGES):
                softmax_top(b)
                if b >= 6 and b % 2 == 0:
                    output_low((b - 6) // 2)
                if b == GI + 5:
                    residual(0)
                if b == GI + 6:
                    ln2(0)
            softmax_sum(IMAGES - 1)
            softmax_scale(IMAGES - 1)
            output_low(IMAGES // 2 - 3)
            route_probe(0)
            w_low(0, 0, 1)
            output_low(IMAGES // 2 - 2)
            output_low(IMAGES // 2 - 1)
            route_choose(0)
            residual(1)
            route_experts(0)
            ln2(1)
            route_gates(0)
            route_rank(0)
            route_probe(1)
            route_choose(1)
            route_experts(1)
            route_gates(1)
            route_rank(1)
            count_rounds()
            w_total(0, 1, 0)
            w_low(0, 1, 0)
            w_total(0, 1, 1)
            w_total(0, 2, 0)
            w_low(0, 1, 1)
            w_total(0, 2, 1)
            slot_low(0, 0)
            w_total(0, 3, 0)
            w_total(0, 3, 1)
            for s in range(E + 1):
                if s >= 2:
                    output_biased(0, s - 2)
                if s < E:
                    hidden_halves(0, s, 0)
                if s == 0:
                    slots(0)
                if s + 1 < E:
                    slot_low(0, s + 1)
                if s in TOTALS_AT[0]:
                    w_total(0, TOTALS_AT[0][s], 0)
                if s < E:
                    hidden_halves(0, s, 1)
                if 2 <= s < E:
                    w_low(0, s, 1)
                if s in TOTALS_AT[1]:
                    w_total(0, TOTALS_AT[1][s], 1)
                if s < E:
                    hidden_halves(0, s, 2)
            output_biased(0, E - 1)
            before = links[0]

            def fallback(r):
                dve.wait_ge(scattered, r * (2 * NT * 16))
                link(vec.tensor_scalar(rank[:, :, :], rank[:, :, :], -float(CAP), None, ALU.add), r)
                place_rows(slice(0, NT), r)
                dve.wait_ge(added, r * (E * ST * 16))
                link(vec.tensor_scalar(cnt[:, :], cnt[:, :], -float(CAP), None, ALU.add), r)
                slots(r)
                for e in range(E):
                    w_total(r, e, 0)
                    w_total(r, e, 1)
                    w_low(r, e, 1)
                    slot_low(r, e)
                    for p in range(3):
                        hidden_halves(r, e, p)
                    output_biased(r, e)
                assert links[0] - before == FALLBACK_LINKS

            more_rounds(dve, fallback)

        @block.gpsimd
        def _(pool):
            gp = nc.gpsimd
            links = [0]

            def link(ins):
                links[0] += 1
                ins.then_inc(pool_self, 1)
                pool.wait_ge(pool_self, links[0])

            gp.memset(ones[:, :], 1.0).then_inc(memset_done, 1)
            gp.memset(nhalf[:, :], -0.5)
            link(gp.memset(phalf[:, :], 0.5))
            gp.memset(zero[:, :], 0.0).then_inc(zero_there, 1)
            pool.wait_ge(zero_there, 1)
            gp.memset(qb[0][:, :, :, :, ROWS:].rearrange("p a c b n -> p (a c b) n"), 0.0).then_inc(q_zeroed, 1)
            gp.memset(vrow[:, :, :, :], 0.0).then_inc(v_zeroed, 1)
            pool.wait_ge(pos_in, 16)
            pool.wait_ge(small_in, 16)
            gp.tensor_tensor(h[:, :, :], h[:, :, :], bc(small_of("bp", TT), 1, NT), ALU.add) \
                .then_inc(pos_biased, 1)

            def hold(k):
                gp.tensor_tensor(held[:, k:k + 1], zero[0:1, 0:1], zero[0:1, 1:2], ALU.add)

            def inverse_std(ln, g):
                tiles = slice(TG * g, TG * (g + 1))
                pool.wait_ge(mv_done, (ln * GROUPS + g + 1) * TG)
                link(gp.tensor_scalar(rstd[:, ln, tiles], mv[:, ln, tiles, 1], EPS, 1.0, ALU.add, ALU.mult))
                gp.tensor_tensor(rstd[:, ln, tiles], rstd[:, ln, tiles], nhalf[0:TT, 0:TG], ALU.pow) \
                    .then_inc(rstd_done, 1)

            def difference(b):
                pool.wait_ge(rec_done, b + 1)
                if b == 0:
                    pool.wait_ge(lam_done, 1)
                link(gp.tensor_tensor(rec[:, b % 3, NTRI:], rec[:, b % 3, NTRI:], lam[:, :], ALU.mult))
                link(gp.tensor_tensor(ex[:, b % 3], ex[:, b % 3], bc(rec[:, b % 3, :], 2, KEYS), ALU.mult))
                at(pool, dT_ready, (b - 4) // 2 + 1 if b >= 4 else 0)
                gp.tensor_tensor(dif[:, b % 4], ex[:, b % 3, 0:NTRI], ex[:, b % 3, NTRI:], ALU.subtract) \
                    .then_inc(dif_done, 1)

            def w_add(r, e, part):
                pool.wait_ge(fast_in[part][e % STAGES], staged_count(r, e))
                if not isinstance(r, int):
                    hold((part + 1) * E + e)
                pool.dma_start(staged(e, part)[:, 1, :], (w1, w2)[part][e, :, 2], accum_op=ALU.add) \
                    .then_inc(w_added[part][e % STAGES], 16)

            def w_low(r, e, part):
                pool.wait_ge(w_hi[part], E * r + e + 1)
                hi, lo = ((w1h, w1l), (w2h, w2l))[part]
                flat = "p k n -> p (k n)"
                gp.tensor_tensor(lo[e % 2].rearrange(flat), staged(e, part)[:, 0, :],
                                 hi[e % 2].rearrange(flat).bitcast(F32), ALU.subtract).then_inc(w_lo[part], 1)

            def probe_norm(g):
                pool.wait_ge(un_clamped, g + 1)
                gp.tensor_tensor(un[:, 0, :], un[:, 1, :], nhalf[0:TT, 0:TG], ALU.pow).then_inc(un_pow, 1)

            def scatter(i, k):
                pool.indirect_dma_start(
                    xs_dram, bass.IndirectOffsetOnAxis(ap=idx[:, i, k:k + 1], axis=0), xrow[:, i, :], None,
                    bounds_check=E * CAP - 1, oob_is_err=False).then_inc(scattered, 16)

            def add_rows(r, e):
                n = E * r + e
                pool.wait_ge(yg_done, n + 1)
                at(pool, added, n * ST * 16)
                pool.wait_ge(out_init, (GROUPS + 1) * 16)
                if not isinstance(r, int):
                    hold(e)
                for s in range(ST):
                    j = e * ST + s
                    pool.indirect_dma_start(
                        out, bass.IndirectOffsetOnAxis(ap=sidx[:, j:j + 1], axis=0),
                        yg[e % 2][:, s, :], None, compute_op=ALU.add).then_inc(added, 16)

            def scatter_rows(g, part):
                pool.wait_ge(idx_done, g + 1)
                pool.wait_ge(row_done, g + 1)
                for j in part:
                    scatter(TG * g + j // 2, j % 2)

            pool.wait_ge(qk_hi0, 1)
            gp.tensor_tensor(fr[0:KP, 1, 0:QKN // 2], qkraw[:, 0:QKN // 2],
                             fr[0:KP, 0, 0:QKN // 2].bitcast(F32), ALU.subtract).then_inc(qk_lo0, 1)
            inverse_std(0, 0)
            w_add(0, 0, 0)
            pool.wait_ge(vo_hi, 1)
            gp.tensor_tensor(fr[0:KP, 1, QKN:QKN + VON], voraw, fr[0:KP, 0, QKN:QKN + VON].bitcast(F32),
                             ALU.subtract).then_inc(vo_lo, 1)
            inverse_std(0, 1)
            pool.wait_ge(gain_n2, 1)
            gp.tensor_tensor(gain[:, 2, :], align[:, 2, :], phalf[0:KP, :], ALU.pow).then_inc(gain_pow, 1)
            gp.tensor_tensor(gain[:, 3, :], gain[:, 1, :], nhalf[0:KP, :], ALU.pow).then_inc(gain_pow, 1)
            w_add(0, 0, 1)
            pool.wait_ge(qk_lo0, 2)
            pool.wait_ge(vo_lo, 1)
            gp.memset(qb[1][:, :, :, :, ROWS:].rearrange("p a c b n -> p (a c b) n"), 0.0).then_inc(q_zeroed, 1)
            pool.dma_start(xs_dram.rearrange("(n p) c -> p n c", p=128), bc(zero[:, :], 1, E * ST)) \
                .then_inc(zero_out, 16)
            pool.wait_ge(xn_done, NT)
            gp.tensor_tensor(h[:, :, :], h[:, :, :], bc(small_of("bo", TT), 1, NT), ALU.add) \
                .then_inc(h_biased, 1)
            for b in range(IMAGES):
                difference(b)
                if b == GI + 2:
                    w_add(0, STAGES, 0)
                if b == GI + 4:
                    inverse_std(1, 0)
            probe_norm(0)
            pool.wait_ge(zero_out, 16)
            for part in range(2):
                w_add(0, 1, part)
            inverse_std(1, 1)
            for part in range(2):
                w_add(0, 2, part)
            w_add(0, STAGES, 1)
            scatter_rows(0, range(0, 2))
            probe_norm(1)
            scatter_rows(0, range(2, 2 * TG))
            scatter_rows(1, range(2 * TG))
            pool.wait_ge(xs_in[1], 16)
            for s in range(E + 2):
                if STAGES < s + 3 < E:
                    w_add(0, s + 3, 0)
                if 2 <= s + 1 < E:
                    w_low(0, s + 1, 0)
                if STAGES < s + 3 < E:
                    w_add(0, s + 3, 1)
                if s >= 2:
                    add_rows(0, s - 2)

            def fallback(r):
                pool.wait_ge(idx_done, GROUPS + r)
                for j in range(len(XS_PARTS)):
                    pool.wait_ge(xs_in[j], r * 16)
                hold(3 * E)
                for i in range(NT):
                    for k in range(2):
                        scatter(i, k)
                for e in range(E):
                    w_add(r, e, 0)
                    w_add(r, e, 1)
                    w_low(r, e, 0)
                    add_rows(r, e)

            n = more_rounds(pool, fallback)
            pool.wait_ge(added, n * (E * ST * 16))
            hold(3 * E + 1)


_INPUTS = ("patches", "pos", "wqk", "wvo", "small", "w1", "w2", "wsmall", "b2")


def kernel(**inputs):
    import concourse.bacc as bacc
    from concourse.bass_utils import run_bass_kernel_spmd as run

    a = {k: np.asarray(v) for k, v in inputs.items()}
    f = "L0_ffn_"
    x = a["x"].reshape(IMAGES, GRID, PATCH, GRID, PATCH, CH).transpose(2, 4, 5, 0, 1, 3)
    chunks = lambda m, n: m.reshape(n, m.shape[0] // n, *m.shape[1:]).swapaxes(0, 1)
    arrays = {}
    arrays["patches"] = np.concatenate([chunks(x.reshape(PATCH * PATCH * CH, TOK), PK),
                                        chunks(a["L0_tok_W_proj"], PK)], axis=2)
    arrays["pos"] = chunks(np.tile(a["L0_tok_pos_table"], (IMAGES, 1)), NT)
    wqk = np.zeros((KP, 2, 2, QC, 128), np.float32)
    for j, name in enumerate(("L0_attn_Wq", "L0_attn_Wk")):
        w = chunks(a[name], 2).reshape(KP, 2, QC, 2, TRI * D)
        for t in range(2):
            wqk[:, :, j, :, 64 * t:64 * t + TRI * D] = w[:, :, :, t, :]
    arrays["wqk"] = wqk.reshape(KP, -1)
    wo = chunks(a["L0_attn_Wo"], 2).reshape(2, TRI, D, 2, C).swapaxes(0, 1).reshape(KP, 2, C)
    wvc = a["L0_attn_Wv"].reshape(C, 2, 2, TRI * D).swapaxes(1, 2).reshape(C, C)
    arrays["wvo"] = np.stack([chunks(wvc, 2), wo], 2).reshape(KP, -1)
    arrays["w1"] = np.stack([a[f + n].reshape(E, 2, KP, HID).swapaxes(1, 2).reshape(E, KP, W1N)
                             for n in ("w_slow1", "w_fast1", "h_fast1")], 2)
    arrays["w2"] = np.stack([a[f + n].reshape(E, HC, 128, C).swapaxes(1, 2).reshape(E, 128, W2N)
                             for n in ("w_slow2", "w_fast2", "h_fast2")], 2)
    ws = np.zeros((128, E, HC + 2), np.float32)
    ws[:, :, 0:HC] = a[f + "b1"].reshape(E, HC, 128).transpose(2, 0, 1)
    ws[:, :, HC] = a[f + "m_gate1"]
    ws[:, :, HC + 1] = a[f + "m_gate2"]
    arrays["wsmall"] = ws
    arrays["b2"] = a[f + "b2"].reshape(1, E * C)

    s = np.zeros((128, SMALL), np.float32)

    def put(name, value):
        lo, hi = _cols[name]
        s[0:value.shape[0], lo:hi] = value.reshape(value.shape[0], -1)

    p = np.arange(128)[:, None]
    put("ident", np.eye(128, dtype=np.float32))
    put("before", np.triu(np.ones((TT, TT), np.float32), 1))
    head = lambda q, n: (q // D == n) & (q < TRI * D)
    put("qmask", np.where(head(p % 64, np.arange(TRI)), np.float32(D ** -0.5), np.float32(0)))
    put("lam", np.repeat(a["L0_attn_lambda_p"].reshape(NTRI, TRI).T, KEYS, axis=0))
    put("energy", np.tile(a[f + "energy"], (128, 1)))
    put("fatigue", np.tile(a[f + "fatigue"], (128, 1)))
    put("iota", np.tile(np.arange(E, dtype=np.float32), (128, 1)))
    put("token", (p[0:TT] + TT * np.arange(NT)).astype(np.float32))
    n = np.arange(E * ST)
    put("slot", (p + 128 * (n % ST)).astype(np.float32))
    put("expert", np.tile((n // ST).astype(np.float32), (128, 1)))
    put("bo", np.tile(a["L0_attn_bo"], (128, 1)))
    put("bp", np.tile(a["L0_tok_b_proj"], (128, 1)))
    put("rw", chunks(a[f + "router_w"].T, 2))
    put("probeT", chunks(a[f + "probe_w"].T, 2))
    put("probe", a[f + "probe_w"])
    put("embT", a[f + "router_emb"].T)
    arrays["small"] = s
    arrays = {f"in_{k}": np.ascontiguousarray(arrays[k]) for k in _INPUTS}

    nc = bacc.Bacc("TRN2", target_bir_lowering=False, num_devices=1)
    ins = [nc.dram_tensor(k, v.shape, mybir.dt.from_np(v.dtype), kind="ExternalInput").ap()
           for k, v in arrays.items()]
    out = nc.dram_tensor("out_rows", (TOK + CAP, C), F32, kind="ExternalOutput").ap()
    build(nc, *ins, out)
    r = run(nc, [arrays], core_ids=[0])
    return r.results[0]["out_rows"][0:TOK].reshape(IMAGES, KEYS, C)
```
